# Optimizing a Trainium2 kernel written in Bass

```python
import numpy as np
import jax
import jax.numpy as jnp

def _softmax(x, axis=-1):
    return jax.nn.softmax(x, axis=axis)

def _gelu(x):
    return jax.nn.gelu(x, approximate=True)

def _silu(x):
    return jax.nn.silu(x)

def _sigmoid(x):
    return jax.nn.sigmoid(x)

def _layernorm(x, axis=-1, eps=1e-05):
    m = jnp.mean(x, axis=axis, keepdims=True)
    v = jnp.var(x, axis=axis, keepdims=True)
    return (x - m) / jnp.sqrt(v + eps)

def _scatter_add(tgt, idx, src, axis=0):
    return tgt.at[idx].add(src)

def _segment_sum(src, seg, n):
    return jax.ops.segment_sum(src, seg, n)
kernel_name = 'mk_audio_tower_d2_tok_audfeat256_r4_4ec9b3'

def setup_inputs(seed: int=0):
    np.random.seed(seed)
    _w = jnp.asarray

    def _rec_inputs():
        import jax
        import jax.numpy as jnp
        _rk = jax.random.key(seed)
        x = 7.22013e-05 + 1.00017 * jax.random.normal(jax.random.fold_in(_rk, 1), (4, 750, 64), jnp.float32)
        return x
    x = _rec_inputs()

    def _L0_tok_setup():
        import jax, jax.numpy as jnp
        import numpy as np
        WIN = 9
        key = jax.random.key(seed)
        ks = jax.random.split(key, 4)
        N, L, C, U = (8, 1024, 64, 64)
        x = jax.random.normal(ks[0], (N, L, C), dtype=jnp.float32)
        W_qry = jax.random.normal(ks[1], (C, U), dtype=jnp.float32) * 0.05
        W_key = jax.random.normal(ks[2], (C, U), dtype=jnp.float32) * 0.05
        v = jax.random.normal(ks[3], (U,), dtype=jnp.float32) * 0.05
        b = jnp.zeros((U,), dtype=jnp.float32)
        return {'x': x, 'W_qry': W_qry, 'W_key': W_key, 'v': v, 'b': b}
    _L0_tok_all = _L0_tok_setup()
    _L0_tok_in = {k: v for k, v in _L0_tok_all.items() if k in ('W_qry', 'W_key', 'v', 'b')}
    del _L0_tok_all

    def _L0_attn_setup():
        import jax, jax.numpy as jnp
        import numpy as np
        DIM = 64
        key = jax.random.key(seed)
        ks = jax.random.split(key, 7)
        x = jax.random.normal(ks[0], (4, 1024, DIM), dtype=jnp.float32)
        s = 1.0 / np.sqrt(DIM)
        Wq = jax.random.uniform(ks[1], (DIM, DIM), jnp.float32, -s, s)
        Wk = jax.random.uniform(ks[2], (DIM, DIM), jnp.float32, -s, s)
        Wv = jax.random.uniform(ks[3], (DIM, DIM), jnp.float32, -s, s)
        bq = jax.random.uniform(ks[4], (DIM,), jnp.float32, -s, s)
        bk = jax.random.uniform(ks[5], (DIM,), jnp.float32, -s, s)
        bv = jax.random.uniform(ks[6], (DIM,), jnp.float32, -s, s)
        return {'x': x, 'Wq': Wq, 'bq': bq, 'Wk': Wk, 'bk': bk, 'Wv': Wv, 'bv': bv}
    _L0_attn_all = _L0_attn_setup()
    _L0_attn_in = {k: v for k, v in _L0_attn_all.items() if k in ('Wq', 'bq', 'Wk', 'bk', 'Wv', 'bv')}
    del _L0_attn_all

    def _L0_ffn_setup():
        import jax, jax.numpy as jnp
        import numpy as np
        B, N, D = (16, 1024, 64)
        NUM_EXPERTS, TOP_K, HEADS = (4, 2, 4)
        N_EDGES = 262144
        LN_EPS = 1e-05

        def _layernorm(x, g, b):
            mu = x.mean(-1, keepdims=True)
            var = ((x - mu) ** 2).mean(-1, keepdims=True)
            return (x - mu) * jax.lax.rsqrt(var + LN_EPS) * g + b

        def _forward(x, edge_index, W_gat, att_src, att_dst, b_gat, ln_gamma, ln_beta, W1, b1, W2, b2):
            Bc, Nc, Dc = x.shape
            M = Bc * Nc
            x_flat = x.reshape(M, Dc)
            h = (x_flat @ W_gat).reshape(M, HEADS, NUM_EXPERTS)
            loops = jnp.arange(M, dtype=edge_index.dtype)
            src = jnp.concatenate([edge_index[0], loops])
            dst = jnp.concatenate([edge_index[1], loops])
            a_src = (h * att_src).sum(-1)
            a_dst = (h * att_dst).sum(-1)
            e = jax.nn.leaky_relu(a_src[src] + a_dst[dst], negative_slope=0.2)
            e_max = jax.ops.segment_max(e, dst, num_segments=M)
            ee = jnp.exp(e - e_max[dst])
            denom = jax.ops.segment_sum(ee, dst, num_segments=M)
            alpha = ee / (denom[dst] + 1e-16)
            msg = h[src] * alpha[:, :, None]
            agg = jax.ops.segment_sum(msg, dst, num_segments=M).reshape(M, HEADS * NUM_EXPERTS) + b_gat
            scores = _layernorm(agg, ln_gamma, ln_beta).reshape(M, HEADS, NUM_EXPERTS).mean(1)
            scores = scores.reshape(Bc, Nc, NUM_EXPERTS)
            topk_s, topk_i = jax.lax.top_k(scores, TOP_K)
            w = jax.nn.softmax(topk_s, axis=-1)
            out = jnp.zeros_like(x)
            for ei in range(NUM_EXPERTS):
                g = jnp.where(topk_i == ei, w, 0.0).sum(-1)
                hh = jax.nn.gelu(x @ W1[ei] + b1[ei], approximate=False)
                out = out + g[..., None] * (hh @ W2[ei] + b2[ei])
            return out
        key = jax.random.key(seed)
        ks = jax.random.split(key, 8)
        s = 0.05
        return {'x': jax.random.normal(ks[0], (B, N, D), jnp.float32), 'W_gat': jax.random.normal(ks[1], (D, HEADS * NUM_EXPERTS), jnp.float32) * s, 'att_src': jax.random.normal(ks[2], (HEADS, NUM_EXPERTS), jnp.float32) * s, 'att_dst': jax.random.normal(ks[3], (HEADS, NUM_EXPERTS), jnp.float32) * s, 'b_gat': jnp.zeros((HEADS * NUM_EXPERTS,), jnp.float32), 'ln_gamma': jnp.ones((HEADS * NUM_EXPERTS,), jnp.float32), 'ln_beta': jnp.zeros((HEADS * NUM_EXPERTS,), jnp.float32), 'W1': jax.random.normal(ks[4], (NUM_EXPERTS, D, 2 * D), jnp.float32) * s, 'b1': jnp.zeros((NUM_EXPERTS, 2 * D), jnp.float32), 'W2': jax.random.normal(ks[5], (NUM_EXPERTS, 2 * D, D), jnp.float32) * s, 'b2': jnp.zeros((NUM_EXPERTS, D), jnp.float32), 'edge_index': jax.random.randint(ks[6], (2, N_EDGES), 0, B * N, jnp.int32)}
    _L0_ffn_all = _L0_ffn_setup()
    _L0_ffn_in = {k: v for k, v in _L0_ffn_all.items() if k in ('W_gat', 'att_src', 'att_dst', 'b_gat', 'ln_gamma', 'ln_beta', 'W1', 'b1', 'W2', 'b2', 'edge_index')}
    del _L0_ffn_all

    def _L1_attn_setup():
        import jax, jax.numpy as jnp
        import numpy as np
        key = jax.random.key(seed)
        k1, k2 = jax.random.split(key)
        B, N, D = (4, 1024, 64)
        inp = jax.random.normal(k1, (B, N, D), dtype=jnp.float32)
        q_weight = jax.random.normal(k2, (D, D), dtype=jnp.float32)
        return {'input': inp, 'q_weight': q_weight}
    _L1_attn_all = _L1_attn_setup()
    _L1_attn_in = {k: v for k, v in _L1_attn_all.items() if k in ('q_weight',)}
    del _L1_attn_all

    def _L1_ffn_setup():
        import jax, jax.numpy as jnp
        import numpy as np
        EPS = 1e-08
        key = jax.random.key(seed)
        kx, kw, kb = jax.random.split(key, 3)
        B, S, K, N = (64, 1024, 64, 64)
        x = jax.random.normal(kx, (B, S, K), dtype=jnp.float32)
        bound_w = np.sqrt(6.0 / K) / np.sqrt(1.0 + 5.0)
        weight = jax.random.uniform(kw, (N, K), dtype=jnp.float32, minval=-bound_w, maxval=bound_w)
        bound_b = 1.0 / np.sqrt(K)
        bias = jax.random.uniform(kb, (N,), dtype=jnp.float32, minval=-bound_b, maxval=bound_b)
        return {'x': x, 'weight': weight, 'bias': bias}
    _L1_ffn_all = _L1_ffn_setup()
    _L1_ffn_in = {k: v for k, v in _L1_ffn_all.items() if k in ('weight', 'bias')}
    del _L1_ffn_all
    return {'x': x, 'L0_tok_W_qry': _L0_tok_in['W_qry'], 'L0_tok_W_key': _L0_tok_in['W_key'], 'L0_tok_v': _L0_tok_in['v'], 'L0_tok_b': _L0_tok_in['b'], 'L0_attn_Wq': _L0_attn_in['Wq'], 'L0_attn_bq': _L0_attn_in['bq'], 'L0_attn_Wk': _L0_attn_in['Wk'], 'L0_attn_bk': _L0_attn_in['bk'], 'L0_attn_Wv': _L0_attn_in['Wv'], 'L0_attn_bv': _L0_attn_in['bv'], 'L0_ffn_W_gat': _L0_ffn_in['W_gat'], 'L0_ffn_att_src': _L0_ffn_in['att_src'], 'L0_ffn_att_dst': _L0_ffn_in['att_dst'], 'L0_ffn_b_gat': _L0_ffn_in['b_gat'], 'L0_ffn_ln_gamma': _L0_ffn_in['ln_gamma'], 'L0_ffn_ln_beta': _L0_ffn_in['ln_beta'], 'L0_ffn_W1': _L0_ffn_in['W1'], 'L0_ffn_b1': _L0_ffn_in['b1'], 'L0_ffn_W2': _L0_ffn_in['W2'], 'L0_ffn_b2': _L0_ffn_in['b2'], 'L0_ffn_edge_index': _L0_ffn_in['edge_index'], 'L1_attn_q_weight': _L1_attn_in['q_weight'], 'L1_ffn_weight': _L1_ffn_in['weight'], 'L1_ffn_bias': _L1_ffn_in['bias']}

def reference(x, L0_tok_W_qry, L0_tok_W_key, L0_tok_v, L0_tok_b, L0_attn_Wq, L0_attn_bq, L0_attn_Wk, L0_attn_bk, L0_attn_Wv, L0_attn_bv, L0_ffn_W_gat, L0_ffn_att_src, L0_ffn_att_dst, L0_ffn_b_gat, L0_ffn_ln_gamma, L0_ffn_ln_beta, L0_ffn_W1, L0_ffn_b1, L0_ffn_W2, L0_ffn_b2, L0_ffn_edge_index, L1_attn_q_weight, L1_ffn_weight, L1_ffn_bias):
    import jax
    import jax.numpy as jnp

    def _L0_tok_ref(x, W_qry, W_key, v, b):
        import jax, jax.numpy as jnp
        import numpy as np
        WIN = 9
        N, L, C = x.shape
        n_w = L - WIN + 1
        idx = jnp.arange(n_w)[:, None] + jnp.arange(WIN)[None, :]
        x_win = x[:, idx]
        x_ctr = x[:, WIN // 2:WIN // 2 + n_w]
        key = jnp.einsum('nwsc,cu->nwsu', x_win, W_key)
        qry = jnp.einsum('nwc,cu->nwu', x_ctr, W_qry)
        score = jnp.einsum('nwsu,u->nws', jnp.tanh(qry[:, :, None, :] + key + b), v)
        weight = jax.nn.softmax(score, axis=2)
        out = jnp.einsum('nwsc,nws->nwc', x_win, weight)
        return out

    def _L0_attn_ref(x, Wq, bq, Wk, bk, Wv, bv):
        import jax, jax.numpy as jnp
        import numpy as np
        DIM = 64
        q = jnp.einsum('bsd,ed->bse', x, Wq) + bq
        k = jnp.einsum('bsd,ed->bse', x, Wk) + bk
        v = jnp.einsum('bsd,ed->bse', x, Wv) + bv
        scale = 1.0 / jnp.sqrt(jnp.float32(x.shape[-1]))
        scores = jnp.einsum('bse,bte->bst', q, k) * scale
        weights = jax.nn.softmax(scores, axis=-1)
        return jnp.einsum('bst,bte->bse', weights, v)

    def _L0_ffn_ref(x, W_gat, att_src, att_dst, b_gat, ln_gamma, ln_beta, W1, b1, W2, b2, edge_index):
        import jax, jax.numpy as jnp
        import numpy as np
        B, N, D = (16, 1024, 64)
        NUM_EXPERTS, TOP_K, HEADS = (4, 2, 4)
        N_EDGES = 262144
        LN_EPS = 1e-05

        def _layernorm(x, g, b):
            mu = x.mean(-1, keepdims=True)
            var = ((x - mu) ** 2).mean(-1, keepdims=True)
            return (x - mu) * jax.lax.rsqrt(var + LN_EPS) * g + b

        def _forward(x, edge_index, W_gat, att_src, att_dst, b_gat, ln_gamma, ln_beta, W1, b1, W2, b2):
            Bc, Nc, Dc = x.shape
            M = Bc * Nc
            x_flat = x.reshape(M, Dc)
            h = (x_flat @ W_gat).reshape(M, HEADS, NUM_EXPERTS)
            loops = jnp.arange(M, dtype=edge_index.dtype)
            src = jnp.concatenate([edge_index[0], loops])
            dst = jnp.concatenate([edge_index[1], loops])
            a_src = (h * att_src).sum(-1)
            a_dst = (h * att_dst).sum(-1)
            e = jax.nn.leaky_relu(a_src[src] + a_dst[dst], negative_slope=0.2)
            e_max = jax.ops.segment_max(e, dst, num_segments=M)
            ee = jnp.exp(e - e_max[dst])
            denom = jax.ops.segment_sum(ee, dst, num_segments=M)
            alpha = ee / (denom[dst] + 1e-16)
            msg = h[src] * alpha[:, :, None]
            agg = jax.ops.segment_sum(msg, dst, num_segments=M).reshape(M, HEADS * NUM_EXPERTS) + b_gat
            scores = _layernorm(agg, ln_gamma, ln_beta).reshape(M, HEADS, NUM_EXPERTS).mean(1)
            scores = scores.reshape(Bc, Nc, NUM_EXPERTS)
            topk_s, topk_i = jax.lax.top_k(scores, TOP_K)
            w = jax.nn.softmax(topk_s, axis=-1)
            out = jnp.zeros_like(x)
            for ei in range(NUM_EXPERTS):
                g = jnp.where(topk_i == ei, w, 0.0).sum(-1)
                hh = jax.nn.gelu(x @ W1[ei] + b1[ei], approximate=False)
                out = out + g[..., None] * (hh @ W2[ei] + b2[ei])
            return out
        return _forward(x, edge_index, W_gat, att_src, att_dst, b_gat, ln_gamma, ln_beta, W1, b1, W2, b2)

    def _L1_attn_ref(input, q_weight):
        import jax, jax.numpy as jnp
        import numpy as np
        query = jnp.einsum('bnd,de->bne', input, q_weight)
        att = jax.nn.sigmoid(jnp.einsum('bnd,bmd->bnm', query, input))
        value = jnp.einsum('bnm,bmd->bnd', att, input)
        return value

    def _L1_ffn_ref(x, weight, bias):
        import jax, jax.numpy as jnp
        import numpy as np
        EPS = 1e-08
        'LNS inference path of LNSLinear.\n\n            log_out[m, n] = logsumexp_k(log(|x[m,k]|+eps) + log(|w[n,k]|+eps))\n            out = sign(sign(x) @ sign(w).T) * exp(log_out) + bias\n            Computed stably as log(exp(lx - mx) @ exp(lw - mw).T) + mx + mw.\n            '
        orig_shape = x.shape
        K = weight.shape[1]
        xf = x.reshape(-1, K)
        log_x = jnp.log(jnp.abs(xf) + EPS)
        x_sign = jnp.sign(xf)
        log_w = jnp.log(jnp.abs(weight) + EPS)
        w_sign = jnp.sign(weight)
        mx = jnp.max(log_x, axis=-1, keepdims=True)
        mw = jnp.max(log_w, axis=-1, keepdims=True)
        acc = jnp.einsum('mk,nk->mn', jnp.exp(log_x - mx), jnp.exp(log_w - mw))
        log_out = jnp.log(acc) + mx + mw.T
        out_sign = jnp.sign(jnp.einsum('mk,nk->mn', x_sign, w_sign))
        out = out_sign * jnp.exp(log_out) + bias
        return out.reshape(orig_shape[:-1] + (weight.shape[0],))
    h = _L0_tok_ref(x, L0_tok_W_qry, L0_tok_W_key, L0_tok_v, L0_tok_b)
    h = h + _L0_attn_ref(_layernorm(h, axis=-1), L0_attn_Wq, L0_attn_bq, L0_attn_Wk, L0_attn_bk, L0_attn_Wv, L0_attn_bv)
    h = h + _L0_ffn_ref(_layernorm(h, axis=-1), L0_ffn_W_gat, L0_ffn_att_src, L0_ffn_att_dst, L0_ffn_b_gat, L0_ffn_ln_gamma, L0_ffn_ln_beta, L0_ffn_W1, L0_ffn_b1, L0_ffn_W2, L0_ffn_b2, L0_ffn_edge_index)
    h = h + _L1_attn_ref(_layernorm(h, axis=-1), L1_attn_q_weight)
    h = h + _L1_ffn_ref(_layernorm(h, axis=-1), L1_ffn_weight, L1_ffn_bias)
    return h

_drawn_inputs = setup_inputs


def setup_inputs(seed=0):
    import zlib

    import numpy as np

    out = dict(_drawn_inputs(seed))
    spreads = {'L0_tok_b': (0.0, 0.3),
     'L0_ffn_b_gat': (0.0, 0.1),
     'L0_ffn_ln_gamma': (1.0, 0.2),
     'L0_ffn_ln_beta': (0.0, 0.1),
     'L0_ffn_b1': (0.0, 0.1),
     'L0_ffn_b2': (0.0, 0.1)}
    factors = {'L0_attn_bk': 64.0, 'L0_ffn_att_src': 3.746, 'L0_ffn_att_dst': 4.584, 'L1_ffn_bias': 64.0}
    for name, (base, spread) in spreads.items():
        noise = np.random.default_rng([zlib.crc32(name.encode()), seed]).standard_normal(out[name].shape)
        drawn = base * np.exp(spread * noise) if base else spread * noise
        out[name] = jnp.asarray(drawn.astype(out[name].dtype))
    for name, factor in factors.items():
        out[name] = (out[name] * factor).astype(out[name].dtype)
    return out
```

```python
import concourse.bass as bass
from concourse import mybir
from contextlib import ExitStack


def audio_tower(
    nc: bass.Bass,
    x: bass.AP,
    tok_W_qry: bass.AP,
    tok_W_key: bass.AP,
    tok_v: bass.AP,
    tok_b: bass.AP,
    attn_Wq: bass.AP,
    attn_bq: bass.AP,
    attn_Wk: bass.AP,
    attn_bk: bass.AP,
    attn_Wv: bass.AP,
    attn_bv: bass.AP,
    W_gat: bass.AP,
    att_src: bass.AP,
    att_dst: bass.AP,
    b_gat: bass.AP,
    ln_gamma: bass.AP,
    ln_beta: bass.AP,
    W1: bass.AP,
    b1: bass.AP,
    W2: bass.AP,
    b2: bass.AP,
    edge_index: bass.AP,
    sig_W: bass.AP,
    lns_W: bass.AP,
    lns_bias: bass.AP,
    out: bass.AP,
):
    F32 = mybir.dt.float32
    I32 = mybir.dt.int32
    ALU = mybir.AluOpType
    ACT = mybir.ActivationFunctionType
    AX = mybir.AxisListType

    B, L, C = x.shape
    WIN = 9
    NW = L - WIN + 1
    P, T = 106, 7
    assert P * T == NW
    G = B * T
    M = B * NW
    HALF = NW // 2
    XP = 125
    XT = L // XP
    PAIRS = B // 2
    H, E = att_src.shape
    HE = H * E
    FF = W1.shape[2]
    NE = edge_index.shape[1]
    EC = NE // 128
    EPAD = EC + 16
    KS = 4096
    assert M < KS
    RC = 8
    TW = H + HE
    DW = 2 * H
    BIG = 3.0e38
    SCALE = 1.0 / float(C) ** 0.5
    ROUND = 12582912.0

    src_table = nc.dram_tensor("src_table", (M + 1, TW), F32, kind="Internal").ap()
    dst_table = nc.dram_tensor("dst_table", (M, DW), F32, kind="Internal").ap()

    ctx = ExitStack()
    with ctx:
        def sb(name, shape, dt=F32):
            return ctx.enter_context(nc.sbuf_tensor(name, shape, dt))

        def sem(name):
            return ctx.enter_context(nc.semaphore(name))

        ident = sb("ident", [128, 128])
        tril = sb("tril", [128, 128])
        iota_lo = sb("iota_lo", [128, P])
        iota_hi = sb("iota_hi", [128, G])
        wk2 = sb("wk2", [128, 128])
        wq2 = sb("wq2", [128, 128])
        v2 = sb("v2", [128, 2])
        tb = sb("tb", [128, 1])
        wraw = sb("wraw", [C, 3, C])
        wT = sb("wT", [C, 3, C])
        bq = sb("bq", [C, 1])
        bk = sb("bk", [C, 1])
        bv_row = sb("bv_row", [P, C])
        wgat = sb("wgat", [C, HE])
        asrc_row = sb("asrc_row", [P, HE])
        adst_row = sb("adst_row", [P, HE])
        bgat_row = sb("bgat_row", [P, HE])
        gamma_row = sb("gamma_row", [P, HE])
        beta_row = sb("beta_row", [P, HE])
        w1 = sb("w1", [C, E, FF])
        b1c = sb("b1c", [FF, E])
        w2 = sb("w2", [FF, E, C])
        b2_row = sb("b2_row", [P, E * C])
        wsig = sb("wsig", [C, 2 * C])
        wl = sb("wl", [128, 2, C])
        wl2 = sb("wl2", [128, 128])
        wlT = sb("wlT", [128, 128])
        mw = sb("mw", [128, 1])
        mw_row = sb("mw_row", [P, C])
        lbias_row = sb("lbias_row", [P, C])
        xt = sb("xt", [XP, XT, B * C])
        xT = sb("xT", [128, PAIRS, L])
        kT2 = sb("kT2", [128, L])
        qT2 = sb("qT2", [128, NW])
        ring = sb("ring", [128, 3, NW])
        big = sb("big", [128, G * WIN * C])
        wts = sb("wts", [P, G, WIN])
        wsm = sb("wsm", [P, G])
        h = sb("h", [P, G, C])
        yb = sb("yb", [P, T, C])
        cen = sb("cen", [P, T, C])
        sq = sb("sq", [P, T, C])
        st = sb("st", [P, 4, T])
        yT = sb("yT", [C, NW])
        qa = sb("qa", [C + 1, NW])
        ka = sb("ka", [C + 1, NW])
        va = sb("va", [P, T, C + 1])
        nm = sb("nm", [P, T])
        rd = sb("rd", [P, T])
        ebuf = sb("ebuf", [128, 2, EPAD], I32)
        fbuf = sb("fbuf", [128, 2, EPAD])
        key = sb("key", [128, EC])
        m8 = sb("m8", [128, RC])
        ki = sb("ki", [128, 2, RC], I32)
        kf = sb("kf", [128, 4, RC])
        cnt = sb("cnt", [128, 1])
        nf = sb("nf", [1, 2])
        ni = sb("ni", [1, 1], I32)
        hg = sb("hg", [P, G, HE])
        Ts = sb("Ts", [P, G, TW])
        Ds = sb("Ds", [P, G, DW])
        zrow = sb("zrow", [1, 560])
        Mx = sb("Mx", [P, H, G])
        tmp16 = sb("tmp16", [P, G, HE])
        small = sb("small", [P, 8, G])
        s4 = sb("s4", [P, 6, G, E])
        idx = sb("idx", [128, 2, 2, RC], I32)
        gs = sb("gs", [128, 2, RC, TW])
        gd = sb("gd", [128, 2, RC, DW])
        col = sb("col", [128, 2, 2, RC])
        dcol = sb("dcol", [128, 2, RC])
        ohhi = sb("ohhi", [128, RC, G])
        ohlo = sb("ohlo", [128, 2, P])
        neg = sb("neg", [128, 128])
        scr = sb("scr", [128, H + 1, 128])
        lead = sb("lead", [128, 2])
        cm = sb("cm", [128, H + 1])
        vr = sb("vr", [128, 2, TW, G])
        cand = sb("cand", [P, H, G])
        nb = sb("nb", [P, G])
        ew = sb("ew", [128, RC, H])
        fe = sb("fe", [128, RC, TW])
        PT = big[0:P, 0:T * NW].rearrange("p (t n) -> p t n", t=T)
        o0 = T * NW
        HH = big[:, o0:o0 + E * NW].rearrange("p (e n) -> p e n", e=E)
        o0 += E * NW
        Oe = big[0:P, o0:o0 + G * E * C].rearrange("p (g e c) -> p g e c", e=E, c=C)
        xw = big[0:P, :].rearrange("p (g s c) -> p g s c", s=WIN, c=C)
        l_src, l_dst = ebuf[:, 0, :], ebuf[:, 1, :]
        l_lo, l_hi = fbuf[:, 0, :], fbuf[:, 1, :]

        ps = ctx.enter_context(nc.psum_tensor("ps", [128, 8, 512], F32))

        def tile(ap, t):
            return ap[:, t * P:(t + 1) * P]

        c_ready = sem("c_ready")
        w_in = sem("w_in")
        z_ready = sem("z_ready")
        x_in = sem("x_in")
        e_in = sem("e_in")
        xw_in = sem("xw_in")
        wT_ps = sem("wT_ps")
        w_prep = sem("w_prep")
        wl_act = sem("wl_act")
        wl_dve = sem("wl_dve")
        cnt_ready = sem("cnt_ready")
        cnt_row = sem("cnt_row")
        rounds_ready = sem("rounds_ready")
        x_tr = sem("x_tr")
        x_ev = sem("x_ev")
        kq_ps = sem("kq_ps")
        k_ev = sem("k_ev")
        q_ev = sem("q_ev")
        add_done = sem("add_done")
        tanh_done = sem("tanh_done")
        sc_ps = sem("sc_ps")
        sc_shift = sem("sc_shift")
        sc_exp = sem("sc_exp")
        tok_done = sem("tok_done")
        var_ready = [sem(f"var_ready{n}") for n in range(4)]
        std_ready = [sem(f"std_ready{n}") for n in range(4)]
        y_ready = [sem(f"y_ready{n}") for n in range(4)]
        yT_ps = [sem(f"yT_ps{n}") for n in range(4)]
        yT_ev = [sem(f"yT_ev{n}") for n in range(4)]
        qkv_ps = sem("qkv_ps")
        qkv_ev = sem("qkv_ev")
        s_ps = sem("s_ps")
        s_max = sem("s_max")
        m_ps = sem("m_ps")
        m_ev = sem("m_ev")
        st_ps = sem("st_ps")
        p_ready = sem("p_ready")
        o_ps = sem("o_ps")
        o_ev = sem("o_ev")
        gat_ps = sem("gat_ps")
        gat_ev = sem("gat_ev")
        hid_ps = sem("hid_ps")
        hid_ev = sem("hid_ev")
        ex_ps = sem("ex_ps")
        ex_ev = sem("ex_ev")
        T_ready = sem("T_ready")
        T_out = sem("T_out")
        D_ready = sem("D_ready")
        D_out = sem("D_out")
        idx_ready = sem("idx_ready")
        g1_idx = sem("g1_idx")
        g1_in = [sem("g1_in0"), sem("g1_in1")]
        g1_free = sem("g1_free")
        row_ps = sem("row_ps")
        row_free = sem("row_free")
        v_ready = sem("v_ready")
        v_ps = sem("v_ps")
        g2_in = [sem("g2_in0"), sem("g2_in1")]
        g2_idx = sem("g2_idx")
        g2_free = sem("g2_free")
        e_arg = sem("e_arg")
        e_exp = sem("e_exp")
        f_ready = sem("f_ready")
        f_ps = sem("f_ps")
        acc_done = sem("acc_done")
        self_arg = sem("self_arg")
        self_exp = sem("self_exp")
        gv_ready = sem("gv_ready")
        gs_ready = sem("gs_ready")
        top_arg = sem("top_arg")
        top_exp = sem("top_exp")
        sq_ps = sem("sq_ps")
        sq_ev = sem("sq_ev")
        sg_ps = sem("sg_ps")
        sg_ev = sem("sg_ev")
        so_ps = sem("so_ps")
        so_ev = sem("so_ev")
        la_ready = sem("la_ready")
        la_ln = sem("la_ln")
        la_sub = sem("la_sub")
        la_exp = sem("la_exp")
        lt_ps = sem("lt_ps")
        lt_ev = sem("lt_ev")
        lo_ps = sem("lo_ps")
        lo_ln = sem("lo_ln")
        lo_arg = sem("lo_arg")
        lo_exp = sem("lo_exp")
        lo_ev = sem("lo_ev")
        h_ready = sem("h_ready")
        out_done = sem("out_done")

        N_W = 32
        block = ctx.enter_context(nc.Block())

        def row(ap, n, parts=P):
            return bass.AP(ap.tensor, 0, [[0, parts], [1, n]])

        @block.sync
        def _(sp):
            xv = x.rearrange("b (t p) c -> p t b c", p=XP)
            for t in range(XT):
                sp.dma_start(xt[:, t, :].rearrange("p (b c) -> p b c", b=B), xv[:, t]).then_inc(x_in, 16)
            ev = edge_index.rearrange("r (p c) -> p r c", p=128)
            sp.dma_start(ebuf[:, :, 0:EC], ev).then_inc(e_in, 16)
            n = 0

            def load(dst, src):
                nonlocal n
                sp.dma_start(dst, src).then_inc(w_in, 16)
                n += 1

            sp.wait_ge(z_ready, 4)
            for k in range(2):
                load(wk2[64 * k:64 * k + 64, 64 * k:64 * k + 64], tok_W_key)
                load(wq2[64 * k:64 * k + 64, 64 * k:64 * k + 64], tok_W_qry)
                load(v2[64 * k:64 * k + 64, k:k + 1], tok_v.rearrange("(p a) -> p a", a=1))
                load(tb[64 * k:64 * k + 64, :], tok_b.rearrange("(p a) -> p a", a=1))
                load(wl[64 * k:64 * k + 64, 0, :], lns_W)
            for k, w in enumerate((attn_Wq, attn_Wk, attn_Wv)):
                load(wraw[:, k, :], w)
            load(bq[:, :], attn_bq.rearrange("(p a) -> p a", a=1))
            load(bk[:, :], attn_bk.rearrange("(p a) -> p a", a=1))
            load(bv_row[:, :], row(attn_bv, C))
            load(wgat[:, :], W_gat)
            load(asrc_row[:, :], row(att_src, HE))
            load(adst_row[:, :], row(att_dst, HE))
            load(bgat_row[:, :], row(b_gat, HE))
            load(gamma_row[:, :], row(ln_gamma, HE))
            load(beta_row[:, :], row(ln_beta, HE))
            load(w1[:, :, :], W1.rearrange("e c f -> c e f"))
            for e in range(E):
                load(b1c[:, e:e + 1], b1[e, :].rearrange("(f a) -> f a", a=1))
            load(w2[:, :, :], W2.rearrange("e f c -> f e c"))
            load(b2_row[:, :], row(b2, E * C))
            load(wsig[:, 0:C], sig_W)
            load(wsig[:, C:2 * C], sig_W)
            load(lbias_row[:, :], row(lns_bias, C))
            assert n == N_W
            for b in range(B):
                sp.dma_start(big[0:P, b * T * WIN * C:(b + 1) * T * WIN * C].rearrange("p (t k) -> p t k", t=T),
                             bass.AP(x.tensor, b * L * C, [[C, P], [P * C, T], [1, WIN * C]])).then_inc(xw_in, 16)
            sp.wait_ge(T_ready, 2)
            sp.dma_start(src_table[0:1, :], zrow[0:1, 0:TW]).then_inc(T_out, 16)
            sp.dma_start(src_table[1:M + 1, :].rearrange("(g p) q -> p g q", p=P), Ts[:, :, :]).then_inc(T_out, 16)
            sp.wait_ge(D_ready, 1)
            sp.dma_start(dst_table.rearrange("(g p) q -> p g q", p=P), Ds[:, :, :]).then_inc(D_out, 16)
            sp.wait_ge(h_ready, B)
            sp.dma_start(out.rearrange("b (t p) c -> p (b t) c", p=P), h[:, :, :]).then_inc(out_done, 16)
            sp.wait_ge(out_done, 16)

        @block.gpsimd
        def _(pool):
            nc.gpsimd.memset(wk2[:, :], 0.0).then_inc(z_ready, 1)
            nc.gpsimd.memset(wq2[:, :], 0.0).then_inc(z_ready, 1)
            nc.gpsimd.memset(v2[:, :], 0.0).then_inc(z_ready, 1)
            nc.gpsimd.memset(wl2[:, :], 0.0).then_inc(z_ready, 1)
            nc.gpsimd.memset(ident[:, :], 0.0)
            nc.gpsimd.memset(tril[:, :], 1.0)
            nc.gpsimd.memset(zrow[:, :], 0.0).then_inc(T_ready, 1)
            pool.drain()
            nc.gpsimd.affine_select(out=ident[:, :], in_=ident[:, :], compare_op=ALU.not_equal, fill=1.0,
                                    base=0, pattern=[[-1, 128]], channel_multiplier=1).then_inc(c_ready, 1)
            nc.gpsimd.affine_select(out=tril[:, :], in_=tril[:, :], compare_op=ALU.is_gt, fill=0.0,
                                    base=0, pattern=[[-1, 128]], channel_multiplier=1).then_inc(c_ready, 1)
            nc.gpsimd.iota(iota_lo[:, :], pattern=[[1, P]], base=0, channel_multiplier=0,
                           allow_small_or_imprecise_dtypes=True).then_inc(c_ready, 1)
            nc.gpsimd.iota(iota_hi[:, :], pattern=[[1, G]], base=0, channel_multiplier=0,
                           allow_small_or_imprecise_dtypes=True).then_inc(c_ready, 1)
            pool.wait_ge(rounds_ready, 1)
            n_pairs = pool.value_load(ni[0:1, 0:1], min_val=1, max_val=EPAD // 16)
            pool.wait_ge(T_out, 32)
            with pool.Fori(0, n_pairs) as i:
                for k in range(2):
                    pool.wait_ge(g1_free, 2 * i + (k + 1))
                    nc.gpsimd.tensor_copy(idx[:, k, 0, :], l_src[:, bass.ds(16 * i + RC * k, RC)])
                    pool.drain()
                    for j in range(RC):
                        nc.gpsimd.indirect_dma_start(
                            gs[:, k, j, :], None, src_table,
                            bass.IndirectOffsetOnAxis(idx[:, k, 0, j:j + 1], 0)).then_inc(g1_in[k], 16)
                    pool.wait_ge(g1_in[k], 128 * i + 128)
            pool.wait_ge(D_out, 16)
            with pool.Fori(0, n_pairs) as i:
                for k in range(2):
                    pool.wait_ge(g2_free, 2 * i + (k + 1))
                    nc.gpsimd.tensor_copy(idx[:, k, 0, :], l_src[:, bass.ds(16 * i + RC * k, RC)])
                    nc.gpsimd.tensor_copy(idx[:, k, 1, :], l_dst[:, bass.ds(16 * i + RC * k, RC)])
                    pool.drain()
                    for j in range(RC):
                        nc.gpsimd.indirect_dma_start(
                            gs[:, k, j, :], None, src_table,
                            bass.IndirectOffsetOnAxis(idx[:, k, 0, j:j + 1], 0)).then_inc(g2_in[k], 16)
                        nc.gpsimd.indirect_dma_start(
                            gd[:, k, j, :], None, dst_table,
                            bass.IndirectOffsetOnAxis(idx[:, k, 1, j:j + 1], 0)).then_inc(g2_in[k], 16)
                    pool.wait_ge(g2_in[k], 256 * i + 256)

        @block.scalar
        def _(act):
            for pr in range(PAIRS):
                act.wait_ge(x_tr, pr + 1)
                for k in range(2):
                    nc.scalar.copy(xT[:, pr, 375 * k:375 * k + 375], ps[:, 2 * pr + k, 0:375]).then_inc(x_ev, 1)
            act.wait_ge(wl_dve, 1)
            nc.scalar.activation(wl[:, 1, :], wl[:, 1, :], ACT.Ln).then_inc(wl_act, 1)
            act.wait_ge(wl_dve, 2)
            nc.scalar.activation(wl2[0:64, 0:64], wl[0:64, 1, :], ACT.Exp).then_inc(wl_act, 1)
            nc.scalar.activation(wl2[64:128, 64:128], wl[64:128, 0, :], ACT.Sign).then_inc(wl_act, 1)
            for pr in range(PAIRS):
                act.wait_ge(kq_ps, pr + 1)
                if pr:
                    act.wait_ge(add_done, WIN)
                for k in range(2):
                    nc.scalar.copy(kT2[:, 375 * k:375 * k + 375], ps[:, 4 + k, 0:375]).then_inc(k_ev, 1)
                for s in range(WIN):
                    n = WIN * pr + s
                    act.wait_ge(add_done, n + 1)
                    nc.scalar.activation(ring[:, n % 3, :], ring[:, n % 3, :], ACT.Tanh).then_inc(tanh_done, 1)
            act.wait_ge(sc_shift, 1)
            nc.scalar.activation(wts[:, :, :], wts[:, :, :], ACT.Exp).then_inc(sc_exp, 1)

            def std(i, n):
                act.wait_ge(var_ready[n], i + 1)
                nc.scalar.activation(st[:, 3, :], st[:, 2, :], ACT.Sqrt).then_inc(std_ready[n], 1)

            def transposed(i, n):
                act.wait_ge(yT_ps[n], i + 1)
                nc.scalar.copy(yT[:, 0:4 * P], ps[0:C, 0, 0:4 * P])
                nc.scalar.copy(yT[:, 4 * P:NW], ps[0:C, 1, 0:3 * P]).then_inc(yT_ev[n], 1)

            with act.Fori(0, B) as i:
                std(i, 0)
                transposed(i, 0)
                act.wait_ge(m_ps, i + 1)
                nc.scalar.copy(qa[C:C + 1, 0:4 * P], ps[C:C + 1, 6, 0:4 * P])
                nc.scalar.copy(qa[C:C + 1, 4 * P:NW], ps[C:C + 1, 7, 0:3 * P]).then_inc(m_ev, 1)
                for t in range(T):
                    act.wait_ge(st_ps, T * i + (t + 1))
                    b0 = 2 * (t % 3)
                    nc.scalar.activation(PT[:, t, :].rearrange("p (a n) -> p a n", a=2),
                                         ps[0:P, b0:b0 + 2, 0:HALF], ACT.Exp, scale=SCALE).then_inc(p_ready, 1)
            with act.Fori(0, B) as i:
                std(i, 1)
                transposed(i, 1)
                for k in range(2 * E):
                    act.wait_ge(hid_ps, 2 * E * i + (k + 1))
                    nc.scalar.activation(HH[:, k // 2, HALF * (k % 2):HALF * (k % 2) + HALF],
                                         ps[:, 4 + k % 4, 0:HALF], ACT.Gelu, bias=b1c[:, k // 2:k // 2 + 1])\
                        .then_inc(hid_ev, 1)
            act.wait_ge(rounds_ready, 1)
            n_pairs = act.value_load(ni[0:1, 0:1], min_val=1, max_val=EPAD // 16)
            with act.Fori(0, n_pairs) as i:
                for k in range(2):
                    act.wait_ge(e_arg, 2 * i + (k + 1))
                    nc.scalar.activation(ew[:, :, :], ew[:, :, :], ACT.Exp).then_inc(e_exp, 1)
            act.wait_ge(self_arg, 1)
            nc.scalar.activation(s4[:, 0], s4[:, 0], ACT.Exp).then_inc(self_exp, 1)
            act.wait_ge(gv_ready, 1)
            nc.scalar.activation(small[:, 2, :], small[:, 1, :], ACT.Sqrt).then_inc(gs_ready, 1)
            act.wait_ge(top_arg, 1)
            nc.scalar.activation(s4[:, 2], s4[:, 2], ACT.Exp).then_inc(top_exp, 1)
            with act.Fori(0, B) as i:
                std(i, 2)
                transposed(i, 2)
                act.wait_ge(sq_ps, i + 1)
                nc.scalar.copy(qa[0:C, :].rearrange("p (a n) -> p a n", a=2), ps[0:C, 2:4, 0:HALF]).then_inc(sq_ev, 1)
                for t in range(T):
                    act.wait_ge(sg_ps, T * i + (t + 1))
                    b0 = 4 + 2 * (t % 2)
                    nc.scalar.activation(PT[:, t, :].rearrange("p (a n) -> p a n", a=2),
                                         ps[0:P, b0:b0 + 2, 0:HALF], ACT.Sigmoid).then_inc(sg_ev, 1)
            with act.Fori(0, B) as i:
                std(i, 3)
                act.wait_ge(la_ready, i + 1)
                nc.scalar.activation(sq[:, :, :], sq[:, :, :], ACT.Ln).then_inc(la_ln, 1)
                act.wait_ge(la_sub, i + 1)
                nc.scalar.activation(PT[:, 0:T, 0:C], sq[:, :, :], ACT.Exp)
                nc.scalar.activation(PT[:, 0:T, C:2 * C], yb[:, :, :], ACT.Sign).then_inc(la_exp, 1)
                act.wait_ge(lt_ps, i + 1)
                nc.scalar.copy(ring[:, 0, 0:4 * P], ps[:, 0, 0:4 * P])
                nc.scalar.copy(ring[:, 0, 4 * P:NW], ps[:, 1, 0:3 * P]).then_inc(lt_ev, 1)
                act.wait_ge(lo_ps, i + 1)
                for b0, t0, t1 in ((2, 0, 4), (3, 4, 7)):
                    v = ps[0:P, b0, 0:128 * (t1 - t0)].rearrange("p (t c) -> p t c", c=128)
                    nc.scalar.activation(cen[:, t0:t1, :], v[:, :, 0:C], ACT.Ln)
                    ins = nc.scalar.activation(sq[:, t0:t1, :], v[:, :, C:2 * C], ACT.Sign)
                ins.then_inc(lo_ln, 1)
                act.wait_ge(lo_arg, i + 1)
                nc.scalar.activation(cen[:, :, :], cen[:, :, :], ACT.Exp).then_inc(lo_exp, 1)

        @block.vector
        def _(dve):
            V = nc.vector
            dve.wait_ge(e_in, 16)
            V.tensor_copy(l_lo[:, 0:EC], ebuf[:, 0, 0:EC])
            V.tensor_copy(l_hi[:, 0:EC], ebuf[:, 1, 0:EC])
            dve.drain()
            V.tensor_scalar(l_lo[:, 0:EC], l_lo[:, 0:EC], float(M - 1), 1.0, ALU.min, ALU.add)
            dve.drain()
            V.scalar_tensor_tensor(key[:, :], l_hi[:, 0:EC], float(KS), l_lo[:, 0:EC], ALU.mult, ALU.add)
            dve.drain()
            V.scalar_tensor_tensor(key[:, :], l_hi[:, 0:EC], float(M), key[:, :], ALU.is_lt, ALU.mult)
            dve.drain()
            V.tensor_scalar(l_lo[:, 0:EC], key[:, :], 0.0, 0.0, ALU.is_gt, ALU.add,
                            accum_out=cnt[:, :]).then_inc(cnt_ready, 1)
            dve.wait_ge(cnt_row, 1)
            V.tensor_reduce(nf[:, 0:1], ps[0:1, 7, 0:128], AX.X, ALU.max)
            dve.drain()
            V.tensor_scalar(nf[:, 1:2], nf[:, 0:1], 1.0 / 16, 15.0 / 16 - 0.5 + 1.0 / 64, ALU.mult, ALU.add)
            dve.drain()
            V.tensor_scalar(nf[:, 0:1], nf[:, 1:2], ROUND, -ROUND, ALU.add, ALU.add)
            dve.drain()
            V.tensor_scalar(ni[:, :], nf[:, 0:1], 1.0, None, ALU.max).then_inc(rounds_ready, 1)
            dve.wait_ge(rounds_ready, 1)
            dve.wait_ge(c_ready, 4)
            dve.wait_ge(w_in, 16 * N_W)
            V.scalar_tensor_tensor(wl[:, 1, :], wl[:, 0, :], -1.0, wl[:, 0, :], ALU.mult, ALU.max)
            dve.drain()
            V.tensor_scalar(wl[:, 1, :], wl[:, 1, :], 1e-8, None, ALU.add).then_inc(wl_dve, 1)
            dve.wait_ge(wl_act, 1)
            V.tensor_reduce(mw[:, :], wl[:, 1, :], AX.X, ALU.max)
            dve.drain()
            V.tensor_scalar(wl[:, 1, :], wl[:, 1, :], mw[:, 0:1], None, ALU.subtract).then_inc(wl_dve, 1)
            n_pairs = dve.value_load(ni[0:1, 0:1], min_val=1, max_val=EPAD // 16)
            with dve.Fori(0, n_pairs) as i:
                for k in range(2):
                    at = bass.ds(16 * i + RC * k, RC)
                    V.max(m8[:, :], key[:, :])
                    dve.drain()
                    V.match_replace(key[:, :], m8[:, :], key[:, :], 0.0)
                    V.tensor_copy(ki[:, 0, :], m8[:, :])
                    dve.drain()
                    V.tensor_scalar(l_src[:, at], ki[:, 0, :], KS - 1, None, ALU.bitwise_and)
                    V.tensor_scalar(l_dst[:, at], ki[:, 0, :], 12, None, ALU.logical_shift_right)
                    V.tensor_scalar(ki[:, 1, :], ki[:, 0, :], 12, None, ALU.logical_shift_right)
                    dve.drain()
                    V.tensor_copy(kf[:, 0, :], ki[:, 1, :])
                    V.tensor_scalar(kf[:, 3, :], m8[:, :], 1.0, 1000.0, ALU.is_lt, ALU.mult)
                    dve.drain()
                    V.tensor_scalar(kf[:, 1, :], kf[:, 0, :], 0.5, 1.0 / P, ALU.add, ALU.mult)
                    dve.drain()
                    V.tensor_scalar(kf[:, 1, :], kf[:, 1, :], -0.5, ROUND, ALU.add, ALU.add)
                    dve.drain()
                    V.tensor_scalar(kf[:, 2, :], kf[:, 1, :], -ROUND, None, ALU.add)
                    dve.drain()
                    V.tensor_copy(l_hi[:, at], kf[:, 2, :])
                    V.scalar_tensor_tensor(kf[:, 1, :], kf[:, 2, :], float(-P), kf[:, 0, :], ALU.mult, ALU.add)
                    dve.drain()
                    V.tensor_tensor(l_lo[:, at], kf[:, 1, :], kf[:, 3, :], ALU.add)
                dve.drain()
            for pr in range(PAIRS):
                dve.wait_ge(kq_ps, pr + 1)
                V.tensor_scalar(qT2[:, 0:HALF], ps[:, 6, 0:HALF], tb[:, 0:1], None, ALU.add)
                V.tensor_scalar(qT2[:, HALF:NW], ps[:, 7, 0:HALF], tb[:, 0:1], None, ALU.add).then_inc(q_ev, 1)
                dve.drain()
                dve.wait_ge(k_ev, 2 * pr + 2)
                for s in range(WIN):
                    n = WIN * pr + s
                    if n >= 3:
                        dve.wait_ge(sc_ps, n - 2)
                    V.tensor_tensor(ring[:, n % 3, :], kT2[:, s:s + NW], qT2[:, :], ALU.add).then_inc(add_done, 1)
            dve.wait_ge(wT_ps, 1)
            V.tensor_copy(wT[:, :, :], ps[0:C, 1, 0:3 * C].rearrange("p (k c) -> p k c", k=3))
            V.tensor_copy(wlT[:, :], ps[:, 1, 3 * C:3 * C + 128])
            V.tensor_copy(mw_row[:, :], ps[0:P, 1, 320:320 + C])
            V.memset(ka[C:C + 1, :], 1.0)
            V.memset(va[:, :, C:C + 1], 1.0).then_inc(w_prep, 1)
            dve.wait_ge(sc_ps, 2 * WIN)
            for pr in range(PAIRS):
                for bb in range(2):
                    b = 2 * pr + bb
                    V.tensor_copy(wts[:, T * b:T * b + T, :],
                                  ps[0:P, 2 * pr, 0:2 * T * WIN].rearrange("p (b t s) -> p b t s", b=2, s=WIN)[:, bb])
            dve.drain()
            V.tensor_reduce(wsm[:, :], wts[:, :, :], AX.X, ALU.max)
            dve.drain()
            V.tensor_tensor(wts[:, :, :], wts[:, :, :], wsm[:, :].to_broadcast([P, G, WIN]), ALU.subtract).then_inc(sc_shift, 1)
            dve.wait_ge(sc_exp, 1)
            V.tensor_reduce(wsm[:, :], wts[:, :, :], AX.X, ALU.add)
            dve.drain()
            V.reciprocal(wsm[:, :], wsm[:, :])
            dve.drain()
            V.tensor_tensor(wts[:, :, :], wts[:, :, :], wsm[:, :].to_broadcast([P, G, WIN]), ALU.mult)
            dve.drain()
            dve.wait_ge(xw_in, 16 * B)
            V.tensor_tensor(xw, xw, wts[:, :, :].to_broadcast([P, G, WIN, C]), ALU.mult)
            dve.drain()
            V.tensor_reduce(h[:, :, :], xw.rearrange("p g s c -> p g c s"), AX.X, ALU.add)
            dve.drain()

            def normed(i, n):
                hb = h[:, bass.ds(i * T, T), :]
                V.tensor_reduce(st[:, 0, :], hb, AX.X, ALU.add)
                dve.drain()
                V.tensor_scalar(st[:, 1, :], st[:, 0, :], 1.0 / C, None, ALU.mult)
                dve.drain()
                V.tensor_tensor(cen[:, :, :], hb, st[:, 1, :].to_broadcast([P, T, C]), ALU.subtract)
                dve.drain()
                V.tensor_tensor(sq[:, :, :], cen[:, :, :], cen[:, :, :], ALU.mult)
                dve.drain()
                V.tensor_reduce(st[:, 0, :], sq[:, :, :], AX.X, ALU.add)
                dve.drain()
                V.tensor_scalar(st[:, 2, :], st[:, 0, :], 1.0 / C, 1e-5, ALU.mult, ALU.add).then_inc(var_ready[n], 1)
                dve.wait_ge(std_ready[n], i + 1)
                V.reciprocal(st[:, 0, :], st[:, 3, :])
                dve.drain()
                V.tensor_tensor(yb[:, :, :], cen[:, :, :], st[:, 0, :].to_broadcast([P, T, C]), ALU.mult)\
                    .then_inc(y_ready[n], 1)
                dve.drain()

            with dve.Fori(0, B) as i:
                normed(i, 0)
                dve.wait_ge(qkv_ps, i + 1)
                V.tensor_scalar(qa[0:C, :].rearrange("p (a n) -> p a n", a=2), ps[0:C, 2:4, 0:HALF], bq[:, 0:1], None, ALU.add)
                V.tensor_scalar(ka[0:C, :].rearrange("p (a n) -> p a n", a=2), ps[0:C, 4:6, 0:HALF], bk[:, 0:1], None, ALU.add)
                V.tensor_tensor(va[:, :, 0:C], ps[0:P, 6, 0:T * C].rearrange("p (t c) -> p t c", t=T),
                                bv_row[:, :].unsqueeze(1).to_broadcast([P, T, C]), ALU.add).then_inc(qkv_ev, 1)
                for t in range(T):
                    dve.wait_ge(s_ps, T * i + (t + 1))
                    b0 = 2 * (t % 2)
                    V.tensor_reduce(nm[:, t:t + 1], ps[0:P, b0:b0 + 2, 0:HALF], AX.XY, ALU.max, negate=True).then_inc(s_max, 1)
                dve.wait_ge(o_ps, i + 1)
                O = ps[0:P, 6, 0:T * (C + 1)].rearrange("p (t c) -> p t c", t=T)
                V.reciprocal(rd[:, :], O[:, :, C])
                dve.drain()
                V.tensor_tensor(cen[:, :, :], O[:, :, 0:C], rd[:, :].to_broadcast([P, T, C]), ALU.mult).then_inc(o_ev, 1)
                dve.drain()
                hb = h[:, bass.ds(i * T, T), :]
                V.tensor_tensor(hb, hb, cen[:, :, :], ALU.add)
                dve.drain()
            with dve.Fori(0, B) as i:
                normed(i, 1)
                dve.wait_ge(gat_ps, i + 1)
                V.tensor_copy(hg[:, bass.ds(i * T, T), :], ps[0:P, 2, 0:T * HE].rearrange("p (t q) -> p t q", t=T)).then_inc(gat_ev, 1)
                for t in range(T):
                    dve.wait_ge(ex_ps, T * i + (t + 1))
                    V.tensor_tensor(Oe[:, bass.ds(i * T + t, 1), :, :].rearrange("p g e c -> p (g e c)"),
                                    ps[0:P, 2 + t % 2, 0:E * C], b2_row[:, :], ALU.add).then_inc(ex_ev, 1)
                dve.drain()
            V.tensor_copy(Ts[:, :, H:TW], hg[:, :, :])
            V.tensor_tensor(tmp16[:, :, :], hg[:, :, :], asrc_row[:, :].unsqueeze(1).to_broadcast([P, G, HE]), ALU.mult)
            dve.drain()
            V.tensor_reduce(Ts[:, :, 0:H], tmp16[:, :, :].rearrange("p g (h k) -> p g h k", h=H), AX.X, ALU.add).then_inc(T_ready, 1)
            dve.drain()
            V.tensor_tensor(tmp16[:, :, :], hg[:, :, :], adst_row[:, :].unsqueeze(1).to_broadcast([P, G, HE]), ALU.mult)
            dve.drain()
            V.tensor_reduce(Ds[:, :, 0:H], tmp16[:, :, :].rearrange("p g (h k) -> p g h k", h=H), AX.X, ALU.add)
            V.tensor_copy(Mx[:, :, :], Ts[:, :, 0:H].rearrange("p g q -> p q g"))
            V.memset(cm[:, H:H + 1], 1.0)
            dve.drain()
            V.memset(scr[0:1, 0, 0:1], 0.0).then_inc(g1_free, 2)

            def decode(i, k):
                at = bass.ds(16 * i + RC * k, RC)
                V.tensor_copy(col[:, k, 0, :], l_lo[:, at])
                V.tensor_copy(col[:, k, 1, :], l_hi[:, at])
                V.tensor_copy(dcol[:, k, :], l_dst[:, at])
                dve.drain()
                for j in range(RC):
                    V.tensor_scalar(ohhi[:, j, :], iota_hi[:, :], col[:, k, 1, j:j + 1], None, ALU.is_equal)
                dve.drain()

            with dve.Fori(0, n_pairs) as i:
                for k in range(2):
                    decode(i, k)
                    V.memset(neg[0:1, 0:1], 0.0).then_inc(idx_ready, 1)
                    for j in range(RC):
                        n = RC * k + j
                        rows = ps[:, 2 * (j % 2), :]
                        drow = ps[:, 2 * (j % 2) + 1, 0:128]
                        dve.wait_ge(row_ps, 16 * i + (n + 1))
                        V.tensor_scalar(neg[:, :], drow, dcol[:, k, j:j + 1], -BIG, ALU.not_equal, ALU.mult)
                        V.scalar_tensor_tensor(scr[:, H, :], drow, dcol[:, k, j:j + 1], tril[:, :], ALU.is_equal, ALU.mult,
                                               accum_out=lead[:, 0:1])
                        dve.drain()
                        V.tensor_scalar(lead[:, 1:2], lead[:, 0:1], 0.5, None, ALU.is_lt)
                        for q in range(H):
                            V.tensor_tensor_reduce(out=scr[:, q, :], in0=rows[:, 128 * q:128 * q + 128], in1=neg[:, :], scale=1.0,
                                                   scalar=-BIG, op0=ALU.add, op1=ALU.max, accum_out=cm[:, q:q + 1])
                        dve.drain()
                        V.tensor_scalar(ohlo[:, j % 2, :], iota_lo[:, :], col[:, k, 0, j:j + 1], lead[:, 1:2],
                                        ALU.is_equal, ALU.mult).then_inc(row_free, 1)
                        V.tensor_tensor(vr[:, j % 2, 0:H + 1, :], cm[:, :].to_broadcast([128, H + 1, G]),
                                        ohhi[:, j, :].unsqueeze(1).to_broadcast([128, H + 1, G]), ALU.mult).then_inc(v_ready, 1)
                        dve.wait_ge(v_ps, 16 * i + (n + 1))
                        vp = ps[0:P, 4 + j % 2, 0:(H + 1) * G].rearrange("p (q g) -> p q g", q=H + 1)
                        V.tensor_scalar(nb[:, :], vp[:, H, :], -1.0, BIG, ALU.add, ALU.mult)
                        dve.drain()
                        V.tensor_tensor(cand[:, :, :], vp[:, 0:H, :], nb[:, :].unsqueeze(1).to_broadcast([P, H, G]), ALU.add)
                        dve.drain()
                        V.tensor_tensor(Mx[:, :, :], Mx[:, :, :], cand[:, :, :], ALU.max)
                        dve.drain()
                    V.memset(neg[0:1, 0:1], 0.0).then_inc(g1_free, 1)
            V.tensor_tensor(s4[:, 0].rearrange("p g q -> p q g"), Mx[:, :, :], Ds[:, :, 0:H].rearrange("p g q -> p q g"), ALU.add)
            dve.drain()
            V.scalar_tensor_tensor(Ds[:, :, H:DW], s4[:, 0], 0.2, s4[:, 0], ALU.mult, ALU.max).then_inc(D_ready, 1)
            V.tensor_tensor(s4[:, 1], Ts[:, :, 0:H], Ds[:, :, 0:H], ALU.add)
            dve.drain()
            V.scalar_tensor_tensor(s4[:, 2], s4[:, 1], 0.2, s4[:, 1], ALU.mult, ALU.max)
            dve.drain()
            V.tensor_tensor(s4[:, 0], s4[:, 2], Ds[:, :, H:DW], ALU.subtract)
            V.memset(scr[0:1, 0, 0:1], 0.0).then_inc(g2_free, 2)
            with dve.Fori(0, n_pairs) as i:
                for k in range(2):
                    decode(i, k)
                    dve.wait_ge(g2_in[k], 256 * i + 256)
                    V.tensor_tensor(fe[:, :, 0:H], gs[:, k, :, 0:H], gd[:, k, :, 0:H], ALU.add)
                    dve.drain()
                    V.scalar_tensor_tensor(fe[:, :, H:2 * H], fe[:, :, 0:H], 0.2, fe[:, :, 0:H], ALU.mult, ALU.max)
                    dve.drain()
                    V.tensor_tensor(fe[:, :, 0:H], fe[:, :, H:2 * H], gd[:, k, :, H:DW], ALU.subtract)
                    dve.drain()
                    V.tensor_scalar(ew[:, :, :], fe[:, :, 0:H], 0.0, None, ALU.min).then_inc(e_arg, 1)
                    dve.wait_ge(e_exp, 2 * i + (k + 1))
                    V.tensor_copy(fe[:, :, 0:H], ew[:, :, :])
                    for q in range(H):
                        V.tensor_tensor(fe[:, :, H + E * q:H + E * (q + 1)], gs[:, k, :, H + E * q:H + E * (q + 1)],
                                        ew[:, :, q:q + 1].to_broadcast([128, RC, E]), ALU.mult)
                    dve.drain()
                    V.memset(neg[0:1, 0:1], 0.0).then_inc(g2_free, 1)
                    for j in range(RC):
                        n = RC * k + j
                        dve.wait_ge(f_ps, 16 * i + (n + 1))
                        V.tensor_scalar(ohlo[:, j % 2, :], iota_lo[:, :], col[:, k, 0, j:j + 1], None, ALU.is_equal)
                        V.tensor_tensor(vr[:, j % 2], fe[:, j, :].to_broadcast([128, TW, G]),
                                        ohhi[:, j, :].unsqueeze(1).to_broadcast([128, TW, G]), ALU.mult).then_inc(f_ready, 1)
                    dve.drain()
            V.memset(scr[0:1, 0, 0:1], 0.0).then_inc(self_arg, 1)
            dve.wait_ge(self_exp, 1)
            dve.wait_ge(acc_done, 1)
            accA = ps[0:P, 6, 0:10 * G].rearrange("p (q g) -> p g q", g=G)
            accB = ps[0:P, 7, 0:10 * G].rearrange("p (q g) -> p g q", g=G)
            V.tensor_tensor(s4[:, 1], s4[:, 0], accA[:, :, 0:H], ALU.add)
            for q in range(H):
                V.tensor_tensor(tmp16[:, :, E * q:E * (q + 1)], hg[:, :, E * q:E * (q + 1)],
                                s4[:, 0, :, q:q + 1].to_broadcast([P, G, E]), ALU.mult)
            dve.drain()
            V.tensor_tensor(tmp16[:, :, 0:6], tmp16[:, :, 0:6], accA[:, :, H:10], ALU.add)
            V.tensor_tensor(tmp16[:, :, 6:16], tmp16[:, :, 6:16], accB, ALU.add)
            V.tensor_scalar(s4[:, 2], s4[:, 1], 1e-16, None, ALU.add)
            dve.drain()
            V.reciprocal(s4[:, 1], s4[:, 2])
            dve.drain()
            for q in range(H):
                V.tensor_tensor(tmp16[:, :, E * q:E * (q + 1)], tmp16[:, :, E * q:E * (q + 1)],
                                s4[:, 1, :, q:q + 1].to_broadcast([P, G, E]), ALU.mult)
            dve.drain()

            def bc16(r):
                return r[:, :].unsqueeze(1).to_broadcast([P, G, HE])

            def each(a):
                return a.to_broadcast([P, G, HE])

            V.tensor_tensor(tmp16[:, :, :], tmp16[:, :, :], bc16(bgat_row), ALU.add)
            dve.drain()
            V.tensor_reduce(small[:, 0, :], tmp16[:, :, :], AX.X, ALU.add)
            dve.drain()
            V.tensor_scalar(small[:, 0, :], small[:, 0, :], 1.0 / HE, None, ALU.mult)
            dve.drain()
            V.tensor_tensor(tmp16[:, :, :], tmp16[:, :, :], each(small[:, 0, :]), ALU.subtract)
            dve.drain()
            V.tensor_tensor(hg[:, :, :], tmp16[:, :, :], tmp16[:, :, :], ALU.mult)
            dve.drain()
            V.tensor_reduce(small[:, 0, :], hg[:, :, :], AX.X, ALU.add)
            dve.drain()
            V.tensor_scalar(small[:, 1, :], small[:, 0, :], 1.0 / HE, 1e-5, ALU.mult, ALU.add).then_inc(gv_ready, 1)
            dve.wait_ge(gs_ready, 1)
            V.reciprocal(small[:, 3, :], small[:, 2, :])
            dve.drain()
            V.tensor_tensor(tmp16[:, :, :], tmp16[:, :, :], each(small[:, 3, :]), ALU.mult)
            dve.drain()
            V.tensor_tensor(tmp16[:, :, :], tmp16[:, :, :], bc16(gamma_row), ALU.mult)
            dve.drain()
            V.tensor_tensor(tmp16[:, :, :], tmp16[:, :, :], bc16(beta_row), ALU.add)
            dve.drain()
            V.tensor_reduce(s4[:, 0], tmp16[:, :, :].rearrange("p g (h k) -> p g k h", h=H), AX.X, ALU.add)
            dve.drain()
            V.tensor_scalar(s4[:, 1], s4[:, 0], 1.0 / H, None, ALU.mult)
            dve.drain()
            V.tensor_reduce(small[:, 0, :], s4[:, 1], AX.X, ALU.max)
            for e in range(E):
                first = True
                for f in range(E):
                    if f == e:
                        continue
                    V.tensor_tensor(small[:, 4, :] if not first else s4[:, 3, :, e], s4[:, 1, :, f], s4[:, 1, :, e],
                                    ALU.is_ge if f < e else ALU.is_gt)
                    dve.drain()
                    if not first:
                        V.tensor_tensor(s4[:, 3, :, e], s4[:, 3, :, e], small[:, 4, :], ALU.add)
                        dve.drain()
                    first = False
            V.tensor_tensor(s4[:, 2], s4[:, 1], small[:, 0, :].to_broadcast([P, G, E]), ALU.subtract).then_inc(top_arg, 1)
            dve.wait_ge(top_exp, 1)
            V.scalar_tensor_tensor(s4[:, 4], s4[:, 3], 1.5, s4[:, 2], ALU.is_lt, ALU.mult)
            dve.drain()
            V.tensor_reduce(small[:, 5, :], s4[:, 4], AX.X, ALU.add)
            dve.drain()
            V.reciprocal(small[:, 6, :], small[:, 5, :])
            dve.drain()
            V.tensor_tensor(s4[:, 5], s4[:, 4], small[:, 6, :].to_broadcast([P, G, E]), ALU.mult)
            dve.drain()
            V.tensor_tensor(Oe, Oe, s4[:, 5].to_broadcast([P, G, E, C]), ALU.mult)
            dve.drain()
            mix = xw_mix = big[0:P, 0:G * C].rearrange("p (g c) -> p g c", g=G)
            V.tensor_reduce(mix, Oe.rearrange("p g e c -> p g c e"), AX.X, ALU.add)
            dve.drain()
            V.tensor_tensor(h[:, :, :], h[:, :, :], mix, ALU.add)
            dve.drain()
            with dve.Fori(0, B) as i:
                normed(i, 2)
                dve.wait_ge(so_ps, i + 1)
                hb = h[:, bass.ds(i * T, T), :]
                V.tensor_tensor(hb, hb, ps[0:P, 2, 0:T * C].rearrange("p (t c) -> p t c", t=T), ALU.add).then_inc(so_ev, 1)
                dve.drain()
            with dve.Fori(0, B) as i:
                normed(i, 3)
                V.scalar_tensor_tensor(sq[:, :, :], yb[:, :, :], -1.0, yb[:, :, :], ALU.mult, ALU.max)
                dve.drain()
                V.tensor_scalar(sq[:, :, :], sq[:, :, :], 1e-8, None, ALU.add).then_inc(la_ready, 1)
                dve.wait_ge(la_ln, i + 1)
                V.tensor_reduce(nm[:, :], sq[:, :, :], AX.X, ALU.max)
                dve.drain()
                V.tensor_tensor(sq[:, :, :], sq[:, :, :], nm[:, :].to_broadcast([P, T, C]), ALU.subtract).then_inc(la_sub, 1)
                dve.wait_ge(lo_ln, i + 1)
                V.tensor_tensor(cen[:, :, :], cen[:, :, :], nm[:, :].to_broadcast([P, T, C]), ALU.add)
                dve.drain()
                V.tensor_tensor(cen[:, :, :], cen[:, :, :], mw_row[:, :].unsqueeze(1).to_broadcast([P, T, C]), ALU.add).then_inc(lo_arg, 1)
                dve.wait_ge(lo_exp, i + 1)
                V.tensor_tensor(cen[:, :, :], cen[:, :, :], sq[:, :, :], ALU.mult)
                dve.drain()
                V.tensor_tensor(cen[:, :, :], cen[:, :, :], lbias_row[:, :].unsqueeze(1).to_broadcast([P, T, C]), ALU.add)
                dve.drain()
                hb = h[:, bass.ds(i * T, T), :]
                V.tensor_tensor(hb, hb, cen[:, :, :], ALU.add).then_inc(h_ready, 1)
                dve.drain()

        @block.tensor
        def _(pe):
            mm = nc.tensor.matmul

            def turn(out_, in_):
                n = in_.shape[0]
                return mm(out_, in_, ident[0:n, 0:n], start=True, stop=True)

            pe.wait_ge(c_ready, 4)
            pe.wait_ge(x_in, 16 * XT)
            for pr in range(PAIRS):
                for t in range(XT):
                    ins = turn(ps[:, 2 * pr + t // 3, XP * (t % 3):XP * (t % 3) + XP], xt[:, t, 128 * pr:128 * pr + 128])
                ins.then_inc(x_tr, 1)
            pe.wait_ge(w_in, 16 * N_W)
            pe.wait_ge(cnt_ready, 1)
            for pr in range(PAIRS):
                pe.wait_ge(x_ev, 2 * pr + 2)
                if pr:
                    pe.wait_ge(k_ev, 2)
                    pe.wait_ge(q_ev, 1)
                else:
                    mm(ps[0:1, 7, 0:128], cnt[:, :], ident[:, :], start=True, stop=True).then_inc(cnt_row, 1)
                    pe.wait_ge(rounds_ready, 1)
                for k in range(2):
                    mm(ps[:, 4 + k, 0:375], wk2[:, :], xT[:, pr, 375 * k:375 * k + 375], start=True, stop=True)
                for k in range(2):
                    o = WIN // 2 + HALF * k
                    ins = mm(ps[:, 6 + k, 0:HALF], wq2[:, :], xT[:, pr, o:o + HALF], start=True, stop=True)
                ins.then_inc(kq_ps, 1)
                if pr == 0:
                    pe.wait_ge(wl_act, 3)
                    pe.wait_ge(x_ev, 4)
                    for k in range(3):
                        turn(ps[0:C, 1, C * k:C * k + C], wraw[:, k, :])
                    turn(ps[:, 1, 3 * C:3 * C + 128], wl2[:, :])
                    mm(ps[0:P, 1, 320:320 + C], mw[0:C, 0:1].to_broadcast([C, P]), ident[0:C, 0:C],
                       start=True, stop=True).then_inc(wT_ps, 1)
                sc = ps[0:P, 2 * pr, 0:2 * T * WIN].rearrange("p (b t s) -> p b t s", b=2, s=WIN)
                for s in range(WIN):
                    n = WIN * pr + s
                    pe.wait_ge(tanh_done, n + 1)
                    for t in range(T):
                        ins = mm(sc[:, :, t, s], tile(ring[:, n % 3, :], t), v2[:, :], start=True, stop=True)
                    ins.then_inc(sc_ps, 1)

            def turn_batch(i, n):
                pe.wait_ge(y_ready[n], i + 1)
                for t in range(T):
                    ins = turn(ps[0:C, t // 4, P * (t % 4):P * (t % 4) + P], yb[:, t, :])
                ins.then_inc(yT_ps[n], 1)
                pe.wait_ge(yT_ev[n], i + 1)

            pe.wait_ge(w_prep, 1)
            with pe.Fori(0, B) as i:
                turn_batch(i, 0)
                for t in range(T):
                    mm(ps[0:P, 6, C * t:C * t + C], tile(yT, t), wT[:, 2, :], start=True, stop=True)
                for k in range(2):
                    mm(ps[0:C, 2 + k, 0:HALF], wT[:, 0, :], yT[:, HALF * k:HALF * k + HALF], start=True, stop=True)
                    ins = mm(ps[0:C, 4 + k, 0:HALF], wT[:, 1, :], yT[:, HALF * k:HALF * k + HALF], start=True, stop=True)
                ins.then_inc(qkv_ps, 1)
                pe.wait_ge(qkv_ev, i + 1)
                for t in range(T):
                    if t >= 2:
                        pe.wait_ge(s_max, T * i + (t - 1))
                    for k in range(2):
                        ins = mm(ps[0:P, 2 * (t % 2) + k, 0:HALF], tile(qa[0:C, :], t), ka[0:C, HALF * k:HALF * k + HALF],
                                 start=True, stop=True)
                    ins.then_inc(s_ps, 1)
                pe.wait_ge(s_max, T * i + T)
                for t in range(T):
                    ins = mm(ps[C:C + 1, 6 + t // 4, P * (t % 4):P * (t % 4) + P], nm[:, t:t + 1], ident[0:P, 0:P],
                             start=True, stop=True)
                ins.then_inc(m_ps, 1)
                pe.wait_ge(m_ev, i + 1)
                for t in range(T):
                    if t >= 3:
                        pe.wait_ge(p_ready, T * i + (t - 2))
                    for k in range(2):
                        ins = mm(ps[0:P, 2 * (t % 3) + k, 0:HALF], tile(ka, t), qa[:, HALF * k:HALF * k + HALF],
                                 start=True, stop=True)
                    ins.then_inc(st_ps, 1)
                pe.wait_ge(p_ready, T * i + T)
                for t in range(T):
                    for u in range(T):
                        ins = mm(ps[0:P, 6, (C + 1) * t:(C + 1) * (t + 1)], tile(PT[:, u, :], t), va[:, u, :],
                                 start=(u == 0), stop=(u == T - 1))
                ins.then_inc(o_ps, 1)
                pe.wait_ge(o_ev, i + 1)
            with pe.Fori(0, B) as i:
                turn_batch(i, 1)
                for t in range(T):
                    ins = mm(ps[0:P, 2, HE * t:HE * t + HE], tile(yT, t), wgat[:, :], start=True, stop=True)
                ins.then_inc(gat_ps, 1)
                for k in range(2 * E):
                    if k >= 4:
                        pe.wait_ge(hid_ev, 2 * E * i + (k - 3))
                    mm(ps[:, 4 + k % 4, 0:HALF], w1[:, k // 2, :], yT[:, HALF * (k % 2):HALF * (k % 2) + HALF],
                       start=True, stop=True).then_inc(hid_ps, 1)
                pe.wait_ge(hid_ev, 2 * E * i + 2 * E)
                pe.wait_ge(gat_ev, i + 1)
                for t in range(T):
                    if t >= 2:
                        pe.wait_ge(ex_ev, T * i + (t - 1))
                    for e in range(E):
                        ins = mm(ps[0:P, 2 + t % 2, C * e:C * e + C], tile(HH[:, e, :], t), w2[:, e, :], start=True, stop=True)
                    ins.then_inc(ex_ps, 1)
                pe.wait_ge(ex_ev, T * i + T)
            pe.wait_ge(rounds_ready, 1)
            n_pairs = pe.value_load(ni[0:1, 0:1], min_val=1, max_val=EPAD // 16)
            with pe.Fori(0, n_pairs) as i:
                for k in range(2):
                    pe.wait_ge(g1_in[k], 128 * i + 128)
                    pe.wait_ge(idx_ready, 2 * i + (k + 1))

                    def spread(j):
                        for q in range(H):
                            mm(ps[:, 2 * (j % 2), 128 * q:128 * q + 128], gs[:, k, j, q:q + 1].to_broadcast([128, 128]),
                               ident[:, :], start=True, stop=True)
                        mm(ps[:, 2 * (j % 2) + 1, 0:128], dcol[:, k, j:j + 1].to_broadcast([128, 128]),
                           ident[:, :], start=True, stop=True).then_inc(row_ps, 1)

                    spread(0)
                    for j in range(RC):
                        n = RC * k + j
                        if j + 1 < RC:
                            if j >= 1:
                                pe.wait_ge(row_free, 16 * i + n)
                            spread(j + 1)
                        pe.wait_ge(v_ready, 16 * i + (n + 1))
                        mm(ps[0:P, 4 + j % 2, 0:(H + 1) * G], ohlo[:, j % 2, :], vr[:, j % 2, 0:H + 1, :].rearrange("p q g -> p (q g)"),
                           start=True, stop=True).then_inc(v_ps, 1)
            for b0 in (6, 7):
                ins = mm(ps[0:P, b0, 0:10 * G], zrow[0:1, 0:P], zrow[0:1, 0:10 * G], start=True, stop=False)
            ins.then_inc(f_ps, 2)
            with pe.Fori(0, n_pairs) as i:
                for k in range(2):
                    for j in range(RC):
                        n = RC * k + j
                        pe.wait_ge(f_ready, 16 * i + (n + 1))
                        for a in range(2):
                            ins = mm(ps[0:P, 6 + a, 0:10 * G], ohlo[:, j % 2, :],
                                     vr[:, j % 2, 10 * a:10 * a + 10, :].rearrange("p q g -> p (q g)"), start=False, stop=False)
                        ins.then_inc(f_ps, 1)
            for b0 in (6, 7):
                ins = mm(ps[0:P, b0, 0:10 * G], zrow[0:1, 0:P], zrow[0:1, 0:10 * G], start=False, stop=True)
            ins.then_inc(acc_done, 1)
            with pe.Fori(0, B) as i:
                turn_batch(i, 2)
                for k in range(2):
                    ins = mm(ps[:, 2 + k, 0:HALF], wsig[:, :], yT[:, HALF * k:HALF * k + HALF], start=True, stop=True)
                ins.then_inc(sq_ps, 1)
                pe.wait_ge(sq_ev, i + 1)
                for t in range(T):
                    if t >= 2:
                        pe.wait_ge(sg_ev, T * i + (t - 1))
                    for k in range(2):
                        ins = mm(ps[0:P, 4 + 2 * (t % 2) + k, 0:HALF], tile(yT, t), qa[0:C, HALF * k:HALF * k + HALF],
                                 start=True, stop=True)
                    ins.then_inc(sg_ps, 1)
                pe.wait_ge(sg_ev, T * i + T)
                for t in range(T):
                    for u in range(T):
                        ins = mm(ps[0:P, 2, C * t:C * t + C], tile(PT[:, u, :], t), yb[:, u, :],
                                 start=(u == 0), stop=(u == T - 1))
                ins.then_inc(so_ps, 1)
                pe.wait_ge(so_ev, i + 1)
            with pe.Fori(0, B) as i:
                pe.wait_ge(la_exp, i + 1)
                for t in range(T):
                    ins = turn(ps[:, t // 4, P * (t % 4):P * (t % 4) + P], PT[:, t, 0:2 * C])
                ins.then_inc(lt_ps, 1)
                pe.wait_ge(lt_ev, i + 1)
                for t in range(T):
                    ins = mm(ps[0:P, 2 + t // 4, 128 * (t % 4):128 * (t % 4) + 128], tile(ring[:, 0, :], t), wlT[:, :],
                             start=True, stop=True)
                ins.then_inc(lo_ps, 1)


_INS = ['x', 'L0_tok_W_qry', 'L0_tok_W_key', 'L0_tok_v', 'L0_tok_b', 'L0_attn_Wq', 'L0_attn_bq', 'L0_attn_Wk',
        'L0_attn_bk', 'L0_attn_Wv', 'L0_attn_bv', 'L0_ffn_W_gat', 'L0_ffn_att_src', 'L0_ffn_att_dst', 'L0_ffn_b_gat',
        'L0_ffn_ln_gamma', 'L0_ffn_ln_beta', 'L0_ffn_W1', 'L0_ffn_b1', 'L0_ffn_W2', 'L0_ffn_b2', 'L0_ffn_edge_index',
        'L1_attn_q_weight', 'L1_ffn_weight', 'L1_ffn_bias']
_OUTS = [((4, 742, 64), 'float32')]


def kernel(**inputs):
    import numpy as _np
    import concourse.bacc as _bacc
    from concourse import mybir as _mybir
    from concourse.bass_utils import run_bass_kernel_spmd as _run

    nc = _bacc.Bacc("TRN2", target_bir_lowering=False, num_devices=1)
    arrays, args = {}, []
    for name in _INS:
        a = _np.ascontiguousarray(inputs[name])
        arrays[f"in_{name}_dram"] = a
        args.append(nc.dram_tensor(f"in_{name}_dram", a.shape, _mybir.dt.from_np(a.dtype), kind="ExternalInput").ap())
    for i, (shape, dtype) in enumerate(_OUTS):
        dt = _mybir.dt.from_np(_np.dtype(dtype))
        args.append(nc.dram_tensor(f"out_{i}_dram", shape, dt, kind="ExternalOutput").ap())
    audio_tower(nc, *args)
    r = _run(nc, [arrays], core_ids=[0])
    return r.results[0]["out_0_dram"]
```

```python
import concourse.bass as bass
from concourse import mybir
from contextlib import ExitStack


def audio_tower(
    nc: bass.Bass,
    x: bass.AP,
    tok_W_qry: bass.AP,
    tok_W_key: bass.AP,
    tok_v: bass.AP,
    tok_b: bass.AP,
    attn_Wq: bass.AP,
    attn_bq: bass.AP,
    attn_Wk: bass.AP,
    attn_bk: bass.AP,
    attn_Wv: bass.AP,
    attn_bv: bass.AP,
    W_gat: bass.AP,
    att_src: bass.AP,
    att_dst: bass.AP,
    b_gat: bass.AP,
    ln_gamma: bass.AP,
    ln_beta: bass.AP,
    W1: bass.AP,
    b1: bass.AP,
    W2: bass.AP,
    b2: bass.AP,
    edge_index: bass.AP,
    sig_W: bass.AP,
    lns_W: bass.AP,
    lns_bias: bass.AP,
    out: bass.AP,
):
    F32 = mybir.dt.float32
    I32 = mybir.dt.int32
    BF16 = mybir.dt.bfloat16
    ALU = mybir.AluOpType
    ACT = mybir.ActivationFunctionType
    AX = mybir.AxisListType

    B, L, C = x.shape
    WIN = 9
    NW = L - WIN + 1
    P, T = 106, 7
    assert P * T == NW
    G = B * T
    M = B * NW
    HALF = NW // 2
    XP = 125
    XT = L // XP
    PAIRS = B // 2
    H, E = att_src.shape
    HE = H * E
    FF = W1.shape[2]
    NE = edge_index.shape[1]
    EC = NE // 128
    EPAD = EC + 16
    KS = 4096
    assert M < KS
    RC = 8
    TW = H + HE
    DW = 2 * H
    BIG = 3.0e38
    FAR = 2.0 ** 115
    DA, DB = 53, 56
    assert DA * DB == M
    HC = 256
    assert EC == 2 * B * HC
    HB = 7
    SCALE = 1.0 / float(C) ** 0.5
    ROUND = 12582912.0

    src_table = nc.dram_tensor("src_table", (M + 1, TW), F32, kind="Internal").ap()
    spill = nc.dram_tensor("spill", (EPAD // RC, 128, RC * TW), F32, kind="Internal").ap()
    hist_dram = nc.dram_tensor("hist_dram", (M,), F32, kind="Internal").ap()
    dst_table = nc.dram_tensor("dst_table", (M, DW), F32, kind="Internal").ap()

    ctx = ExitStack()
    with ctx:
        def sb(name, shape, dt=F32):
            return ctx.enter_context(nc.sbuf_tensor(name, shape, dt))

        def sem(name):
            return ctx.enter_context(nc.semaphore(name))

        ident = sb("ident", [128, 128])
        tril = sb("tril", [128, 128])
        iota_lo = sb("iota_lo", [128, P])
        iota_hi = sb("iota_hi", [128, G])
        wk2 = sb("wk2", [128, 128])
        wq2 = sb("wq2", [128, 128])
        v2 = sb("v2", [128, 2])
        tb = sb("tb", [128, 1])
        wraw = sb("wraw", [C, 3, C])
        wT = sb("wT", [C, 3, C])
        bq = sb("bq", [C, 1])
        bk = sb("bk", [C, 1])
        bv_row = sb("bv_row", [P, C])
        wgat = sb("wgat", [C, HE])
        asrc_row = sb("asrc_row", [P, HE])
        adst_row = sb("adst_row", [P, HE])
        bgat_row = sb("bgat_row", [P, HE])
        gamma_row = sb("gamma_row", [P, HE])
        beta_row = sb("beta_row", [P, HE])
        w1 = sb("w1", [C, E, FF])
        b1c = sb("b1c", [FF, E])
        w2 = sb("w2", [FF, E, C])
        b2_row = sb("b2_row", [P, E * C])
        wsig = sb("wsig", [C, 2 * C])
        wl = sb("wl", [128, 2, C])
        wl2 = sb("wl2", [128, 128])
        wlT = sb("wlT", [128, 128])
        mw = sb("mw", [128, 1])
        mw_row = sb("mw_row", [P, C])
        lbias_row = sb("lbias_row", [P, C])
        tok = sb("tok", [128, DB * HC // 2])
        o0 = XT * B * C
        xt = tok[0:XP, 0:o0].rearrange("p (t k) -> p t k", t=XT)
        xT = tok[:, o0:o0 + PAIRS * L].rearrange("p (r n) -> p r n", r=PAIRS)
        o0 += PAIRS * L
        kT2 = tok[:, o0:o0 + L]
        qT2 = tok[:, o0 + L:o0 + L + NW]
        o0 += L + NW
        ring = tok[:, o0:o0 + 3 * NW].rearrange("p (a n) -> p a n", a=3)
        assert o0 + 3 * NW <= DB * HC // 2
        big = sb("big", [128, E * NW + G * E * C])
        wts = sb("wts", [P, G, WIN])
        wsm = sb("wsm", [P, G])
        h = sb("h", [P, G, C])
        yb = sb("yb", [P, T, C])
        cen = sb("cen", [P, T, C])
        sq = sb("sq", [P, T, C])
        st = sb("st", [P, 4, T])
        yT = sb("yT", [C, NW])
        qa = sb("qa", [C + 1, NW])
        ka = sb("ka", [C + 1, NW])
        va = sb("va", [P, T, C + 1])
        nm = sb("nm", [P, T])
        rd = sb("rd", [P, T])
        ebuf = sb("ebuf", [128, 2, EPAD], I32)
        fbuf = sb("fbuf", [128, 2, EPAD])
        key = sb("key", [128, EC])
        m8 = sb("m8", [128, RC])
        ki = sb("ki", [128, 2, RC], I32)
        kf = sb("kf", [128, 4, RC])
        cnt = sb("cnt", [128, 1])
        nf = sb("nf", [1, 2])
        ni = sb("ni", [1, 1], I32)
        hg = sb("hg", [P, G, HE])
        Ts = sb("Ts", [P, G, TW])
        Ds = sb("Ds", [P, G, DW])
        zrow = sb("zrow", [1, 560])
        Mx = sb("Mx", [P, H, G])
        tmp16 = sb("tmp16", [P, G, HE])
        small = sb("small", [P, 8, G])
        s4 = sb("s4", [P, 6, G, E])
        idx = sb("idx", [128, 2, 2, RC], I32)
        gs = sb("gs", [128, 2, RC, TW])
        gd = sb("gd", [128, 2, RC, DW])
        gs2 = sb("gs2", [128, 2, RC, TW])
        col = sb("col", [128, 2, 2, RC])
        dcol = sb("dcol", [128, 2, RC])
        ncol = sb("ncol", [128, 2, RC])
        apart = sb("apart", [128, 2, 128])
        digit = sb("digit", [128, 2, EC], BF16)
        room = sb("room", [128, DA * HC], BF16)
        oha = room[:, 0:DA * HC].rearrange("p (v c) -> p v c", v=DA)
        ohb = tok[:, :].bitcast(BF16).rearrange("p (v c) -> p v c", v=DB)
        roomf = room[:, :].bitcast(F32)
        o0 = 2 * RC * G
        ohhi = roomf[:, 0:o0].rearrange("p (k j g) -> p k j g", k=2, j=RC)
        ohlo = roomf[:, o0:o0 + 2 * RC * P].rearrange("p (k j g) -> p k j g", k=2, j=RC)
        o0 += 2 * RC * P
        scr = roomf[:, o0:o0 + (H + 1) * 128].rearrange("p (q n) -> p q n", q=H + 1)
        o0 += (H + 1) * 128
        vr = roomf[:, o0:o0 + 2 * TW * G].rearrange("p (k q g) -> p k q g", k=2, q=TW)
        mark = sb("mark", [1, 1])
        hist_sb = sb("hist_sb", [DA, DB])
        ccnt = sb("ccnt", [P, G])
        crow = sb("crow", [P, TW])
        cw = sb("cw", [P, G, H])
        c16 = sb("c16", [P, G, HE])
        lead = sb("lead", [128, 2])
        cm = sb("cm", [128, H + 1])
        cand = sb("cand", [P, H, G])
        nb = sb("nb", [P, 2, G])
        ew = sb("ew", [128, RC, H])
        fe = sb("fe", [128, 2, RC, TW])
        xw = big[0:P, 0:2 * T * WIN * C].rearrange("p (a t s c) -> p a t s c", a=2, s=WIN, c=C)
        PT = big[0:P, 0:T * NW].rearrange("p (t n) -> p t n", t=T)
        HH = big[:, 0:E * NW].rearrange("p (e n) -> p e n", e=E)
        Oe = big[0:P, E * NW:E * NW + G * E * C].rearrange("p (g e c) -> p g e c", e=E, c=C)
        esT = HH[:, 3, :]
        ES = big[0:P, 0:T * 2 * C].rearrange("p (t c) -> p t c", t=T)
        l_src, l_dst = ebuf[:, 0, :], ebuf[:, 1, :]
        l_lo, l_hi = fbuf[:, 0, :], fbuf[:, 1, :]

        ps = ctx.enter_context(nc.psum_tensor("ps", [128, 8, 512], F32))

        def tile(ap, t):
            return ap[:, t * P:(t + 1) * P]

        c_ready = sem("c_ready")
        w_in = sem("w_in")
        z_ready = sem("z_ready")
        x_in = sem("x_in")
        e_in = sem("e_in")
        xw_in = [sem("xw_in0"), sem("xw_in1")]
        xw_used = sem("xw_used")
        wT_ps = sem("wT_ps")
        w_prep = sem("w_prep")
        wl_act = sem("wl_act")
        wl_dve = sem("wl_dve")
        cnt_ready = sem("cnt_ready")
        cnt_row = sem("cnt_row")
        rounds_ready = sem("rounds_ready")
        x_tr = sem("x_tr")
        x_ev = sem("x_ev")
        kq_ps = sem("kq_ps")
        k_ev = sem("k_ev")
        q_ev = sem("q_ev")
        add_done = sem("add_done")
        tanh_done = sem("tanh_done")
        sc_ps = sem("sc_ps")
        sc_shift = sem("sc_shift")
        sc_exp = sem("sc_exp")
        tok_done = sem("tok_done")
        var_ready = [sem(f"var_ready{n}") for n in range(4)]
        std_ready = [sem(f"std_ready{n}") for n in range(4)]
        y_ready = [sem(f"y_ready{n}") for n in range(4)]
        yT_ps = [sem(f"yT_ps{n}") for n in range(4)]
        yT_ev = [sem(f"yT_ev{n}") for n in range(4)]
        qkv_ps = sem("qkv_ps")
        qkv_ev = sem("qkv_ev")
        s_ps = sem("s_ps")
        s_max = sem("s_max")
        m_ps = sem("m_ps")
        m_ev = sem("m_ev")
        st_ps = sem("st_ps")
        p_ready = sem("p_ready")
        o_ps = sem("o_ps")
        o_ev = sem("o_ev")
        gat_ps = sem("gat_ps")
        gat_ev = sem("gat_ev")
        hid_ps = sem("hid_ps")
        hid_ev = sem("hid_ev")
        ex_ps = sem("ex_ps")
        ex_ev = sem("ex_ev")
        T_ready = sem("T_ready")
        T_out = sem("T_out")
        D_ready = sem("D_ready")
        D_out = sem("D_out")
        digits_ready = sem("digits_ready")
        oh_ready = sem("oh_ready")
        oh_free = sem("oh_free")
        hist_ps = sem("hist_ps")
        hist_ev = sem("hist_ev")
        hist_out = sem("hist_out")
        hist_in = sem("hist_in")
        crow_in = sem("crow_in")
        col1_ready = sem("col1_ready")
        oh1_ready = sem("oh1_ready")
        far_ready = sem("far_ready")
        nb_ready = sem("nb_ready")
        v_used = sem("v_used")
        spilled = [sem("spilled0"), sem("spilled1")]
        spill_in = [sem("spill_in0"), sem("spill_in1")]
        spill_used = sem("spill_used")
        oh2_ready = sem("oh2_ready")
        drow_ps = sem("drow_ps")
        g1_in = [sem("g1_in0"), sem("g1_in1")]
        row_ps = sem("row_ps")
        row_free = sem("row_free")
        v_ready = sem("v_ready")
        v_ps = sem("v_ps")
        g2_in = [sem("g2_in0"), sem("g2_in1")]
        e_arg = sem("e_arg")
        e_exp = sem("e_exp")
        f_ready = sem("f_ready")
        f_ps = sem("f_ps")
        acc_done = sem("acc_done")
        self_arg = sem("self_arg")
        self_exp = sem("self_exp")
        gv_ready = sem("gv_ready")
        gs_ready = sem("gs_ready")
        top_arg = sem("top_arg")
        top_exp = sem("top_exp")
        sq_ps = sem("sq_ps")
        sq_ev = sem("sq_ev")
        sg_ps = sem("sg_ps")
        sg_ev = sem("sg_ev")
        so_ps = sem("so_ps")
        so_ev = sem("so_ev")
        la_ready = sem("la_ready")
        la_ln = sem("la_ln")
        la_sub = sem("la_sub")
        la_exp = sem("la_exp")
        lt_ps = sem("lt_ps")
        lt_ev = sem("lt_ev")
        lo_ps = sem("lo_ps")
        lo_ln = sem("lo_ln")
        lo_arg = sem("lo_arg")
        lo_exp = sem("lo_exp")
        lo_ev = sem("lo_ev")
        h_ready = sem("h_ready")
        out_done = sem("out_done")

        N_W = 32
        block = ctx.enter_context(nc.Block())

        def row(ap, n, parts=P):
            return bass.AP(ap.tensor, 0, [[0, parts], [1, n]])

        @block.sync
        def _(sp):
            xv = x.rearrange("b (t p) c -> p t b c", p=XP)
            for t in range(XT):
                sp.dma_start(xt[:, t, :].rearrange("p (b c) -> p b c", b=B), xv[:, t]).then_inc(x_in, 16)
            ev = edge_index.rearrange("r (p c) -> p r c", p=128)
            sp.dma_start(ebuf[:, :, 0:EC], ev).then_inc(e_in, 16)
            n = 0

            def load(dst, src):
                nonlocal n
                sp.dma_start(dst, src).then_inc(w_in, 16)
                n += 1

            sp.wait_ge(z_ready, 4)
            for k in range(2):
                load(wk2[64 * k:64 * k + 64, 64 * k:64 * k + 64], tok_W_key)
                load(wq2[64 * k:64 * k + 64, 64 * k:64 * k + 64], tok_W_qry)
                load(v2[64 * k:64 * k + 64, k:k + 1], tok_v.rearrange("(p a) -> p a", a=1))
                load(tb[64 * k:64 * k + 64, :], tok_b.rearrange("(p a) -> p a", a=1))
                load(wl[64 * k:64 * k + 64, 0, :], lns_W)
            for k, w in enumerate((attn_Wq, attn_Wk, attn_Wv)):
                load(wraw[:, k, :], w)
            load(bq[:, :], attn_bq.rearrange("(p a) -> p a", a=1))
            load(bk[:, :], attn_bk.rearrange("(p a) -> p a", a=1))
            load(bv_row[:, :], row(attn_bv, C))
            load(wgat[:, :], W_gat)
            load(asrc_row[:, :], row(att_src, HE))
            load(adst_row[:, :], row(att_dst, HE))
            load(bgat_row[:, :], row(b_gat, HE))
            load(gamma_row[:, :], row(ln_gamma, HE))
            load(beta_row[:, :], row(ln_beta, HE))
            load(w1[:, :, :], W1.rearrange("e c f -> c e f"))
            for e in range(E):
                load(b1c[:, e:e + 1], b1[e, :].rearrange("(f a) -> f a", a=1))
            load(w2[:, :, :], W2.rearrange("e f c -> f e c"))
            load(b2_row[:, :], row(b2, E * C))
            load(wsig[:, 0:C], sig_W)
            load(wsig[:, C:2 * C], sig_W)
            load(lbias_row[:, :], row(lns_bias, C))
            assert n == N_W
            for b in range(B):
                if b >= 2:
                    sp.wait_ge(xw_used, b - 1)
                sp.dma_start(xw[:, b % 2].rearrange("p t s c -> p t (s c)"),
                             bass.AP(x.tensor, b * L * C, [[C, P], [P * C, T], [1, WIN * C]])).then_inc(xw_in[b % 2], 16)
            sp.wait_ge(hist_ev, 1)
            sp.dma_start(hist_dram.rearrange("(a b) -> a b", a=DA), hist_sb[:, :]).then_inc(hist_out, 16)
            sp.wait_ge(hist_out, 16)
            sp.dma_start(ccnt[:, :], bass.AP(hist_dram.tensor, 0, [[1, P], [P, G]]),
                         allow_slow_non_contiguous=True).then_inc(hist_in, 16)
            sp.dma_start(spill[0, 0:1, 0:16], zrow[0:1, 0:16]).then_inc(spilled[0], 16)
            sp.dma_start(spill[1, 0:1, 0:16], zrow[0:1, 0:16]).then_inc(spilled[1], 16)
            sp.wait_ge(spilled[0], 16)
            sp.wait_ge(spilled[1], 16)
            sp.wait_ge(T_ready, 2)
            sp.dma_start(src_table[0:1, :], zrow[0:1, 0:TW]).then_inc(T_out, 16)
            sp.dma_start(src_table[1:M + 1, :].rearrange("(g p) q -> p g q", p=P), Ts[:, :, :]).then_inc(T_out, 16)
            sp.wait_ge(T_out, 32)
            sp.dma_start(crow[:, :], bass.AP(src_table.tensor, M * TW, [[0, P], [1, TW]])).then_inc(crow_in, 16)
            sp.wait_ge(rounds_ready, 1)
            n_pairs = sp.value_load(ni[0:1, 0:1], min_val=1, max_val=EPAD // 16)
            with sp.Fori(0, n_pairs) as i:
                for k in range(2):
                    sp.wait_ge(g1_in[k], 128 * i + 128)
                    sp.dma_start(spill[bass.ds(2 * i + k, 1), :, :].rearrange("a p q -> (a p) q"),
                                 gs[:, k, :, :].rearrange("p j q -> p (j q)")).then_inc(spilled[k], 16)
            sp.wait_ge(D_ready, 1)
            sp.wait_ge(spilled[0], 16 * n_pairs + 16)
            sp.wait_ge(spilled[1], 16 * n_pairs + 16)
            sp.dma_start(dst_table.rearrange("(g p) q -> p g q", p=P), Ds[:, :, :]).then_inc(D_out, 16)
            with sp.Fori(0, n_pairs) as i:
                for k in range(2):
                    sp.wait_ge(spill_used, 2 * i + (k + 1))
                    sp.dma_start(gs2[:, k, :, :].rearrange("p j q -> p (j q)"),
                                 spill[bass.ds(2 * i + k, 1), :, :].rearrange("a p q -> (a p) q")).then_inc(spill_in[k], 16)
            sp.wait_ge(h_ready, B)
            sp.dma_start(out.rearrange("b (t p) c -> p (b t) c", p=P), h[:, :, :]).then_inc(out_done, 16)
            sp.wait_ge(out_done, 16)

        @block.gpsimd
        def _(pool):
            nc.gpsimd.memset(wk2[:, :], 0.0).then_inc(z_ready, 1)
            nc.gpsimd.memset(wq2[:, :], 0.0).then_inc(z_ready, 1)
            nc.gpsimd.memset(v2[:, :], 0.0).then_inc(z_ready, 1)
            nc.gpsimd.memset(wl2[:, :], 0.0).then_inc(z_ready, 1)
            nc.gpsimd.memset(ident[:, :], 0.0)
            nc.gpsimd.memset(tril[:, :], 1.0)
            nc.gpsimd.memset(zrow[:, :], 0.0).then_inc(T_ready, 1)
            pool.drain()
            nc.gpsimd.affine_select(out=ident[:, :], in_=ident[:, :], compare_op=ALU.not_equal, fill=1.0,
                                    base=0, pattern=[[-1, 128]], channel_multiplier=1).then_inc(c_ready, 1)
            nc.gpsimd.affine_select(out=tril[:, :], in_=tril[:, :], compare_op=ALU.is_gt, fill=0.0,
                                    base=0, pattern=[[-1, 128]], channel_multiplier=1).then_inc(c_ready, 1)
            nc.gpsimd.iota(iota_lo[:, :], pattern=[[1, P]], base=0, channel_multiplier=0,
                           allow_small_or_imprecise_dtypes=True).then_inc(c_ready, 1)
            nc.gpsimd.iota(iota_hi[:, :], pattern=[[1, G]], base=0, channel_multiplier=0,
                           allow_small_or_imprecise_dtypes=True).then_inc(c_ready, 1)
            pool.wait_ge(rounds_ready, 1)
            n_pairs = pool.value_load(ni[0:1, 0:1], min_val=1, max_val=EPAD // 16)
            pool.wait_ge(T_out, 32)
            with pool.Fori(0, n_pairs) as i:
                for k in range(2):
                    at = bass.ds(16 * i + RC * k, RC)
                    pool.wait_ge(v_ps, 16 * i + max(RC * k, 1))
                    pool.wait_ge(spilled[k], 16 * i + 16)
                    nc.gpsimd.tensor_copy(idx[:, k, 0, :], l_src[:, at])
                    nc.gpsimd.tensor_copy(col[:, k, 0, :], l_lo[:, at])
                    nc.gpsimd.tensor_copy(col[:, k, 1, :], l_hi[:, at])
                    nc.gpsimd.tensor_copy(dcol[:, k, :], l_dst[:, at])
                    pool.drain()
                    nc.gpsimd.tensor_scalar(ncol[:, k, :], dcol[:, k, :], -FAR, None, ALU.mult).then_inc(col1_ready, 1)
                    for j in range(RC):
                        nc.gpsimd.indirect_dma_start(
                            gs[:, k, j, :], None, src_table,
                            bass.IndirectOffsetOnAxis(idx[:, k, 0, j:j + 1], 0)).then_inc(g1_in[k], 16)
                    for j in range(RC):
                        ins = nc.gpsimd.tensor_scalar(ohlo[:, k, j, :], iota_lo[:, :], col[:, k, 0, j:j + 1], None, ALU.is_equal)
                    ins.then_inc(oh1_ready, 1)
            pool.wait_ge(D_out, 16)
            with pool.Fori(0, n_pairs) as i:
                for k in range(2):
                    at = bass.ds(16 * i + RC * k, RC)
                    pool.wait_ge(f_ps, 16 * i + (RC * k + 2))
                    nc.gpsimd.tensor_copy(idx[:, k, 1, :], l_dst[:, at])
                    nc.gpsimd.tensor_copy(col[:, k, 0, :], l_lo[:, at])
                    nc.gpsimd.tensor_copy(col[:, k, 1, :], l_hi[:, at])
                    pool.drain()
                    for j in range(RC):
                        nc.gpsimd.indirect_dma_start(
                            gd[:, k, j, :], None, dst_table,
                            bass.IndirectOffsetOnAxis(idx[:, k, 1, j:j + 1], 0)).then_inc(g2_in[k], 16)
                    for j in range(RC):
                        nc.gpsimd.tensor_scalar(ohhi[:, k, j, :], iota_hi[:, :], col[:, k, 1, j:j + 1], None, ALU.is_equal)
                        ins = nc.gpsimd.tensor_scalar(ohlo[:, k, j, :], iota_lo[:, :], col[:, k, 0, j:j + 1], None, ALU.is_equal)
                    ins.then_inc(oh2_ready, 1)

        @block.scalar
        def _(act):
            for pr in range(PAIRS):
                act.wait_ge(x_tr, pr + 1)
                for k in range(2):
                    nc.scalar.copy(xT[:, pr, 375 * k:375 * k + 375], ps[:, 2 * pr + k, 0:375]).then_inc(x_ev, 1)
            act.wait_ge(wl_dve, 1)
            nc.scalar.activation(wl[:, 1, :], wl[:, 1, :], ACT.Ln).then_inc(wl_act, 1)
            act.wait_ge(wl_dve, 2)
            nc.scalar.activation(wl2[0:64, 0:64], wl[0:64, 1, :], ACT.Exp).then_inc(wl_act, 1)
            nc.scalar.activation(wl2[64:128, 64:128], wl[64:128, 0, :], ACT.Sign).then_inc(wl_act, 1)
            for pr in range(PAIRS):
                act.wait_ge(kq_ps, pr + 1)
                if pr:
                    act.wait_ge(add_done, WIN)
                for k in range(2):
                    nc.scalar.copy(kT2[:, 375 * k:375 * k + 375], ps[:, 4 + k, 0:375]).then_inc(k_ev, 1)
                for s in range(WIN):
                    n = WIN * pr + s
                    act.wait_ge(add_done, n + 1)
                    nc.scalar.activation(ring[:, n % 3, :], ring[:, n % 3, :], ACT.Tanh).then_inc(tanh_done, 1)
            act.wait_ge(sc_shift, 1)
            nc.scalar.activation(wts[:, :, :], wts[:, :, :], ACT.Exp).then_inc(sc_exp, 1)

            def std(i, n):
                act.wait_ge(var_ready[n], i + 1)
                nc.scalar.activation(st[:, 3, :], st[:, 2, :], ACT.Sqrt).then_inc(std_ready[n], 1)

            def transposed(i, n):
                act.wait_ge(yT_ps[n], i + 1)
                nc.scalar.copy(yT[:, 0:4 * P], ps[0:C, 0, 0:4 * P])
                nc.scalar.copy(yT[:, 4 * P:NW], ps[0:C, 1, 0:3 * P]).then_inc(yT_ev[n], 1)

            with act.Fori(0, B) as i:
                std(i, 0)
                transposed(i, 0)
                act.wait_ge(m_ps, i + 1)
                nc.scalar.copy(qa[C:C + 1, 0:4 * P], ps[C:C + 1, 6, 0:4 * P])
                nc.scalar.copy(qa[C:C + 1, 4 * P:NW], ps[C:C + 1, 7, 0:3 * P]).then_inc(m_ev, 1)
                for t in range(T):
                    act.wait_ge(st_ps, T * i + (t + 1))
                    b0 = 2 * (t % 3)
                    nc.scalar.activation(PT[:, t, :].rearrange("p (a n) -> p a n", a=2),
                                         ps[0:P, b0:b0 + 2, 0:HALF], ACT.Exp, scale=SCALE).then_inc(p_ready, 1)
            with act.Fori(0, B) as i:
                std(i, 1)
                transposed(i, 1)
                for k in range(2 * E):
                    act.wait_ge(hid_ps, 2 * E * i + (k + 1))
                    nc.scalar.activation(HH[:, k // 2, HALF * (k % 2):HALF * (k % 2) + HALF],
                                         ps[:, 4 + k % 4, 0:HALF], ACT.Gelu, bias=b1c[:, k // 2:k // 2 + 1])\
                        .then_inc(hid_ev, 1)
            act.wait_ge(rounds_ready, 1)
            n_pairs = act.value_load(ni[0:1, 0:1], min_val=1, max_val=EPAD // 16)
            nc.scalar.copy(apart[:, 0, :], ident[:, :]).then_inc(far_ready, RC)
            act.drain()
            with act.Fori(0, n_pairs) as i:
                for k in range(2):
                    act.wait_ge(col1_ready, 2 * i + (k + 1))
                    for j in range(RC + 1):
                        n = RC * k + j
                        if j < RC:
                            act.wait_ge(drow_ps, 4 * i + (2 * k + j // 4 + 1))
                            act.wait_ge(row_free, 16 * i + (n + 1))
                            nc.scalar.activation(apart[:, j % 2, :], ps[:, j // 4, 128 * (j % 4):128 * (j % 4) + 128], ACT.Abs,
                                                 bias=ncol[:, k, j:j + 1], scale=FAR).then_inc(far_ready, 1)
                        if j >= 1:
                            act.wait_ge(v_ps, 16 * i + (n + RC))
                            nc.scalar.activation(nb[:, (j - 1) % 2, :], ps[0:P, 5 + (j - 1) % 2, H * G:(H + 1) * G], ACT.Copy,
                                                 bias=-BIG, scale=BIG).then_inc(nb_ready, 1)
            with act.Fori(0, n_pairs) as i:
                for k in range(2):
                    act.wait_ge(e_arg, 2 * i + (k + 1))
                    nc.scalar.activation(ew[:, :, :], ew[:, :, :], ACT.Exp).then_inc(e_exp, 1)
            act.wait_ge(self_arg, 1)
            nc.scalar.activation(s4[:, 0], s4[:, 0], ACT.Exp)
            nc.scalar.activation(cw[:, :, :], cw[:, :, :], ACT.Exp).then_inc(self_exp, 1)
            act.wait_ge(gv_ready, 1)
            nc.scalar.activation(small[:, 2, :], small[:, 1, :], ACT.Sqrt).then_inc(gs_ready, 1)
            act.wait_ge(top_arg, 1)
            nc.scalar.activation(s4[:, 2], s4[:, 2], ACT.Exp).then_inc(top_exp, 1)
            with act.Fori(0, B) as i:
                std(i, 2)
                transposed(i, 2)
                act.wait_ge(sq_ps, i + 1)
                nc.scalar.copy(qa[0:C, :].rearrange("p (a n) -> p a n", a=2), ps[0:C, 2:4, 0:HALF]).then_inc(sq_ev, 1)
                for t in range(T):
                    act.wait_ge(sg_ps, T * i + (t + 1))
                    b0 = 4 + 2 * (t % 2)
                    nc.scalar.activation(PT[:, t, :].rearrange("p (a n) -> p a n", a=2),
                                         ps[0:P, b0:b0 + 2, 0:HALF], ACT.Sigmoid).then_inc(sg_ev, 1)
            with act.Fori(0, B) as i:
                std(i, 3)
                act.wait_ge(la_ready, i + 1)
                nc.scalar.activation(sq[:, :, :], sq[:, :, :], ACT.Ln).then_inc(la_ln, 1)
                act.wait_ge(la_sub, i + 1)
                nc.scalar.activation(ES[:, :, 0:C], sq[:, :, :], ACT.Exp)
                nc.scalar.activation(ES[:, :, C:2 * C], yb[:, :, :], ACT.Sign).then_inc(la_exp, 1)
                act.wait_ge(lt_ps, i + 1)
                nc.scalar.copy(esT[:, 0:4 * P], ps[:, 0, 0:4 * P])
                nc.scalar.copy(esT[:, 4 * P:NW], ps[:, 1, 0:3 * P]).then_inc(lt_ev, 1)
                act.wait_ge(lo_ps, i + 1)
                for b0, t0, t1 in ((2, 0, 4), (3, 4, 7)):
                    v = ps[0:P, b0, 0:128 * (t1 - t0)].rearrange("p (t c) -> p t c", c=128)
                    nc.scalar.activation(cen[:, t0:t1, :], v[:, :, 0:C], ACT.Ln)
                    ins = nc.scalar.activation(sq[:, t0:t1, :], v[:, :, C:2 * C], ACT.Sign)
                ins.then_inc(lo_ln, 1)
                act.wait_ge(lo_arg, i + 1)
                nc.scalar.activation(cen[:, :, :], cen[:, :, :], ACT.Exp).then_inc(lo_exp, 1)

        @block.vector
        def _(dve):
            V = nc.vector
            dve.wait_ge(e_in, 16)
            V.tensor_copy(l_lo[:, 0:EC], ebuf[:, 0, 0:EC])
            V.tensor_copy(l_hi[:, 0:EC], ebuf[:, 1, 0:EC])
            dve.drain()
            V.scalar_tensor_tensor(key[:, :], l_hi[:, 0:EC], float(KS), l_lo[:, 0:EC], ALU.mult, ALU.add)
            dve.drain()
            V.tensor_scalar(key[:, :], key[:, :], 1.0, None, ALU.add)
            dve.drain()
            V.scalar_tensor_tensor(key[:, :], l_hi[:, 0:EC], float(M), key[:, :], ALU.is_lt, ALU.mult)
            dve.drain()
            V.scalar_tensor_tensor(key[:, :], l_lo[:, 0:EC], float(M - 1), key[:, :], ALU.is_lt, ALU.mult)
            V.tensor_scalar(l_lo[:, 0:EC], l_lo[:, 0:EC], float(M - 1), 2.0 * M, ALU.is_lt, ALU.mult)
            dve.drain()
            V.tensor_tensor(l_hi[:, 0:EC], l_hi[:, 0:EC], l_lo[:, 0:EC], ALU.add)
            dve.drain()
            V.tensor_scalar(l_lo[:, 0:EC], l_hi[:, 0:EC], 0.5, 1.0 / DB, ALU.add, ALU.mult)
            dve.drain()
            V.tensor_scalar(l_lo[:, 0:EC], l_lo[:, 0:EC], -0.5, ROUND, ALU.add, ALU.add)
            dve.drain()
            V.tensor_scalar(l_lo[:, 0:EC], l_lo[:, 0:EC], -ROUND, None, ALU.add)
            dve.drain()
            V.tensor_copy(digit[:, 0, :], l_lo[:, 0:EC])
            V.scalar_tensor_tensor(digit[:, 1, :], l_lo[:, 0:EC], float(-DB), l_hi[:, 0:EC], ALU.mult, ALU.add)\
                .then_inc(digits_ready, 1)
            dve.drain()
            V.tensor_scalar(l_lo[:, 0:EC], key[:, :], 0.0, 0.0, ALU.is_gt, ALU.add,
                            accum_out=cnt[:, :]).then_inc(cnt_ready, 1)
            dve.wait_ge(cnt_row, 1)
            V.tensor_reduce(nf[:, 0:1], ps[0:1, 7, 0:128], AX.X, ALU.max)
            dve.drain()
            V.tensor_scalar(nf[:, 1:2], nf[:, 0:1], 1.0 / 16, 15.0 / 16 - 0.5 + 1.0 / 64, ALU.mult, ALU.add)
            dve.drain()
            V.tensor_scalar(nf[:, 0:1], nf[:, 1:2], ROUND, -ROUND, ALU.add, ALU.add)
            dve.drain()
            V.tensor_scalar(ni[:, :], nf[:, 0:1], 1.0, None, ALU.max).then_inc(rounds_ready, 1)
            dve.wait_ge(rounds_ready, 1)
            dve.wait_ge(c_ready, 4)
            dve.wait_ge(w_in, 16 * N_W)
            V.scalar_tensor_tensor(wl[:, 1, :], wl[:, 0, :], -1.0, wl[:, 0, :], ALU.mult, ALU.max)
            dve.drain()
            V.tensor_scalar(wl[:, 1, :], wl[:, 1, :], 1e-8, None, ALU.add).then_inc(wl_dve, 1)
            dve.wait_ge(wl_act, 1)
            V.tensor_reduce(mw[:, :], wl[:, 1, :], AX.X, ALU.max)
            dve.drain()
            V.tensor_scalar(wl[:, 1, :], wl[:, 1, :], mw[:, 0:1], None, ALU.subtract).then_inc(wl_dve, 1)
            n_pairs = dve.value_load(ni[0:1, 0:1], min_val=1, max_val=EPAD // 16)
            with dve.Fori(0, n_pairs) as i:
                for k in range(2):
                    at = bass.ds(16 * i + RC * k, RC)
                    V.max(m8[:, :], key[:, :])
                    dve.drain()
                    V.match_replace(key[:, :], m8[:, :], key[:, :], 0.0)
                    V.tensor_copy(ki[:, 0, :], m8[:, :])
                    dve.drain()
                    V.tensor_scalar(l_src[:, at], ki[:, 0, :], KS - 1, None, ALU.bitwise_and)
                    V.tensor_scalar(l_dst[:, at], ki[:, 0, :], 12, None, ALU.logical_shift_right)
                    V.tensor_scalar(ki[:, 1, :], ki[:, 0, :], 12, None, ALU.logical_shift_right)
                    dve.drain()
                    V.tensor_copy(kf[:, 0, :], ki[:, 1, :])
                    V.tensor_scalar(kf[:, 3, :], m8[:, :], 1.0, 1000.0, ALU.is_lt, ALU.mult)
                    dve.drain()
                    V.tensor_scalar(kf[:, 1, :], kf[:, 0, :], 0.5, 1.0 / P, ALU.add, ALU.mult)
                    dve.drain()
                    V.tensor_scalar(kf[:, 1, :], kf[:, 1, :], -0.5, ROUND, ALU.add, ALU.add)
                    dve.drain()
                    V.tensor_scalar(kf[:, 2, :], kf[:, 1, :], -ROUND, None, ALU.add)
                    dve.drain()
                    V.tensor_copy(l_hi[:, at], kf[:, 2, :])
                    V.scalar_tensor_tensor(kf[:, 1, :], kf[:, 2, :], float(-P), kf[:, 0, :], ALU.mult, ALU.add)
                    dve.drain()
                    V.tensor_tensor(l_lo[:, at], kf[:, 1, :], kf[:, 3, :], ALU.add)
                dve.drain()
            for pr in range(PAIRS):
                dve.wait_ge(kq_ps, pr + 1)
                V.tensor_scalar(qT2[:, 0:HALF], ps[:, 6, 0:HALF], tb[:, 0:1], None, ALU.add)
                V.tensor_scalar(qT2[:, HALF:NW], ps[:, 7, 0:HALF], tb[:, 0:1], None, ALU.add).then_inc(q_ev, 1)
                dve.drain()
                dve.wait_ge(k_ev, 2 * pr + 2)
                for s in range(WIN):
                    n = WIN * pr + s
                    if n >= 3:
                        dve.wait_ge(sc_ps, n - 2)
                    V.tensor_tensor(ring[:, n % 3, :], kT2[:, s:s + NW], qT2[:, :], ALU.add).then_inc(add_done, 1)
            dve.wait_ge(wT_ps, 1)
            V.tensor_copy(wT[:, :, :], ps[0:C, 1, 0:3 * C].rearrange("p (k c) -> p k c", k=3))
            V.tensor_copy(wlT[:, :], ps[:, 1, 3 * C:3 * C + 128])
            V.tensor_copy(mw_row[:, :], ps[0:P, 1, 320:320 + C])
            V.memset(ka[C:C + 1, :], 1.0)
            V.memset(va[:, :, C:C + 1], 1.0).then_inc(w_prep, 1)
            dve.wait_ge(sc_ps, 2 * WIN)
            for pr in range(PAIRS):
                for bb in range(2):
                    b = 2 * pr + bb
                    V.tensor_copy(wts[:, T * b:T * b + T, :],
                                  ps[0:P, 2 * pr, 0:2 * T * WIN].rearrange("p (b t s) -> p b t s", b=2, s=WIN)[:, bb])
            dve.drain()
            V.tensor_reduce(wsm[:, :], wts[:, :, :], AX.X, ALU.max)
            dve.drain()
            V.tensor_tensor(wts[:, :, :], wts[:, :, :], wsm[:, :].to_broadcast([P, G, WIN]), ALU.subtract).then_inc(sc_shift, 1)
            dve.wait_ge(sc_exp, 1)
            V.tensor_reduce(wsm[:, :], wts[:, :, :], AX.X, ALU.add)
            dve.drain()
            V.reciprocal(wsm[:, :], wsm[:, :])
            dve.drain()
            V.tensor_tensor(wts[:, :, :], wts[:, :, :], wsm[:, :].to_broadcast([P, G, WIN]), ALU.mult)
            dve.drain()
            for b in range(B):
                w, hb = xw[:, b % 2], slice(T * b, T * b + T)
                dve.wait_ge(xw_in[b % 2], 16 * (b // 2 + 1))
                V.tensor_tensor(w, w, wts[:, hb, :].to_broadcast([P, T, WIN, C]), ALU.mult)
                dve.drain()
                V.tensor_reduce(h[:, hb, :], w.rearrange("p t s c -> p t c s"), AX.X, ALU.add).then_inc(xw_used, 1)
            dve.drain()

            def normed(i, n):
                hb = h[:, bass.ds(i * T, T), :]
                V.tensor_reduce(st[:, 0, :], hb, AX.X, ALU.add)
                dve.drain()
                V.tensor_scalar(st[:, 1, :], st[:, 0, :], 1.0 / C, None, ALU.mult)
                dve.drain()
                V.tensor_tensor(cen[:, :, :], hb, st[:, 1, :].to_broadcast([P, T, C]), ALU.subtract)
                dve.drain()
                V.tensor_tensor(sq[:, :, :], cen[:, :, :], cen[:, :, :], ALU.mult)
                dve.drain()
                V.tensor_reduce(st[:, 0, :], sq[:, :, :], AX.X, ALU.add)
                dve.drain()
                V.tensor_scalar(st[:, 2, :], st[:, 0, :], 1.0 / C, 1e-5, ALU.mult, ALU.add).then_inc(var_ready[n], 1)
                dve.wait_ge(std_ready[n], i + 1)
                V.reciprocal(st[:, 0, :], st[:, 3, :])
                dve.drain()
                V.tensor_tensor(yb[:, :, :], cen[:, :, :], st[:, 0, :].to_broadcast([P, T, C]), ALU.mult)\
                    .then_inc(y_ready[n], 1)
                dve.drain()

            def digits(c):
                at = bass.ds(HC * c, HC)
                for v in range(DA):
                    V.tensor_scalar(oha[:, v, :], digit[:, 0, at], float(v), None, ALU.is_equal)
                for v in range(DB):
                    ins = V.tensor_scalar(ohb[:, v, :], digit[:, 1, at], float(v), None, ALU.is_equal)
                ins.then_inc(oh_ready, 1)

            with dve.Fori(0, B) as i:
                normed(i, 0)
                dve.wait_ge(qkv_ps, i + 1)
                V.tensor_scalar(qa[0:C, :].rearrange("p (a n) -> p a n", a=2), ps[0:C, 2:4, 0:HALF], bq[:, 0:1], None, ALU.add)
                V.tensor_scalar(ka[0:C, :].rearrange("p (a n) -> p a n", a=2), ps[0:C, 4:6, 0:HALF], bk[:, 0:1], None, ALU.add)
                V.tensor_tensor(va[:, :, 0:C], ps[0:P, 6, 0:T * C].rearrange("p (t c) -> p t c", t=T),
                                bv_row[:, :].unsqueeze(1).to_broadcast([P, T, C]), ALU.add).then_inc(qkv_ev, 1)
                for t in range(T):
                    dve.wait_ge(s_ps, T * i + (t + 1))
                    b0 = 2 * (t % 2)
                    V.tensor_reduce(nm[:, t:t + 1], ps[0:P, b0:b0 + 2, 0:HALF], AX.XY, ALU.max, negate=True).then_inc(s_max, 1)
                dve.wait_ge(oh_free, 2 * i + 1)
                digits(2 * i)
                dve.wait_ge(oh_free, 2 * i + 2)
                digits(2 * i + 1)
                dve.wait_ge(o_ps, i + 1)
                O = ps[0:P, 6, 0:T * (C + 1)].rearrange("p (t c) -> p t c", t=T)
                V.reciprocal(rd[:, :], O[:, :, C])
                dve.drain()
                V.tensor_tensor(cen[:, :, :], O[:, :, 0:C], rd[:, :].to_broadcast([P, T, C]), ALU.mult).then_inc(o_ev, 1)
                dve.drain()
                hb = h[:, bass.ds(i * T, T), :]
                V.tensor_tensor(hb, hb, cen[:, :, :], ALU.add)
                dve.drain()
            dve.wait_ge(hist_ps, 1)
            V.tensor_copy(hist_sb[:, :], ps[0:DA, HB, 0:DB]).then_inc(hist_ev, 1)
            with dve.Fori(0, B) as i:
                normed(i, 1)
                dve.wait_ge(gat_ps, i + 1)
                V.tensor_copy(hg[:, bass.ds(i * T, T), :], ps[0:P, 2, 0:T * HE].rearrange("p (t q) -> p t q", t=T)).then_inc(gat_ev, 1)
                for t in range(T):
                    dve.wait_ge(ex_ps, T * i + (t + 1))
                    V.tensor_tensor(Oe[:, bass.ds(i * T + t, 1), :, :].rearrange("p g e c -> p (g e c)"),
                                    ps[0:P, 2 + t % 2, 0:E * C], b2_row[:, :], ALU.add).then_inc(ex_ev, 1)
                dve.drain()
            V.tensor_copy(Ts[:, :, H:TW], hg[:, :, :])
            V.tensor_tensor(tmp16[:, :, :], hg[:, :, :], asrc_row[:, :].unsqueeze(1).to_broadcast([P, G, HE]), ALU.mult)
            dve.drain()
            V.tensor_reduce(Ts[:, :, 0:H], tmp16[:, :, :].rearrange("p g (h k) -> p g h k", h=H), AX.X, ALU.add).then_inc(T_ready, 1)
            dve.drain()
            V.tensor_tensor(tmp16[:, :, :], hg[:, :, :], adst_row[:, :].unsqueeze(1).to_broadcast([P, G, HE]), ALU.mult)
            dve.drain()
            V.tensor_reduce(Ds[:, :, 0:H], tmp16[:, :, :].rearrange("p g (h k) -> p g h k", h=H), AX.X, ALU.add)
            dve.wait_ge(hist_in, 16)
            dve.wait_ge(crow_in, 16)
            V.tensor_scalar(small[:, 0, :], ccnt[:, :], 0.5, -BIG, ALU.is_lt, ALU.mult)
            dve.drain()
            V.tensor_tensor(cand[:, :, :], small[:, 0, :].unsqueeze(1).to_broadcast([P, H, G]),
                            crow[:, 0:H].to_broadcast([P, H, G]), ALU.add)
            dve.drain()
            V.tensor_tensor(Mx[:, :, :], cand[:, :, :], Ts[:, :, 0:H].rearrange("p g q -> p q g"), ALU.max)
            V.memset(cm[:, H:H + 1], 1.0)
            dve.drain()
            V.memset(mark[:, :], 0.0).then_inc(row_free, 2)
            dve.drain()
            V.memset(mark[:, :], 0.0).then_inc(spill_used, 2)

            with dve.Fori(0, n_pairs) as i:
                for k in range(2):
                    dve.wait_ge(col1_ready, 2 * i + (k + 1))
                    for j in range(RC + 1):
                        n = RC * k + j
                        if j < RC:
                            rows = ps[:, 2 + j % 3, :]
                            dve.wait_ge(far_ready, 16 * i + (n + 1 + RC))
                            V.scalar_tensor_tensor(scr[:, H, :], apart[:, j % 2, :], 0.0, tril[:, :], ALU.is_equal, ALU.mult,
                                                   accum_out=lead[:, 0:1])
                            dve.drain()
                            dve.wait_ge(row_ps, 16 * i + (n + 1))
                            V.tensor_scalar(lead[:, 1:2], lead[:, 0:1], 0.5, None, ALU.is_lt)
                            for q in range(H):
                                V.tensor_tensor_reduce(out=scr[:, q, :], in0=rows[:, 128 * q:128 * q + 128],
                                                       in1=apart[:, j % 2, :], scale=1.0, scalar=-BIG,
                                                       op0=ALU.subtract, op1=ALU.max, accum_out=cm[:, q:q + 1])
                            dve.drain()
                            V.tensor_scalar(ohhi[:, 0, j % 2, :], iota_hi[:, :], col[:, k, 1, j:j + 1], lead[:, 1:2],
                                            ALU.is_equal, ALU.mult).then_inc(row_free, 1)
                            dve.drain()
                            V.tensor_tensor(vr[:, j % 2, 0:H + 1, :], cm[:, :].to_broadcast([128, H + 1, G]),
                                            ohhi[:, 0, j % 2, :].unsqueeze(1).to_broadcast([128, H + 1, G]), ALU.mult)\
                                .then_inc(v_ready, 1)
                        if j >= 1:
                            if j == RC:
                                dve.drain()
                            dve.wait_ge(nb_ready, 16 * i + n)
                            vp = ps[0:P, 5 + (j - 1) % 2, 0:H * G].rearrange("p (q g) -> p q g", q=H)
                            V.tensor_tensor(cand[:, :, :], vp, nb[:, (j - 1) % 2, :].unsqueeze(1).to_broadcast([P, H, G]),
                                            ALU.add).then_inc(v_used, 1)
                            dve.drain()
                            V.tensor_tensor(Mx[:, :, :], Mx[:, :, :], cand[:, :, :], ALU.max)
                            if j == RC:
                                dve.drain()
            V.tensor_tensor(s4[:, 0].rearrange("p g q -> p q g"), Mx[:, :, :], Ds[:, :, 0:H].rearrange("p g q -> p q g"), ALU.add)
            dve.drain()
            V.scalar_tensor_tensor(Ds[:, :, H:DW], s4[:, 0], 0.2, s4[:, 0], ALU.mult, ALU.max).then_inc(D_ready, 1)
            V.tensor_tensor(s4[:, 1], Ts[:, :, 0:H], Ds[:, :, 0:H], ALU.add)
            dve.drain()
            V.scalar_tensor_tensor(s4[:, 2], s4[:, 1], 0.2, s4[:, 1], ALU.mult, ALU.max)
            dve.drain()
            V.tensor_tensor(s4[:, 0], s4[:, 2], Ds[:, :, H:DW], ALU.subtract)
            V.tensor_tensor(cw[:, :, :], Ds[:, :, 0:H], crow[:, 0:H].unsqueeze(1).to_broadcast([P, G, H]), ALU.add)
            dve.drain()
            V.scalar_tensor_tensor(s4[:, 3], cw[:, :, :], 0.2, cw[:, :, :], ALU.mult, ALU.max)
            dve.drain()
            V.tensor_tensor(cw[:, :, :], s4[:, 3], Ds[:, :, H:DW], ALU.subtract)
            dve.drain()
            V.tensor_scalar(cw[:, :, :], cw[:, :, :], 0.0, None, ALU.min).then_inc(self_arg, 1)
            with dve.Fori(0, n_pairs) as i:
                for k in range(2):
                    dve.wait_ge(g2_in[k], 128 * i + 128)
                    dve.wait_ge(spill_in[k], 16 * i + 16)
                    V.tensor_tensor(fe[:, k, :, 0:H], gs2[:, k, :, 0:H], gd[:, k, :, 0:H], ALU.add)
                    dve.drain()
                    V.scalar_tensor_tensor(fe[:, k, :, H:2 * H], fe[:, k, :, 0:H], 0.2, fe[:, k, :, 0:H], ALU.mult, ALU.max)
                    dve.drain()
                    V.tensor_tensor(fe[:, k, :, 0:H], fe[:, k, :, H:2 * H], gd[:, k, :, H:DW], ALU.subtract)
                    dve.drain()
                    V.tensor_scalar(ew[:, :, :], fe[:, k, :, 0:H], 0.0, None, ALU.min).then_inc(e_arg, 1)
                    dve.wait_ge(e_exp, 2 * i + (k + 1))
                    V.tensor_copy(fe[:, k, :, 0:H], ew[:, :, :])
                    for q in range(H):
                        ins = V.tensor_tensor(fe[:, k, :, H + E * q:H + E * (q + 1)], gs2[:, k, :, H + E * q:H + E * (q + 1)],
                                              ew[:, :, q:q + 1].to_broadcast([128, RC, E]), ALU.mult)
                    ins.then_inc(spill_used, 1)
                    dve.drain()
                    dve.wait_ge(oh2_ready, 2 * i + (k + 1))
                    for j in range(RC):
                        n = RC * k + j
                        dve.wait_ge(f_ps, 16 * i + (n + 1 + RC))
                        V.tensor_tensor(vr[:, j % 2], fe[:, k, j, :].to_broadcast([128, TW, G]),
                                        ohhi[:, k, j, :].unsqueeze(1).to_broadcast([128, TW, G]), ALU.mult).then_inc(f_ready, 1)
                    dve.drain()
            dve.wait_ge(self_exp, 1)
            dve.wait_ge(acc_done, 1)
            V.tensor_tensor(cw[:, :, :], cw[:, :, :], ccnt[:, :].to_broadcast([P, G, H]), ALU.mult)
            dve.drain()
            for q in range(H):
                V.tensor_tensor(c16[:, :, E * q:E * (q + 1)], cw[:, :, q:q + 1].to_broadcast([P, G, E]),
                                crow[:, H + E * q:H + E * (q + 1)].unsqueeze(1).to_broadcast([P, G, E]), ALU.mult)
            accA = ps[0:P, 6, 0:10 * G].rearrange("p (q g) -> p g q", g=G)
            accB = ps[0:P, 7, 0:10 * G].rearrange("p (q g) -> p g q", g=G)
            V.tensor_tensor(s4[:, 1], s4[:, 0], accA[:, :, 0:H], ALU.add)
            for q in range(H):
                V.tensor_tensor(tmp16[:, :, E * q:E * (q + 1)], hg[:, :, E * q:E * (q + 1)],
                                s4[:, 0, :, q:q + 1].to_broadcast([P, G, E]), ALU.mult)
            dve.drain()
            V.tensor_tensor(s4[:, 1], s4[:, 1], cw[:, :, :], ALU.add)
            V.tensor_tensor(tmp16[:, :, :], tmp16[:, :, :], c16[:, :, :], ALU.add)
            dve.drain()
            V.tensor_tensor(tmp16[:, :, 0:6], tmp16[:, :, 0:6], accA[:, :, H:10], ALU.add)
            V.tensor_tensor(tmp16[:, :, 6:16], tmp16[:, :, 6:16], accB, ALU.add)
            V.tensor_scalar(s4[:, 2], s4[:, 1], 1e-16, None, ALU.add)
            dve.drain()
            V.reciprocal(s4[:, 1], s4[:, 2])
            dve.drain()
            for q in range(H):
                V.tensor_tensor(tmp16[:, :, E * q:E * (q + 1)], tmp16[:, :, E * q:E * (q + 1)],
                                s4[:, 1, :, q:q + 1].to_broadcast([P, G, E]), ALU.mult)
            dve.drain()

            def bc16(r):
                return r[:, :].unsqueeze(1).to_broadcast([P, G, HE])

            def each(a):
                return a.to_broadcast([P, G, HE])

            V.tensor_tensor(tmp16[:, :, :], tmp16[:, :, :], bc16(bgat_row), ALU.add)
            dve.drain()
            V.tensor_reduce(small[:, 0, :], tmp16[:, :, :], AX.X, ALU.add)
            dve.drain()
            V.tensor_scalar(small[:, 0, :], small[:, 0, :], 1.0 / HE, None, ALU.mult)
            dve.drain()
            V.tensor_tensor(tmp16[:, :, :], tmp16[:, :, :], each(small[:, 0, :]), ALU.subtract)
            dve.drain()
            V.tensor_tensor(hg[:, :, :], tmp16[:, :, :], tmp16[:, :, :], ALU.mult)
            dve.drain()
            V.tensor_reduce(small[:, 0, :], hg[:, :, :], AX.X, ALU.add)
            dve.drain()
            V.tensor_scalar(small[:, 1, :], small[:, 0, :], 1.0 / HE, 1e-5, ALU.mult, ALU.add).then_inc(gv_ready, 1)
            dve.wait_ge(gs_ready, 1)
            V.reciprocal(small[:, 3, :], small[:, 2, :])
            dve.drain()
            V.tensor_tensor(tmp16[:, :, :], tmp16[:, :, :], each(small[:, 3, :]), ALU.mult)
            dve.drain()
            V.tensor_tensor(tmp16[:, :, :], tmp16[:, :, :], bc16(gamma_row), ALU.mult)
            dve.drain()
            V.tensor_tensor(tmp16[:, :, :], tmp16[:, :, :], bc16(beta_row), ALU.add)
            dve.drain()
            V.tensor_reduce(s4[:, 0], tmp16[:, :, :].rearrange("p g (h k) -> p g k h", h=H), AX.X, ALU.add)
            dve.drain()
            V.tensor_scalar(s4[:, 1], s4[:, 0], 1.0 / H, None, ALU.mult)
            dve.drain()
            V.tensor_reduce(small[:, 0, :], s4[:, 1], AX.X, ALU.max)
            for e in range(E):
                first = True
                for f in range(E):
                    if f == e:
                        continue
                    V.tensor_tensor(small[:, 4, :] if not first else s4[:, 3, :, e], s4[:, 1, :, f], s4[:, 1, :, e],
                                    ALU.is_ge if f < e else ALU.is_gt)
                    dve.drain()
                    if not first:
                        V.tensor_tensor(s4[:, 3, :, e], s4[:, 3, :, e], small[:, 4, :], ALU.add)
                        dve.drain()
                    first = False
            V.tensor_tensor(s4[:, 2], s4[:, 1], small[:, 0, :].to_broadcast([P, G, E]), ALU.subtract).then_inc(top_arg, 1)
            dve.wait_ge(top_exp, 1)
            V.scalar_tensor_tensor(s4[:, 4], s4[:, 3], 1.5, s4[:, 2], ALU.is_lt, ALU.mult)
            dve.drain()
            V.tensor_reduce(small[:, 5, :], s4[:, 4], AX.X, ALU.add)
            dve.drain()
            V.reciprocal(small[:, 6, :], small[:, 5, :])
            dve.drain()
            V.tensor_tensor(s4[:, 5], s4[:, 4], small[:, 6, :].to_broadcast([P, G, E]), ALU.mult)
            dve.drain()
            V.tensor_tensor(Oe, Oe, s4[:, 5].to_broadcast([P, G, E, C]), ALU.mult)
            dve.drain()
            mix = big[0:P, 0:G * C].rearrange("p (g c) -> p g c", g=G)
            V.tensor_reduce(mix, Oe.rearrange("p g e c -> p g c e"), AX.X, ALU.add)
            dve.drain()
            V.tensor_tensor(h[:, :, :], h[:, :, :], mix, ALU.add)
            dve.drain()
            with dve.Fori(0, B) as i:
                normed(i, 2)
                dve.wait_ge(so_ps, i + 1)
                hb = h[:, bass.ds(i * T, T), :]
                V.tensor_tensor(hb, hb, ps[0:P, 2, 0:T * C].rearrange("p (t c) -> p t c", t=T), ALU.add).then_inc(so_ev, 1)
                dve.drain()
            with dve.Fori(0, B) as i:
                normed(i, 3)
                V.scalar_tensor_tensor(sq[:, :, :], yb[:, :, :], -1.0, yb[:, :, :], ALU.mult, ALU.max)
                dve.drain()
                V.tensor_scalar(sq[:, :, :], sq[:, :, :], 1e-8, None, ALU.add).then_inc(la_ready, 1)
                dve.wait_ge(la_ln, i + 1)
                V.tensor_reduce(nm[:, :], sq[:, :, :], AX.X, ALU.max)
                dve.drain()
                V.tensor_tensor(sq[:, :, :], sq[:, :, :], nm[:, :].to_broadcast([P, T, C]), ALU.subtract).then_inc(la_sub, 1)
                dve.wait_ge(lo_ln, i + 1)
                V.tensor_tensor(cen[:, :, :], cen[:, :, :], nm[:, :].to_broadcast([P, T, C]), ALU.add)
                dve.drain()
                V.tensor_tensor(cen[:, :, :], cen[:, :, :], mw_row[:, :].unsqueeze(1).to_broadcast([P, T, C]), ALU.add).then_inc(lo_arg, 1)
                dve.wait_ge(lo_exp, i + 1)
                V.tensor_tensor(cen[:, :, :], cen[:, :, :], sq[:, :, :], ALU.mult)
                dve.drain()
                V.tensor_tensor(cen[:, :, :], cen[:, :, :], lbias_row[:, :].unsqueeze(1).to_broadcast([P, T, C]), ALU.add)
                dve.drain()
                hb = h[:, bass.ds(i * T, T), :]
                V.tensor_tensor(hb, hb, cen[:, :, :], ALU.add).then_inc(h_ready, 1)
                dve.drain()

        @block.tensor
        def _(pe):
            mm = nc.tensor.matmul

            def turn(out_, in_):
                n = in_.shape[0]
                return mm(out_, in_, ident[0:n, 0:n], start=True, stop=True)

            pe.wait_ge(c_ready, 4)
            pe.wait_ge(x_in, 16 * XT)
            for pr in range(PAIRS):
                for t in range(XT):
                    ins = turn(ps[:, 2 * pr + t // 3, XP * (t % 3):XP * (t % 3) + XP], xt[:, t, 128 * pr:128 * pr + 128])
                ins.then_inc(x_tr, 1)
            pe.wait_ge(w_in, 16 * N_W)
            pe.wait_ge(cnt_ready, 1)
            for pr in range(PAIRS):
                pe.wait_ge(x_ev, 2 * pr + 2)
                if pr:
                    pe.wait_ge(k_ev, 2)
                    pe.wait_ge(q_ev, 1)
                else:
                    mm(ps[0:1, 7, 0:128], cnt[:, :], ident[:, :], start=True, stop=True).then_inc(cnt_row, 1)
                    pe.wait_ge(rounds_ready, 1)
                for k in range(2):
                    mm(ps[:, 4 + k, 0:375], wk2[:, :], xT[:, pr, 375 * k:375 * k + 375], start=True, stop=True)
                for k in range(2):
                    o = WIN // 2 + HALF * k
                    ins = mm(ps[:, 6 + k, 0:HALF], wq2[:, :], xT[:, pr, o:o + HALF], start=True, stop=True)
                ins.then_inc(kq_ps, 1)
                if pr == 0:
                    pe.wait_ge(wl_act, 3)
                    pe.wait_ge(x_ev, 4)
                    for k in range(3):
                        turn(ps[0:C, 1, C * k:C * k + C], wraw[:, k, :])
                    turn(ps[:, 1, 3 * C:3 * C + 128], wl2[:, :])
                    mm(ps[0:P, 1, 320:320 + C], mw[0:C, 0:1].to_broadcast([C, P]), ident[0:C, 0:C],
                       start=True, stop=True).then_inc(wT_ps, 1)
                sc = ps[0:P, 2 * pr, 0:2 * T * WIN].rearrange("p (b t s) -> p b t s", b=2, s=WIN)
                for s in range(WIN):
                    n = WIN * pr + s
                    pe.wait_ge(tanh_done, n + 1)
                    for t in range(T):
                        ins = mm(sc[:, :, t, s], tile(ring[:, n % 3, :], t), v2[:, :], start=True, stop=True)
                    ins.then_inc(sc_ps, 1)

            def turn_batch(i, n):
                pe.wait_ge(y_ready[n], i + 1)
                for t in range(T):
                    ins = turn(ps[0:C, t // 4, P * (t % 4):P * (t % 4) + P], yb[:, t, :])
                ins.then_inc(yT_ps[n], 1)
                pe.wait_ge(yT_ev[n], i + 1)

            def count(c):
                pe.wait_ge(oh_ready, c + 1)
                for n in range(HC):
                    ins = mm(ps[0:DA, HB, 0:DB], oha[:, :, n], ohb[:, :, n], start=False, stop=False)
                ins.then_inc(oh_free, 1)

            pe.wait_ge(w_prep, 1)
            mm(ps[0:DA, HB, 0:DB], zrow[0:1, 0:DA], zrow[0:1, 0:DB], start=True, stop=False).then_inc(oh_free, 1)
            with pe.Fori(0, B) as i:
                turn_batch(i, 0)
                for t in range(T):
                    mm(ps[0:P, 6, C * t:C * t + C], tile(yT, t), wT[:, 2, :], start=True, stop=True)
                for k in range(2):
                    mm(ps[0:C, 2 + k, 0:HALF], wT[:, 0, :], yT[:, HALF * k:HALF * k + HALF], start=True, stop=True)
                    ins = mm(ps[0:C, 4 + k, 0:HALF], wT[:, 1, :], yT[:, HALF * k:HALF * k + HALF], start=True, stop=True)
                ins.then_inc(qkv_ps, 1)
                pe.wait_ge(qkv_ev, i + 1)
                for t in range(T):
                    if t >= 2:
                        pe.wait_ge(s_max, T * i + (t - 1))
                    for k in range(2):
                        ins = mm(ps[0:P, 2 * (t % 2) + k, 0:HALF], tile(qa[0:C, :], t), ka[0:C, HALF * k:HALF * k + HALF],
                                 start=True, stop=True)
                    ins.then_inc(s_ps, 1)
                pe.wait_ge(s_max, T * i + T)
                for t in range(T):
                    ins = mm(ps[C:C + 1, 6 + t // 4, P * (t % 4):P * (t % 4) + P], nm[:, t:t + 1], ident[0:P, 0:P],
                             start=True, stop=True)
                ins.then_inc(m_ps, 1)
                pe.wait_ge(m_ev, i + 1)
                for t in range(T):
                    if t >= 3:
                        pe.wait_ge(p_ready, T * i + (t - 2))
                    for k in range(2):
                        ins = mm(ps[0:P, 2 * (t % 3) + k, 0:HALF], tile(ka, t), qa[:, HALF * k:HALF * k + HALF],
                                 start=True, stop=True)
                    ins.then_inc(st_ps, 1)
                count(2 * i)
                pe.wait_ge(p_ready, T * i + T)
                for t in range(T):
                    for u in range(T):
                        ins = mm(ps[0:P, 6, (C + 1) * t:(C + 1) * (t + 1)], tile(PT[:, u, :], t), va[:, u, :],
                                 start=(u == 0), stop=(u == T - 1))
                ins.then_inc(o_ps, 1)
                count(2 * i + 1)
                pe.wait_ge(o_ev, i + 1)
            mm(ps[0:DA, HB, 0:DB], zrow[0:1, 0:DA], zrow[0:1, 0:DB], start=False, stop=True).then_inc(hist_ps, 1)
            with pe.Fori(0, B) as i:
                turn_batch(i, 1)
                for t in range(T):
                    ins = mm(ps[0:P, 2, HE * t:HE * t + HE], tile(yT, t), wgat[:, :], start=True, stop=True)
                ins.then_inc(gat_ps, 1)
                for k in range(2 * E):
                    if k >= 4:
                        pe.wait_ge(hid_ev, 2 * E * i + (k - 3))
                    mm(ps[:, 4 + k % 4, 0:HALF], w1[:, k // 2, :], yT[:, HALF * (k % 2):HALF * (k % 2) + HALF],
                       start=True, stop=True).then_inc(hid_ps, 1)
                pe.wait_ge(hid_ev, 2 * E * i + 2 * E)
                pe.wait_ge(gat_ev, i + 1)
                for t in range(T):
                    if t >= 2:
                        pe.wait_ge(ex_ev, T * i + (t - 1))
                    for e in range(E):
                        ins = mm(ps[0:P, 2 + t % 2, C * e:C * e + C], tile(HH[:, e, :], t), w2[:, e, :], start=True, stop=True)
                    ins.then_inc(ex_ps, 1)
                pe.wait_ge(ex_ev, T * i + T)
            pe.wait_ge(rounds_ready, 1)
            n_pairs = pe.value_load(ni[0:1, 0:1], min_val=1, max_val=EPAD // 16)
            pe.wait_ge(T_ready, 2)
            nc.tensor.matmul(ps[0:1, 7, 0:1], zrow[0:1, 0:1], zrow[0:1, 0:1], start=True, stop=True).then_inc(v_ps, RC)
            nc.tensor.matmul(ps[0:1, 7, 0:1], zrow[0:1, 0:1], zrow[0:1, 0:1], start=True, stop=True).then_inc(v_used, 2)
            with pe.Fori(0, n_pairs) as i:
                for k in range(2):
                    pe.wait_ge(col1_ready, 2 * i + (k + 1))
                    for c in range(2):
                        pe.wait_ge(far_ready, 16 * i + (RC * k + 4 * c + 4))
                        for j in range(4 * c, 4 * c + 4):
                            ins = mm(ps[:, c, 128 * (j % 4):128 * (j % 4) + 128], dcol[:, k, j:j + 1].to_broadcast([128, 128]),
                                     ident[:, :], start=True, stop=True)
                        ins.then_inc(drow_ps, 1)
                    pe.wait_ge(g1_in[k], 128 * i + 128)
                    pe.wait_ge(oh1_ready, 2 * i + (k + 1))

                    def spread(j):
                        n = RC * k + j
                        pe.wait_ge(row_free, 16 * i + (n if j >= 2 else n + 1))
                        for q in range(H):
                            ins = mm(ps[:, 2 + j % 3, 128 * q:128 * q + 128], gs[:, k, j, q:q + 1].to_broadcast([128, 128]),
                                     ident[:, :], start=True, stop=True)
                        ins.then_inc(row_ps, 1)

                    spread(0)
                    spread(1)
                    for j in range(RC):
                        n = RC * k + j
                        if j + 2 < RC:
                            spread(j + 2)
                        pe.wait_ge(v_ready, 16 * i + (n + 1))
                        pe.wait_ge(v_used, 16 * i + (n + 1))
                        ins = mm(ps[0:P, 5 + j % 2, 0:(H + 1) * G], ohlo[:, k, j, :],
                                 vr[:, j % 2, 0:H + 1, :].rearrange("p q g -> p (q g)"), start=True, stop=True)
                        ins.then_inc(v_ps, 1)
            pe.wait_ge(v_used, 16 * n_pairs + 2)
            for b0 in (6, 7):
                ins = mm(ps[0:P, b0, 0:10 * G], zrow[0:1, 0:P], zrow[0:1, 0:10 * G], start=True, stop=False)
            ins.then_inc(f_ps, RC + 2)
            with pe.Fori(0, n_pairs) as i:
                for k in range(2):
                    for j in range(RC):
                        n = RC * k + j
                        pe.wait_ge(f_ready, 16 * i + (n + 1))
                        for a in range(2):
                            ins = mm(ps[0:P, 6 + a, 0:10 * G], ohlo[:, k, j, :],
                                     vr[:, j % 2, 10 * a:10 * a + 10, :].rearrange("p q g -> p (q g)"), start=False, stop=False)
                        ins.then_inc(f_ps, 1)
            for b0 in (6, 7):
                ins = mm(ps[0:P, b0, 0:10 * G], zrow[0:1, 0:P], zrow[0:1, 0:10 * G], start=False, stop=True)
            ins.then_inc(acc_done, 1)
            with pe.Fori(0, B) as i:
                turn_batch(i, 2)
                for k in range(2):
                    ins = mm(ps[:, 2 + k, 0:HALF], wsig[:, :], yT[:, HALF * k:HALF * k + HALF], start=True, stop=True)
                ins.then_inc(sq_ps, 1)
                pe.wait_ge(sq_ev, i + 1)
                for t in range(T):
                    if t >= 2:
                        pe.wait_ge(sg_ev, T * i + (t - 1))
                    for k in range(2):
                        ins = mm(ps[0:P, 4 + 2 * (t % 2) + k, 0:HALF], tile(yT, t), qa[0:C, HALF * k:HALF * k + HALF],
                                 start=True, stop=True)
                    ins.then_inc(sg_ps, 1)
                pe.wait_ge(sg_ev, T * i + T)
                for t in range(T):
                    for u in range(T):
                        ins = mm(ps[0:P, 2, C * t:C * t + C], tile(PT[:, u, :], t), yb[:, u, :],
                                 start=(u == 0), stop=(u == T - 1))
                ins.then_inc(so_ps, 1)
                pe.wait_ge(so_ev, i + 1)
            with pe.Fori(0, B) as i:
                pe.wait_ge(la_exp, i + 1)
                for t in range(T):
                    ins = turn(ps[:, t // 4, P * (t % 4):P * (t % 4) + P], ES[:, t, :])
                ins.then_inc(lt_ps, 1)
                pe.wait_ge(lt_ev, i + 1)
                for t in range(T):
                    ins = mm(ps[0:P, 2 + t // 4, 128 * (t % 4):128 * (t % 4) + 128], tile(esT, t), wlT[:, :],
                             start=True, stop=True)
                ins.then_inc(lo_ps, 1)


_INS = ['x', 'L0_tok_W_qry', 'L0_tok_W_key', 'L0_tok_v', 'L0_tok_b', 'L0_attn_Wq', 'L0_attn_bq', 'L0_attn_Wk',
        'L0_attn_bk', 'L0_attn_Wv', 'L0_attn_bv', 'L0_ffn_W_gat', 'L0_ffn_att_src', 'L0_ffn_att_dst', 'L0_ffn_b_gat',
        'L0_ffn_ln_gamma', 'L0_ffn_ln_beta', 'L0_ffn_W1', 'L0_ffn_b1', 'L0_ffn_W2', 'L0_ffn_b2', 'L0_ffn_edge_index',
        'L1_attn_q_weight', 'L1_ffn_weight', 'L1_ffn_bias']
_OUTS = [((4, 742, 64), 'float32')]


def kernel(**inputs):
    import numpy as _np
    import concourse.bacc as _bacc
    from concourse import mybir as _mybir
    from concourse.bass_utils import run_bass_kernel_spmd as _run

    nc = _bacc.Bacc("TRN2", target_bir_lowering=False, num_devices=1)
    arrays, args = {}, []
    for name in _INS:
        a = _np.ascontiguousarray(inputs[name])
        arrays[f"in_{name}_dram"] = a
        args.append(nc.dram_tensor(f"in_{name}_dram", a.shape, _mybir.dt.from_np(a.dtype), kind="ExternalInput").ap())
    for i, (shape, dtype) in enumerate(_OUTS):
        dt = _mybir.dt.from_np(_np.dtype(dtype))
        args.append(nc.dram_tensor(f"out_{i}_dram", shape, dt, kind="ExternalOutput").ap())
    audio_tower(nc, *args)
    r = _run(nc, [arrays], core_ids=[0])
    return r.results[0]["out_0_dram"]
```

```python
import concourse.bass as bass
from concourse import mybir
from contextlib import ExitStack


def audio_tower(
    nc: bass.Bass,
    x: bass.AP,
    tok_W_qry: bass.AP,
    tok_W_key: bass.AP,
    tok_v: bass.AP,
    tok_b: bass.AP,
    attn_Wq: bass.AP,
    attn_bq: bass.AP,
    attn_Wk: bass.AP,
    attn_bk: bass.AP,
    attn_Wv: bass.AP,
    attn_bv: bass.AP,
    W_gat: bass.AP,
    att_src: bass.AP,
    att_dst: bass.AP,
    b_gat: bass.AP,
    ln_gamma: bass.AP,
    ln_beta: bass.AP,
    W1: bass.AP,
    b1: bass.AP,
    W2: bass.AP,
    b2: bass.AP,
    edge_index: bass.AP,
    sig_W: bass.AP,
    lns_W: bass.AP,
    lns_bias: bass.AP,
    out: bass.AP,
):
    F32 = mybir.dt.float32
    I32 = mybir.dt.int32
    BF16 = mybir.dt.bfloat16
    F32R = mybir.dt.float32r
    ALU = mybir.AluOpType
    ACT = mybir.ActivationFunctionType
    AX = mybir.AxisListType

    B, L, C = x.shape
    WIN = 9
    NW = L - WIN + 1
    P, T = 106, 7
    assert P * T == NW
    G = B * T
    M = B * NW
    EVEN = 372
    NP = 2 * EVEN
    LAST = NW - EVEN
    HALF = NW // 2
    XP = 125
    XT = L // XP
    PAIRS = B // 2
    H, E = att_src.shape
    HE = H * E
    FF = W1.shape[2]
    NE = edge_index.shape[1]
    EC = NE // 128
    EPAD = EC + 16
    KS = 4096
    assert M < KS
    RC = 8
    TW = H + HE
    U = 24
    OW = -(-M // U)
    MP = OW * U
    assert OW < 128
    SC = 16
    ROWS = NE // SC + 128
    NONE = NE + 128 * SC
    HU = H * U
    AU = TW * U
    BIG = 1.0e38
    DA, DB = 53, 56
    assert DA * DB == M
    HC = 256
    assert EC == 2 * B * HC
    HB = 7
    SCALE = 1.0 / float(C) ** 0.5
    ROUND = 12582912.0

    src_table = nc.dram_tensor("src_table", (MP + 1, TW), F32, kind="Internal").ap()
    adst_table = nc.dram_tensor("adst_table", (MP, H), F32, kind="Internal").ap()
    routed = nc.dram_tensor("routed", (NONE + 128 * EPAD, 1), I32, kind="Internal").ap()
    routed_rows = bass.AP(routed.tensor, 0, [[SC, ROWS], [1, SC]])
    hist_dram = nc.dram_tensor("hist_dram", (MP,), F32, kind="Internal").ap()
    gate_dram = nc.dram_tensor("gate_dram", (MP, E), F32, kind="Internal").ap()

    ctx = ExitStack()
    with ctx:
        def sb(name, shape, dt=F32):
            return ctx.enter_context(nc.sbuf_tensor(name, shape, dt))

        def sem(name):
            return ctx.enter_context(nc.semaphore(name))

        ident = sb("ident", [128, 128])
        before = sb("before", [128, 128])
        ones = sb("ones", [128, 128])
        iota_u = sb("iota_u", [128, U])
        bound = sb("bound", [128, OW + 1])
        node0 = sb("node0", [128, 1])
        away = sb("away", [128, 1])
        wk2 = sb("wk2", [128, 128])
        wq2 = sb("wq2", [128, 128])
        v2 = sb("v2", [128, 2])
        tb = sb("tb", [128, 1])
        wraw = sb("wraw", [C, 3, C])
        wT = sb("wT", [C, 3, C])
        wq_st = sb("wq_st", [C, 2 * C])
        wk_st = sb("wk_st", [C, 2 * C])
        bq = sb("bq", [128, 1])
        bk = sb("bk", [128, 1])
        bv_row = sb("bv_row", [P, C])
        wgat = sb("wgat", [C, HE])
        asrc_row = sb("asrc_row", [P, HE])
        adst_row = sb("adst_row", [P, HE])
        bgat_row = sb("bgat_row", [128, HE])
        gamma_row = sb("gamma_row", [128, HE])
        beta_row = sb("beta_row", [128, HE])
        w1 = sb("w1", [C, E, FF])
        b1c = sb("b1c", [FF, E])
        w2 = sb("w2", [FF, E, C])
        b2_row = sb("b2_row", [P, E * C])
        wsig = sb("wsig", [C, C])
        wsT2 = sb("wsT2", [C, 2 * C])
        wl = sb("wl", [128, 2, C])
        wl2 = sb("wl2", [128, 128])
        wlT = sb("wlT", [128, 128])
        mw = sb("mw", [128, 1])
        mw_row = sb("mw_row", [P, C])
        lbias_row = sb("lbias_row", [P, C])
        tok = sb("tok", [128, DB * HC // 2])
        o0 = XT * B * C
        xt = tok[0:XP, 0:o0].rearrange("p (t k) -> p t k", t=XT)
        xT = tok[:, o0:o0 + PAIRS * L].rearrange("p (r n) -> p r n", r=PAIRS)
        o0 += PAIRS * L
        ring = tok[:, o0:o0 + 3 * NW].rearrange("p (a n) -> p a n", a=3)
        assert o0 + 3 * NW <= DB * HC // 2
        big = sb("big", [128, E * NW + G * E * C])
        wts = sb("wts", [P, G, WIN])
        wsm = sb("wsm", [P, G])
        h = sb("h", [P, G, C])
        yA = tok[0:P, M:M + G * C].rearrange("p (g c) -> p g c", c=C)
        yT2 = tok[:, 0:M]
        yT = tok[0:C, 0:M]
        o0 = M + G * C
        own = tok[:, o0:o0 + U * TW].rearrange("p (u q) -> p u q", u=U)
        own_ad = tok[:, o0 + U * TW:o0 + U * (TW + H)].rearrange("p (u q) -> p u q", u=U)
        o0 += U * (TW + H)
        hg = tok[0:P, o0:o0 + G * HE].rearrange("p (g q) -> p g q", g=G)
        tmp16 = tok[0:P, o0 + G * HE:o0 + 2 * G * HE].rearrange("p (g q) -> p g q", g=G)
        o0 += 2 * G * HE
        Ts = tok[0:P, o0:o0 + G * TW].rearrange("p (g q) -> p g q", g=G)
        assert o0 + G * TW <= DB * HC // 2
        cen = sb("cen", [P, T, C])
        st = sb("st", [P, 4, G])
        parts = sb("parts", [128, NP], F32R)
        highs = sb("highs", [128, NP], F32R)
        lows = sb("lows", [128, NP], F32R)
        mrow = sb("mrow", [33, NP], F32R)
        ones33 = sb("ones33", [33, P], F32R)
        nmr = sb("nmr", [P, T], F32R)
        nmx = sb("nmx", [P, T, 33])
        nm = sb("nm", [P, T])
        rd = sb("rd", [P, T])
        ebuf = sb("ebuf", [128, 2, EPAD], I32)
        eroom = sb("eroom", [128, SC * AU])
        m8 = sb("m8", [128, RC])
        cnt = sb("cnt", [128, 1])
        nf = sb("nf", [1, 4])
        ni = sb("ni", [1, 2], I32)
        zrow = sb("zrow", [1, 560])
        empty_row = sb("empty_row", [1, TW])
        zfill = sb("zfill", [128, NONE // 2048], I32)
        kc = sb("kc", [128, 2, RC])
        kint = sb("kint", [128, 2, RC], I32)
        spare = ebuf[:, 1, :].bitcast(F32)
        cmp8 = spare[:, 0:RC * 128].rearrange("p (s o) -> p s o", s=RC)
        sel8 = spare[:, RC * 128:RC * 192].rearrange("p (s o) -> p s o", s=RC)
        above = sb("above", [128, OW + 1])
        share = sb("share", [128, OW])
        place = sb("place", [128, 129])
        step_to = sb("step_to", [128, 128])
        slot8 = sb("slot8", [128, RC])
        pos8 = sb("pos8", [128, 3, RC])
        posi = sb("posi", [128, 2, RC], I32)
        rows_o = sb("rows_o", [128, 1])
        row0 = sb("row0", [128, 1])
        cf = sb("cf", [128, 3])
        ridx = sb("ridx", [128, 2], I32)
        ad = sb("ad", [128, H, U])
        kr = sb("kr", [128, 2, SC], I32)
        sidx = sb("sidx", [128, 2, SC], I32)
        didx = sb("didx", [128, 2, SC], I32)
        lg = sb("lg", [128, 2, SC])
        gs = sb("gs", [128, 2, SC, TW])
        Ds = sb("Ds", [P, G, H])
        Mx = sb("Mx", [128, H, U])
        cm = sb("cm", [128, H, U])
        am = sb("am", [128, H, U])
        mtop = sb("mtop", [128, 2, H, U])
        carg = sb("carg", [128, 2, H, U])
        corr = sb("corr", [128, 2, H, U])
        acc = spare[:, RC * 192:RC * 192 + AU].rearrange("p (a u) -> p a u", u=U)
        assert RC * 192 + AU <= EPAD
        s16 = sb("s16", [128, HE, U])
        su = sb("su", [128, 8, U])
        s4 = sb("s4", [128, 6, E, U])
        gown = sb("gown", [128, U, E])
        gate = sb("gate", [P, G, E])
        digit = sb("digit", [128, 2, EC], BF16)
        room = sb("room", [128, DA * HC], BF16)
        oha = room[:, 0:DA * HC].rearrange("p (v c) -> p v c", v=DA)
        ohb = [r.bitcast(BF16).rearrange("p (v c) -> p v c", v=DB) for r in (tok[:, :], eroom[:, 0:DB * HC // 2])]
        roomf = room[:, :].bitcast(F32)
        d_lo, d_hi = roomf[:, 0:EC], roomf[:, EC:2 * EC]
        D0 = roomf[:, 0:SC * HU].rearrange("p (s q u) -> p s q u", s=SC, u=U)
        D1 = roomf[:, SC * HU:2 * SC * HU].rearrange("p (s q u) -> p s q u", s=SC, u=U)
        other = roomf[:, 2 * SC * HU:2 * SC * HU + SC * U].rearrange("p (s u) -> p s u", s=SC)
        vr = eroom[:, :].rearrange("p (s a) -> p s a", s=SC)
        hist_sb = sb("hist_sb", [DA, DB])
        ccnt = sb("ccnt", [128, U])
        crow = sb("crow", [128, TW])
        wself = sb("wself", [128, H, U])
        wcl = sb("wcl", [128, H, U])
        mark = sb("mark", [1, 1])
        zcol = sb("zcol", [C, 1])
        xw = big[0:P, 0:2 * T * WIN * C].rearrange("p (a t s c) -> p a t s c", a=2, s=WIN, c=C)
        PT = big[0:P, 0:T * NP].rearrange("p (t n) -> p t n", t=T)
        HH = big[:, 0:E * NW].rearrange("p (e n) -> p e n", e=E)
        Oe = big[0:P, E * NW:E * NW + G * E * C].rearrange("p (g e c) -> p g e c", e=E, c=C)
        o0 = T * NP
        yTa = big[0:C, o0:o0 + M]
        va = big[0:P, o0 + M:o0 + M + G * (C + 1)].rearrange("p (g c) -> p g c", c=C + 1)
        assert o0 + M + G * (C + 1) <= E * NW + G * E * C
        ES = big[0:P, 0:G * 2 * C].rearrange("p (g c) -> p g c", c=2 * C)
        esT = big[:, G * 2 * C:G * 2 * C + M]
        o0 = G * 2 * C + M
        cenA = big[0:P, o0:o0 + G * C].rearrange("p (g c) -> p g c", c=C)
        sqA = big[0:P, o0 + G * C:o0 + 2 * G * C].rearrange("p (g c) -> p g c", c=C)
        assert o0 + 2 * G * C <= E * NW + G * E * C
        mix = big[0:P, 0:G * C].rearrange("p (g c) -> p g c", c=C)
        l_lo, l_hi, key = eroom[:, 0:EC], eroom[:, EC:2 * EC], eroom[:, 2 * EC:3 * EC]
        lists = ebuf[:, 0, :].bitcast(F32)

        ps = ctx.enter_context(nc.psum_tensor("ps", [128, 8, 512], F32))

        def tile(ap, t):
            return ap[:, t * P:(t + 1) * P]

        c_ready = sem("c_ready")
        w_in = sem("w_in")
        z_ready = sem("z_ready")
        x_in = sem("x_in")
        e_in = sem("e_in")
        xw_in = [sem("xw_in0"), sem("xw_in1")]
        xw_used = sem("xw_used")
        wT_ps = sem("wT_ps")
        w_prep = sem("w_prep")
        wl_act = sem("wl_act")
        wl_dve = sem("wl_dve")
        cnt_ready = sem("cnt_ready")
        cnt_row = sem("cnt_row")
        rounds_ready = sem("rounds_ready")
        x_tr = sem("x_tr")
        x_ev = sem("x_ev")
        kq_ps = sem("kq_ps")
        tanh_done = sem("tanh_done")
        sc_ps = sem("sc_ps")
        sc_shift = sem("sc_shift")
        sc_exp = sem("sc_exp")
        tok_done = sem("tok_done")
        var_ready = [sem(f"var_ready{n}") for n in range(4)]
        std_ready = [sem(f"std_ready{n}") for n in range(4)]
        y_ready = [sem(f"y_ready{n}") for n in range(4)]
        yT_ps = [sem(f"yT_ps{n}") for n in range(3)]
        yT_ev = [sem(f"yT_ev{n}") for n in range(3)]
        v_all_ps = sem("v_all_ps")
        v_all = sem("v_all")
        qkv_ps = sem("qkv_ps")
        qkv_ev = sem("qkv_ev")
        s_ps = sem("s_ps")
        s_max = sem("s_max")
        nm_ready = sem("nm_ready")
        m_ps = sem("m_ps")
        m_ev = sem("m_ev")
        st_ps = sem("st_ps")
        p_ready = sem("p_ready")
        o_ps = sem("o_ps")
        o_ev = sem("o_ev")
        gat_ps = sem("gat_ps")
        gat_ev = sem("gat_ev")
        hid_ps = sem("hid_ps")
        hid_ev = sem("hid_ev")
        ex_ps = sem("ex_ps")
        ex_ev = sem("ex_ev")
        b2_added = sem("b2_added")
        listed = sem("listed")
        shares_ready = sem("shares_ready")
        tot_ps = sem("tot_ps")
        own_rows = sem("own_rows")
        base_ps = sem("base_ps")
        place_ready = sem("place_ready")
        zf_ready = sem("zf_ready")
        filled = sem("filled")
        sent = [sem("sent0"), sem("sent1")]
        T_ready = sem("T_ready")
        T_out = sem("T_out")
        own_in = sem("own_in")
        oh_ready = sem("oh_ready")
        oh_free = sem("oh_free")
        hist_ps = sem("hist_ps")
        hist_ev = sem("hist_ev")
        hist_out = sem("hist_out")
        hist_in = sem("hist_in")
        crow_in = sem("crow_in")
        row_in = [sem("row_in0"), sem("row_in1")]
        decoded = sem("decoded")
        g_in = [sem("g_in0"), sem("g_in1")]
        g_used = sem("g_used")
        e_arg = sem("e_arg")
        e_exp = sem("e_exp")
        num_ready = sem("num_ready")
        sum_ps = sem("sum_ps")
        self_arg = sem("self_arg")
        self_exp = sem("self_exp")
        gv_ready = sem("gv_ready")
        gs_ready = sem("gs_ready")
        top_arg = sem("top_arg")
        top_exp = sem("top_exp")
        gate_ready = sem("gate_ready")
        gate_out = sem("gate_out")
        gate_in = sem("gate_in")
        sq_ps = sem("sq_ps")
        sq_hi = sem("sq_hi")
        sq_ev = sem("sq_ev")
        sg_ps = sem("sg_ps")
        sg_ev = sem("sg_ev")
        so_ps = sem("so_ps")
        so_ev = sem("so_ev")
        la_ready = sem("la_ready")
        la_ln = sem("la_ln")
        la_sub = sem("la_sub")
        la_exp = sem("la_exp")
        lt_ps = sem("lt_ps")
        lt_ev = sem("lt_ev")
        lo_ps = sem("lo_ps")
        lo_ln = sem("lo_ln")
        lo_arg = sem("lo_arg")
        lo_exp = sem("lo_exp")
        lo_ev = sem("lo_ev")
        h_ready = sem("h_ready")
        out_done = sem("out_done")

        N_W = 33
        block = ctx.enter_context(nc.Block())

        def row(ap, n, parts=P):
            return bass.AP(ap.tensor, 0, [[0, parts], [1, n]])

        @block.sync
        def _(sp):
            xv = x.rearrange("b (t p) c -> p t b c", p=XP)
            for t in range(XT):
                sp.dma_start(xt[:, t, :].rearrange("p (b c) -> p b c", b=B), xv[:, t]).then_inc(x_in, 16)
            ev = edge_index.rearrange("r (p c) -> p r c", p=128)
            sp.dma_start(ebuf[:, :, 0:EC], ev).then_inc(e_in, 16)
            n = 0

            def load(dst, src):
                nonlocal n
                sp.dma_start(dst, src).then_inc(w_in, 16)
                n += 1

            sp.wait_ge(z_ready, 4)
            for k in range(2):
                load(wk2[64 * k:64 * k + 64, 64 * k:64 * k + 64], tok_W_key)
                load(wq2[64 * k:64 * k + 64, 64 * k:64 * k + 64], tok_W_qry)
                load(v2[64 * k:64 * k + 64, k:k + 1], tok_v.rearrange("(p a) -> p a", a=1))
                load(bq[64 * k:64 * k + 64, :], attn_bq.rearrange("(p a) -> p a", a=1))
                load(bk[64 * k:64 * k + 64, :], attn_bk.rearrange("(p a) -> p a", a=1))
                load(tb[64 * k:64 * k + 64, :], tok_b.rearrange("(p a) -> p a", a=1))
                load(wl[64 * k:64 * k + 64, 0, :], lns_W)
            for k, w in enumerate((attn_Wq, attn_Wk, attn_Wv)):
                load(wraw[:, k, :], w)
            load(bv_row[:, :], row(attn_bv, C))
            load(wgat[:, :], W_gat)
            load(asrc_row[:, :], row(att_src, HE))
            load(adst_row[:, :], row(att_dst, HE))
            load(bgat_row[:, :], row(b_gat, HE, 128))
            load(gamma_row[:, :], row(ln_gamma, HE, 128))
            load(beta_row[:, :], row(ln_beta, HE, 128))
            load(w1[:, :, :], W1.rearrange("e c f -> c e f"))
            for e in range(E):
                load(b1c[:, e:e + 1], b1[e, :].rearrange("(f a) -> f a", a=1))
            load(w2[:, :, :], W2.rearrange("e f c -> f e c"))
            load(b2_row[:, :], row(b2, E * C))
            load(wsig[:, :], sig_W)
            load(lbias_row[:, :], row(lns_bias, C))
            assert n == N_W
            for b in range(B):
                if b >= 2:
                    sp.wait_ge(xw_used, b - 1)
                sp.dma_start(xw[:, b % 2].rearrange("p t s c -> p t (s c)"),
                             bass.AP(x.tensor, b * L * C, [[C, P], [P * C, T], [1, WIN * C]])).then_inc(xw_in[b % 2], 16)
            sp.wait_ge(zf_ready, 1)
            sp.dma_start(routed[0:NONE, :].rearrange("(p a n) o -> p a (n o)", p=128, a=16),
                         zfill[:, :].unsqueeze(1).to_broadcast([128, 16, NONE // 2048])).then_inc(filled, 16)
            sp.wait_ge(hist_ev, 1)
            sp.dma_start(hist_dram[0:M].rearrange("(a b) -> a b", a=DA), hist_sb[:, :]).then_inc(hist_out, 16)
            sp.dma_start(bass.AP(hist_dram.tensor, M, [[0, 1], [1, MP - M]]), zrow[0:1, 0:MP - M]).then_inc(hist_out, 16)
            sp.wait_ge(T_ready, 3)
            sp.dma_start(src_table[0:1, :], empty_row[:, :]).then_inc(T_out, 16)
            sp.dma_start(src_table[1:M + 1, :].rearrange("(g p) q -> p g q", p=P), Ts[:, :, :]).then_inc(T_out, 16)
            sp.dma_start(bass.AP(src_table.tensor, (M + 1) * TW, [[0, 1], [1, (MP - M) * TW]]),
                         zrow[0:1, 0:(MP - M) * TW]).then_inc(T_out, 16)
            sp.dma_start(adst_table[0:M, :].rearrange("(g p) q -> p g q", p=P), Ds[:, :, :]).then_inc(T_out, 16)
            sp.dma_start(bass.AP(adst_table.tensor, M * H, [[0, 1], [1, (MP - M) * H]]),
                         zrow[0:1, 0:(MP - M) * H]).then_inc(T_out, 16)
            sp.wait_ge(hist_out, 32)
            sp.dma_start(ccnt[0:OW, :], hist_dram.rearrange("(o u) -> o u", u=U)).then_inc(hist_in, 16)
            sp.wait_ge(T_out, 80)
            sp.dma_start(crow[:, :], bass.AP(src_table.tensor, M * TW, [[0, 128], [1, TW]])).then_inc(crow_in, 16)
            sp.dma_start(own[0:OW, :, :].rearrange("p u q -> p (u q)"),
                         src_table[1:MP + 1, :].rearrange("(o u) q -> o (u q)", u=U)).then_inc(own_in, 16)
            sp.dma_start(own_ad[0:OW, :, :].rearrange("p u q -> p (u q)"),
                         adst_table.rearrange("(o u) q -> o (u q)", u=U)).then_inc(own_in, 16)
            sp.wait_ge(gate_ready, 1)
            sp.dma_start(gate_dram.rearrange("(o u) e -> o (u e)", u=U),
                         gown[0:OW, :, :].rearrange("p u e -> p (u e)")).then_inc(gate_out, 16)
            sp.wait_ge(gate_out, 16)
            sp.dma_start(gate[:, :, :], gate_dram[0:M, :].rearrange("(g p) e -> p g e", p=P)).then_inc(gate_in, 16)
            sp.wait_ge(h_ready, 1)
            sp.dma_start(out.rearrange("b (t p) c -> p (b t) c", p=P), h[:, :, :]).then_inc(out_done, 16)
            sp.wait_ge(out_done, 16)

        @block.gpsimd
        def _(pool):
            nc.gpsimd.memset(wk2[:, :], 0.0).then_inc(z_ready, 1)
            nc.gpsimd.memset(wq2[:, :], 0.0).then_inc(z_ready, 1)
            nc.gpsimd.memset(v2[:, :], 0.0).then_inc(z_ready, 1)
            nc.gpsimd.memset(wl2[:, :], 0.0).then_inc(z_ready, 1)
            nc.gpsimd.memset(ident[:, :], 0.0)
            nc.gpsimd.memset(before[:, :], 1.0)
            nc.gpsimd.memset(zrow[:, :], 0.0).then_inc(T_ready, 1)
            nc.gpsimd.memset(empty_row[:, :], 0.0)
            nc.gpsimd.memset(zfill[:, :], 0).then_inc(zf_ready, 1)
            nc.gpsimd.memset(zcol[:, :], 0.0)
            nc.gpsimd.memset(ones[:, :], 1.0)
            nc.gpsimd.memset(above[:, :], 0.0)
            nc.gpsimd.memset(ccnt[:, :], 0.0)
            nc.gpsimd.memset(cf[:, :], 0.0)
            pool.drain()
            nc.gpsimd.memset(empty_row[:, 0:H], -BIG).then_inc(T_ready, 1)
            nc.gpsimd.affine_select(out=ident[:, :], in_=ident[:, :], compare_op=ALU.not_equal, fill=1.0,
                                    base=0, pattern=[[-1, 128]], channel_multiplier=1).then_inc(c_ready, 1)
            nc.gpsimd.affine_select(out=before[:, :], in_=before[:, :], compare_op=ALU.is_gt, fill=0.0,
                                    base=0, pattern=[[1, 128]], channel_multiplier=-1).then_inc(c_ready, 1)
            nc.gpsimd.iota(iota_u[:, :], pattern=[[1, U]], base=0, channel_multiplier=0,
                           allow_small_or_imprecise_dtypes=True).then_inc(c_ready, 1)
            nc.gpsimd.iota(bound[:, :], pattern=[[U, OW + 1]], base=0, channel_multiplier=0,
                           allow_small_or_imprecise_dtypes=True)
            nc.gpsimd.iota(away[:, :], pattern=[[0, 1]], base=0, channel_multiplier=EPAD,
                           allow_small_or_imprecise_dtypes=True)
            nc.gpsimd.iota(slot8[:, :], pattern=[[1, RC]], base=0, channel_multiplier=0,
                           allow_small_or_imprecise_dtypes=True)
            nc.gpsimd.iota(node0[:, :], pattern=[[0, 1]], base=0, channel_multiplier=U,
                           allow_small_or_imprecise_dtypes=True)
            pool.drain()
            nc.gpsimd.tensor_scalar(bound[:, :], bound[:, :], float(KS), None, ALU.mult)
            nc.gpsimd.tensor_scalar(away[:, :], away[:, :], float(NONE), None, ALU.add)
            pool.drain()
            nc.gpsimd.memset(zrow[0:1, 0:1], 0.0).then_inc(c_ready, 1)
            pool.wait_ge(rounds_ready, 1)
            nc.gpsimd.memset(cmp8[:, :, :], 0.0)
            pool.drain()
            n_pairs = pool.value_load(ni[0:1, 0:1], min_val=2, max_val=EPAD // 16)

            def sign_bounds(i, k):
                nc.gpsimd.tensor_copy(kc[:, k, :], lists[:, bass.ds(16 * i + RC * k, RC)])
                pool.drain()
                for j in range(RC):
                    nc.gpsimd.tensor_scalar(cmp8[:, j, 0:OW + 1], bound[:, :], kc[:, k, j:j + 1], None, ALU.is_lt)
                pool.drain()

            with pool.Fori(0, n_pairs) as i:
                for k in range(2):
                    pool.wait_ge(listed, 2 * i + (k + 1))
                    sign_bounds(i, k)
                    for n in (4, 2, 1):
                        nc.gpsimd.tensor_tensor(cmp8[:, 0:n, :], cmp8[:, 0:n, :], cmp8[:, n:2 * n, :], ALU.add)
                        pool.drain()
                    nc.gpsimd.tensor_tensor(above[:, :], above[:, :], cmp8[:, 0, 0:OW + 1], ALU.add)
                    pool.drain()
            nc.gpsimd.tensor_tensor(share[:, :], above[:, 0:OW], above[:, 1:OW + 1], ALU.subtract).then_inc(shares_ready, 1)
            pool.wait_ge(place_ready, 1)
            pool.wait_ge(filled, 16)
            nc.gpsimd.memset(cmp8[:, :, OW:128], 0.0)
            nc.gpsimd.memset(cf[:, :], 0.0)
            pool.drain()
            def route(i, first):
                for k in range(2):
                    sign_bounds(i, k)
                    nc.gpsimd.tensor_tensor(cmp8[:, :, 0:OW], cmp8[:, :, 0:OW],
                                            step_to[:, 0:OW].unsqueeze(1).to_broadcast([128, RC, OW]), ALU.mult)
                    nc.gpsimd.memset(cmp8[:, :, OW:OW + 1], 0.0)
                    pool.drain()
                    n = 64
                    nc.gpsimd.tensor_tensor(sel8[:, :, 0:n], cmp8[:, :, 0:n], cmp8[:, :, n:2 * n], ALU.add)
                    pool.drain()
                    while n > 1:
                        n //= 2
                        nc.gpsimd.tensor_tensor(sel8[:, :, 0:n], sel8[:, :, 0:n], sel8[:, :, n:2 * n], ALU.add)
                        pool.drain()
                    nc.gpsimd.tensor_scalar(pos8[:, 0, :], kc[:, k, :], 0.5, away[:, 0:1], ALU.is_lt, ALU.mult)
                    if not first:
                        pool.wait_ge(sent[k], 128 * i)
                    nc.gpsimd.tensor_tensor(pos8[:, 1, :], sel8[:, :, 0], slot8[:, :], ALU.add)
                    nc.gpsimd.tensor_copy(kint[:, k, :], kc[:, k, :])
                    pool.drain()
                    nc.gpsimd.tensor_tensor(pos8[:, 2, :], pos8[:, 0, :], pos8[:, 1, :], ALU.add)
                    nc.gpsimd.tensor_scalar(slot8[:, :], slot8[:, :], float(RC), None, ALU.add)
                    pool.drain()
                    nc.gpsimd.tensor_copy(posi[:, k, :], pos8[:, 2, :])
                    pool.drain()
                    for j in range(RC):
                        nc.gpsimd.indirect_dma_start(routed, bass.IndirectOffsetOnAxis(posi[:, k, j:j + 1], 0),
                                                     kint[:, k, j:j + 1], None).then_inc(sent[k], 16)

            route(0, True)
            with pool.Fori(1, n_pairs) as i:
                route(i, False)
            for k in range(2):
                pool.wait_ge(sent[k], 128 * n_pairs)

            def fetch_row(k):
                nc.gpsimd.tensor_tensor(cf[:, 1:2], cf[:, 0:1], row0[:, :], ALU.add)
                nc.gpsimd.tensor_scalar(cf[:, 2:3], cf[:, 0:1], rows_o[:, 0:1], None, ALU.is_lt)
                pool.drain()
                nc.gpsimd.tensor_tensor(cf[:, 1:2], cf[:, 1:2], cf[:, 2:3], ALU.mult)
                nc.gpsimd.tensor_scalar(cf[:, 0:1], cf[:, 0:1], 1.0, None, ALU.add)
                pool.drain()
                nc.gpsimd.tensor_scalar(ridx[:, k:k + 1], cf[:, 1:2], float(ROWS - 1), None, ALU.add)
                pool.drain()
                nc.gpsimd.indirect_dma_start(kr[:, k, :], None, routed_rows,
                                             bass.IndirectOffsetOnAxis(ridx[:, k:k + 1], 0)).then_inc(row_in[k], 16)

            def fetch_sources(k):
                for j in range(SC):
                    nc.gpsimd.indirect_dma_start(gs[:, k, j, :], None, src_table,
                                                 bass.IndirectOffsetOnAxis(sidx[:, k, j:j + 1], 0)).then_inc(g_in[k], 16)

            fetch_row(0)
            fetch_row(1)
            n_chunks2 = pool.value_load(ni[0:1, 1:2], min_val=PAIRS + 1, max_val=NE // (2 * SC) + 1)
            pool.wait_ge(decoded, 1)
            pool.wait_ge(T_out, 80)
            fetch_sources(0)
            with pool.Fori(0, n_chunks2) as i:
                for k in range(2):
                    pool.wait_ge(decoded, 2 * i + (k + 2))
                    pool.wait_ge(g_used, 2 * i + (k + 1))
                    fetch_row(k)
                    fetch_sources(1 - k)
            for k in range(2):
                pool.wait_ge(row_in[k], 16 * n_chunks2 + 16)
            pool.wait_ge(g_in[0], 256 * n_chunks2 + 256)
            pool.wait_ge(ex_ev, B * T)
            nc.gpsimd.tensor_tensor(Oe.rearrange("p g e c -> p g (e c)"), Oe.rearrange("p g e c -> p g (e c)"),
                                    b2_row[:, :].unsqueeze(1).to_broadcast([P, G, E * C]), ALU.add).then_inc(b2_added, 1)

        @block.scalar
        def _(act):
            for pr in range(PAIRS):
                act.wait_ge(x_tr, pr + 1)
                for k in range(2):
                    nc.scalar.copy(xT[:, pr, 375 * k:375 * k + 375], ps[:, 2 * pr + k, 0:375]).then_inc(x_ev, 1)
            for pr in range(PAIRS):
                for s in range(WIN):
                    n = WIN * pr + s
                    act.wait_ge(kq_ps, n + 1)
                    if n >= 3:
                        act.wait_ge(sc_ps, n - 2)
                    b0 = 4 + 2 * (n % 2)
                    nc.scalar.activation(ring[:, n % 3, :].rearrange("p (a n) -> p a n", a=2), ps[:, b0:b0 + 2, 0:HALF],
                                         ACT.Tanh, bias=tb[:, 0:1]).then_inc(tanh_done, 1)
            act.wait_ge(wl_dve, 1)
            nc.scalar.activation(wl[:, 1, :], wl[:, 1, :], ACT.Ln).then_inc(wl_act, 1)
            act.wait_ge(wl_dve, 2)
            nc.scalar.activation(wl2[0:64, 0:64], wl[0:64, 1, :], ACT.Exp).then_inc(wl_act, 1)
            nc.scalar.activation(wl2[64:128, 64:128], wl[64:128, 0, :], ACT.Sign).then_inc(wl_act, 1)
            act.wait_ge(sc_shift, 1)
            nc.scalar.activation(wts[:, :, :], wts[:, :, :], ACT.Exp).then_inc(sc_exp, 1)

            def std(n):
                act.wait_ge(var_ready[n], 1)
                nc.scalar.activation(st[:, 3, :], st[:, 2, :], ACT.Sqrt).then_inc(std_ready[n], 1)

            def transposed(n, to):
                m = to.shape[0]
                for b in range(B):
                    act.wait_ge(yT_ps[n], b + 1)
                    nc.scalar.copy(to[:, b * NW:b * NW + 4 * P], ps[0:m, 2 * b, 0:4 * P])
                    nc.scalar.copy(to[:, b * NW + 4 * P:b * NW + NW], ps[0:m, 2 * b + 1, 0:3 * P]).then_inc(yT_ev[n], 1)

            std(0)
            transposed(0, yTa)
            with act.Fori(0, B) as i:
                act.wait_ge(m_ps, i + 1)
                nc.scalar.copy(mrow[:, 0:4 * P], ps[64:97, 6, 0:4 * P])
                nc.scalar.copy(mrow[:, 4 * P:NW], ps[64:97, 7, 0:3 * P]).then_inc(m_ev, 1)
                for t in range(T):
                    act.wait_ge(st_ps, T * i + (t + 1))
                    b0 = 2 * (t % 3)
                    nc.scalar.activation(PT[:, t, :].rearrange("p (a n) -> p a n", a=2),
                                         ps[0:P, b0:b0 + 2, 0:EVEN], ACT.Exp, scale=SCALE).then_inc(p_ready, 1)
            std(1)
            transposed(1, yT)
            act.wait_ge(self_arg, 1)
            nc.scalar.activation(wself[:, :, :], wself[:, :, :], ACT.Exp)
            nc.scalar.activation(wcl[:, :, :], wcl[:, :, :], ACT.Exp).then_inc(self_exp, 1)

            def weights(i, k):
                act.wait_ge(e_arg, 2 * i + (k + 1))
                act.wait_ge(sum_ps, 2 * i + (k + 1))
                nc.scalar.activation(vr[:, :, 0:HU].rearrange("p s (q u) -> p s q u", u=U), D1, ACT.Exp)
                nc.scalar.activation(corr[:, k], carg[:, k], ACT.Exp).then_inc(e_exp, 1)

            act.wait_ge(own_rows, 3)
            n_chunks2 = act.value_load(ni[0:1, 1:2], min_val=PAIRS + 1, max_val=NE // (2 * SC) + 1)
            with act.Fori(0, PAIRS) as i:
                for k in range(2):
                    weights(i, k)
                    for n in range(2 * E):
                        act.wait_ge(hid_ps, 4 * E * i + (2 * E * k + n + 1))
                        nc.scalar.activation(HH[:, n // 2, HALF * (n % 2):HALF * (n % 2) + HALF],
                                             ps[:, n % 4, 0:HALF], ACT.Gelu, bias=b1c[:, n // 2:n // 2 + 1]).then_inc(hid_ev, 1)
                    for t in range(T):
                        act.wait_ge(ex_ps, 2 * T * i + (T * k + t + 1))
                        nc.scalar.copy(Oe[:, bass.ds(2 * T * i + (T * k + t), 1), :, :].rearrange("p g e c -> p (g e c)"),
                                       ps[0:P, 4 + t % 2, 0:E * C]).then_inc(ex_ev, 1)
            with act.Fori(PAIRS, n_chunks2) as i:
                for k in range(2):
                    weights(i, k)
            act.wait_ge(gv_ready, 1)
            nc.scalar.activation(su[:, 2, :], su[:, 1, :], ACT.Sqrt).then_inc(gs_ready, 1)
            act.wait_ge(top_arg, 1)
            nc.scalar.activation(s4[:, 2], s4[:, 2], ACT.Exp).then_inc(top_exp, 1)
            std(2)
            transposed(2, yT2)

            def keys(i):
                act.wait_ge(sq_ps, i + 1)
                nc.scalar.copy(highs[:, 0:NW], yT2[:, bass.ds(i * NW, NW)]).then_inc(sq_hi, 1)
                nc.scalar.copy(parts[:, 0:NW].rearrange("p (a n) -> p a n", a=2), ps[:, 2:4, 0:HALF]).then_inc(sq_hi, 1)

            def attend_sigmoid(i, last):
                for t in range(T):
                    act.wait_ge(sg_ps, T * i + (t + 1))
                    b0 = 4 + 2 * (t % 2)
                    nc.scalar.activation(PT[:, t, :].rearrange("p (a n) -> p a n", a=2),
                                         ps[0:P, b0:b0 + 2, 0:EVEN], ACT.Sigmoid).then_inc(sg_ev, 1)
                if not last:
                    keys(i + 1)

            keys(0)
            with act.Fori(0, B - 1) as i:
                attend_sigmoid(i, False)
            attend_sigmoid(B - 1, True)
            std(3)
            act.wait_ge(la_ready, 1)
            nc.scalar.activation(sqA, sqA, ACT.Ln).then_inc(la_ln, 1)
            nc.scalar.activation(ES[:, :, C:2 * C], yA, ACT.Sign)
            act.wait_ge(la_sub, 1)
            nc.scalar.activation(ES[:, :, 0:C], sqA, ACT.Exp).then_inc(la_exp, 1)
            for b in range(B):
                act.wait_ge(lt_ps, b + 1)
                nc.scalar.copy(esT[:, b * NW:b * NW + 4 * P], ps[:, 2 * b, 0:4 * P])
                nc.scalar.copy(esT[:, b * NW + 4 * P:b * NW + NW], ps[:, 2 * b + 1, 0:3 * P]).then_inc(lt_ev, 1)
            for n in range(G // 4):
                act.wait_ge(lo_ps, n + 1)
                v = ps[0:P, n, :].rearrange("p (t c) -> p t c", c=128)
                nc.scalar.activation(cenA[:, 4 * n:4 * n + 4, :], v[:, :, 0:C], ACT.Ln)
                ins = nc.scalar.activation(sqA[:, 4 * n:4 * n + 4, :], v[:, :, C:2 * C], ACT.Sign)
            ins.then_inc(lo_ln, 1)
            act.wait_ge(lo_arg, 1)
            nc.scalar.activation(cenA, cenA, ACT.Exp).then_inc(lo_exp, 1)

        @block.vector
        def _(dve):
            V = nc.vector
            dve.wait_ge(e_in, 16)
            V.tensor_copy(l_lo[:, 0:EC], ebuf[:, 0, 0:EC])
            V.tensor_copy(l_hi[:, 0:EC], ebuf[:, 1, 0:EC])
            dve.drain()
            V.scalar_tensor_tensor(key[:, :], l_hi[:, 0:EC], float(KS), l_lo[:, 0:EC], ALU.mult, ALU.add)
            dve.drain()
            V.tensor_scalar(key[:, :], key[:, :], 1.0, None, ALU.add)
            dve.drain()
            V.scalar_tensor_tensor(key[:, :], l_hi[:, 0:EC], float(M), key[:, :], ALU.is_lt, ALU.mult)
            dve.drain()
            V.scalar_tensor_tensor(key[:, :], l_lo[:, 0:EC], float(M - 1), key[:, :], ALU.is_lt, ALU.mult)
            dve.drain()
            V.tensor_scalar(d_lo, key[:, :], 0.0, 0.0, ALU.is_gt, ALU.add,
                            accum_out=cnt[:, :]).then_inc(cnt_ready, 1)
            dve.wait_ge(cnt_row, 1)
            V.tensor_reduce(nf[:, 0:1], ps[0:1, 3, 0:128], AX.X, ALU.max)
            dve.drain()
            V.tensor_scalar(nf[:, 1:2], nf[:, 0:1], 1.0 / 16, 15.0 / 16 - 0.5 + 1.0 / 64, ALU.mult, ALU.add)
            dve.drain()
            V.tensor_scalar(nf[:, 0:1], nf[:, 1:2], ROUND, -ROUND, ALU.add, ALU.add)
            dve.drain()
            V.tensor_scalar(ni[:, 0:1], nf[:, 0:1], 2.0, None, ALU.max).then_inc(rounds_ready, 1)
            dve.wait_ge(rounds_ready, 1)
            dve.wait_ge(c_ready, 4)
            dve.wait_ge(w_in, 16 * N_W)
            V.scalar_tensor_tensor(wl[:, 1, :], wl[:, 0, :], -1.0, wl[:, 0, :], ALU.mult, ALU.max)
            dve.drain()
            V.tensor_scalar(wl[:, 1, :], wl[:, 1, :], 1e-8, None, ALU.add).then_inc(wl_dve, 1)
            n_pairs = dve.value_load(ni[0:1, 0:1], min_val=2, max_val=EPAD // 16)
            with dve.Fori(0, n_pairs) as i:
                for k in range(2):
                    V.max(m8[:, :], key)
                    dve.drain()
                    V.match_replace(key, m8[:, :], key, 0.0)
                    V.tensor_copy(lists[:, bass.ds(16 * i + RC * k, RC)], m8[:, :]).then_inc(listed, 1)
                    dve.drain()
            dve.wait_ge(wl_act, 1)
            V.tensor_reduce(mw[:, :], wl[:, 1, :], AX.X, ALU.max)
            dve.drain()
            V.tensor_scalar(wl[:, 1, :], wl[:, 1, :], mw[:, 0:1], None, ALU.subtract).then_inc(wl_dve, 1)
            dve.wait_ge(wT_ps, 1)
            V.tensor_copy(wT[:, :, :], ps[0:C, 1, 0:3 * C].rearrange("p (k c) -> p k c", k=3))
            for n, w in enumerate((wq_st, wk_st)):
                V.tensor_copy(w[:, :].rearrange("p (a c) -> p a c", a=2),
                              ps[0:C, 1, C * n:C * n + C].unsqueeze(1).to_broadcast([C, 2, C]))
            V.tensor_copy(wlT[:, :], ps[:, 1, 3 * C:3 * C + 128])
            V.tensor_copy(mw_row[:, :], ps[0:P, 1, 320:320 + C])
            V.memset(nmx[:, :, :], 0.0)
            V.tensor_copy(ones33[:, :], ones[0:33, 0:P])
            for a in (parts, highs, lows):
                V.tensor_scalar(a[:, NW:NP], ones[:, 0:NP - NW], 0.0, None, ALU.mult)
            V.tensor_scalar(mrow[:, NW:NP], ones[0:33, 0:NP - NW], 0.0, None, ALU.mult)
            V.tensor_copy(wsT2[:, :].rearrange("p (a c) -> p a c", a=2),
                          ps[0:C, 1, 384:384 + C].unsqueeze(1).to_broadcast([C, 2, C])).then_inc(w_prep, 1)
            dve.wait_ge(sc_ps, 2 * WIN)
            for pr in range(PAIRS):
                for bb in range(2):
                    b = 2 * pr + bb
                    V.tensor_copy(wts[:, T * b:T * b + T, :],
                                  ps[0:P, 2 * pr, 0:2 * T * WIN].rearrange("p (b t s) -> p b t s", b=2, s=WIN)[:, bb])
            dve.drain()
            V.tensor_reduce(wsm[:, :], wts[:, :, :], AX.X, ALU.max)
            dve.drain()
            V.tensor_tensor(wts[:, :, :], wts[:, :, :], wsm[:, :].to_broadcast([P, G, WIN]), ALU.subtract).then_inc(sc_shift, 1)
            dve.wait_ge(sc_exp, 1)
            V.tensor_reduce(wsm[:, :], wts[:, :, :], AX.X, ALU.add)
            dve.drain()
            V.reciprocal(wsm[:, :], wsm[:, :])
            dve.drain()
            V.tensor_tensor(wts[:, :, :], wts[:, :, :], wsm[:, :].to_broadcast([P, G, WIN]), ALU.mult)
            dve.drain()
            for b in range(B):
                w, hb = xw[:, b % 2], slice(T * b, T * b + T)
                dve.wait_ge(xw_in[b % 2], 16 * (b // 2 + 1))
                V.tensor_tensor(w, w, wts[:, hb, :].to_broadcast([P, T, WIN, C]), ALU.mult)
                dve.drain()
                V.tensor_reduce(h[:, hb, :], w.rearrange("p t s c -> p t c s"), AX.X, ALU.add).then_inc(xw_used, 1)
            dve.drain()

            def normed(n):
                V.tensor_reduce(st[:, 0, :], h[:, :, :], AX.X, ALU.add)
                dve.drain()
                V.tensor_scalar(st[:, 1, :], st[:, 0, :], 1.0 / C, None, ALU.mult)
                dve.drain()
                V.tensor_tensor(cenA, h[:, :, :], st[:, 1, :].to_broadcast([P, G, C]), ALU.subtract)
                dve.drain()
                V.tensor_tensor(sqA, cenA, cenA, ALU.mult)
                dve.drain()
                V.tensor_reduce(st[:, 0, :], sqA, AX.X, ALU.add)
                dve.drain()
                V.tensor_scalar(st[:, 2, :], st[:, 0, :], 1.0 / C, 1e-5, ALU.mult, ALU.add).then_inc(var_ready[n], 1)
                dve.wait_ge(std_ready[n], 1)
                V.reciprocal(st[:, 0, :], st[:, 3, :])
                dve.drain()
                for b in range(B):
                    at = slice(T * b, T * b + T)
                    V.tensor_tensor(yA[:, at], cenA[:, at], st[:, 0, at].to_broadcast([P, T, C]), ALU.mult)\
                        .then_inc(y_ready[n], 1)
                dve.drain()

            def second_digits(c, k):
                for v in range(DB):
                    V.tensor_scalar(ohb[k][:, v, :], digit[:, 1, bass.ds(HC * c, HC)], float(v), None, ALU.is_equal)

            def first_digits(c):
                for v in range(DA):
                    ins = V.tensor_scalar(oha[:, v, :], digit[:, 0, bass.ds(HC * c, HC)], float(v), None, ALU.is_equal)
                ins.then_inc(oh_ready, 1)

            dve.wait_ge(tot_ps, 1)
            V.tensor_reduce(nf[:, 2:3], ps[0:1, 5, 0:OW], AX.X, ALU.max)
            V.memset(rows_o[:, :], 0.0)
            V.memset(row0[:, :], 0.0)
            V.memset(step_to[:, :], 0.0)
            V.memset(place[:, :], 0.0)
            dve.drain()
            V.tensor_scalar(rows_o[0:OW, :], ps[0:OW, 5, 256:257], 1.0 / SC, 0.5 - 0.5 / SC, ALU.mult, ALU.add)
            V.tensor_scalar(nf[:, 3:4], nf[:, 2:3], 0.5 / SC, 0.5 - 0.25 / SC, ALU.mult, ALU.add)
            dve.drain()
            V.tensor_scalar(rows_o[0:OW, :], rows_o[0:OW, :], ROUND, -ROUND, ALU.add, ALU.add).then_inc(own_rows, 1)
            V.tensor_scalar(nf[:, 2:3], nf[:, 3:4], ROUND, -ROUND, ALU.add, ALU.add)
            dve.drain()
            V.tensor_scalar(ni[:, 1:2], nf[:, 2:3], float(PAIRS + 1), None, ALU.max).then_inc(own_rows, 2)
            dve.wait_ge(base_ps, 1)
            V.tensor_scalar(row0[0:OW, :], ps[0:OW, 6, 256:257], float(-(ROWS - 1)), None, ALU.add)
            V.scalar_tensor_tensor(place[:, 1:OW + 1], ps[:, 6, 0:OW], float(SC), above[:, 1:OW + 1], ALU.mult, ALU.subtract)
            dve.drain()
            V.tensor_tensor(place[:, 1:OW + 1], place[:, 1:OW + 1], ps[:, 5, 128:128 + OW], ALU.add)
            dve.drain()
            V.tensor_tensor(step_to[:, 0:OW], place[:, 1:OW + 1], place[:, 0:OW], ALU.subtract).then_inc(place_ready, 1)
            normed(0)
            V.memset(va[:, :, C:C + 1], 1.0)
            V.tensor_scalar(d_lo, l_lo, float(M - 1), 2.0 * M, ALU.is_lt, ALU.mult)
            dve.drain()
            V.tensor_tensor(d_hi, l_hi, d_lo, ALU.add)
            dve.drain()
            V.tensor_scalar(d_lo, d_hi, 0.5, 1.0 / DB, ALU.add, ALU.mult)
            dve.drain()
            V.tensor_scalar(d_lo, d_lo, -0.5, ROUND, ALU.add, ALU.add)
            dve.drain()
            V.tensor_scalar(d_lo, d_lo, -ROUND, None, ALU.add)
            dve.drain()
            V.tensor_copy(digit[:, 0, :], d_lo)
            V.scalar_tensor_tensor(digit[:, 1, :], d_lo, float(-DB), d_hi, ALU.mult, ALU.add)
            dve.drain()
            for b in range(B):
                dve.wait_ge(v_all_ps, b + 1)
                V.tensor_tensor(va[:, T * b:T * b + T, 0:C], ps[0:P, b, 0:T * C].rearrange("p (t c) -> p t c", t=T),
                                bv_row[:, :].unsqueeze(1).to_broadcast([P, T, C]), ALU.add).then_inc(v_all, 1)

            def keys_queries(i):
                dve.wait_ge(qkv_ps, i + 1)
                def halves(a):
                    return a.rearrange("p (a n) -> p a n", a=2)

                q, kk = ps[:, 2:4, 0:HALF], ps[:, 4:6, 0:HALF]
                V.tensor_scalar(halves(parts[:, 0:NW]), q, bq[:, 0:1], None, ALU.add)
                V.tensor_scalar(halves(highs[:, 0:NW]), kk, bk[:, 0:1], None, ALU.add)
                dve.drain()
                V.scalar_tensor_tensor(halves(parts[64:128, 0:NW]), q[64:128], bq[64:128, 0:1],
                                       halves(parts[64:128, 0:NW].bitcast(F32)), ALU.add, ALU.subtract)
                V.scalar_tensor_tensor(halves(lows[:, 0:NW]), kk, bk[:, 0:1], halves(highs[:, 0:NW].bitcast(F32)),
                                       ALU.add, ALU.subtract).then_inc(qkv_ev, 1)

            def attend(i, last):
                for t in range(T):
                    dve.wait_ge(s_ps, T * i + (t + 1))
                    b0 = 2 * (t % 2)
                    V.tensor_reduce(nm[:, t:t + 1], ps[0:P, b0:b0 + 2, 0:EVEN], AX.XY, ALU.max, negate=True).then_inc(s_max, 1)
                dve.drain()
                V.tensor_copy(nmr[:, :], nm[:, :])
                dve.drain()
                V.tensor_copy(nmx[:, :, 0], nmr[:, :].bitcast(F32))
                V.tensor_tensor(nmx[:, :, 32], nm[:, :], nmr[:, :].bitcast(F32), ALU.subtract).then_inc(nm_ready, 1)
                dve.wait_ge(oh_free, 2 * i + 1)
                second_digits(2 * i + 1, 1)
                dve.wait_ge(oh_free, 2 * i + 2)
                first_digits(2 * i + 1)
                if not last:
                    second_digits(2 * i + 2, 0)
                    keys_queries(i + 1)
                    dve.wait_ge(oh_free, 2 * i + 3)
                    first_digits(2 * i + 2)
                dve.wait_ge(o_ps, i + 1)
                O = ps[0:P, 6, 0:T * (C + 1)].rearrange("p (t c) -> p t c", t=T)
                V.reciprocal(rd[:, :], O[:, :, C])
                dve.drain()
                V.tensor_tensor(cen[:, :, :], O[:, :, 0:C], rd[:, :].to_broadcast([P, T, C]), ALU.mult).then_inc(o_ev, 1)
                dve.drain()
                hb = h[:, bass.ds(i * T, T), :]
                V.tensor_tensor(hb, hb, cen[:, :, :], ALU.add)
                dve.drain()

            keys_queries(0)
            dve.wait_ge(oh_free, 1)
            second_digits(0, 0)
            first_digits(0)
            V.memset(mark[:, :], 0.0).then_inc(o_ev, 1)
            with dve.Fori(0, B - 1) as i:
                attend(i, False)
            attend(B - 1, True)
            dve.wait_ge(hist_ps, 1)
            V.tensor_copy(hist_sb[:, :], ps[0:DA, HB, 0:DB]).then_inc(hist_ev, 1)
            V.memset(own, 0.0)
            V.memset(own_ad, 0.0)
            normed(1)
            dve.wait_ge(gat_ps, 1)
            V.tensor_copy(hg[:, :, :], ps[0:P, 0, 0:G * HE].rearrange("p (g q) -> p g q", q=HE))
            dve.drain()
            V.tensor_copy(Ts[:, :, H:TW], hg[:, :, :])
            V.tensor_tensor(tmp16[:, :, :], hg[:, :, :], asrc_row[:, :].unsqueeze(1).to_broadcast([P, G, HE]), ALU.mult)
            dve.drain()
            V.tensor_reduce(Ts[:, :, 0:H], tmp16[:, :, :].rearrange("p g (h k) -> p g h k", h=H), AX.X, ALU.add)
            dve.drain()
            V.tensor_tensor(tmp16[:, :, :], hg[:, :, :], adst_row[:, :].unsqueeze(1).to_broadcast([P, G, HE]), ALU.mult)
            dve.drain()
            V.tensor_reduce(Ds[:, :, :], tmp16[:, :, :].rearrange("p g (h k) -> p g h k", h=H), AX.X, ALU.add).then_inc(T_ready, 1)

            def decode(k, row):
                dve.wait_ge(row_in[k], row)
                V.tensor_scalar(sidx[:, k, :], kr[:, k, :], KS - 1, None, ALU.bitwise_and)
                V.tensor_scalar(didx[:, k, :], kr[:, k, :], 12, None, ALU.logical_shift_right)
                dve.drain()
                V.tensor_scalar(lg[:, k, :], didx[:, k, :], node0[:, 0:1], None, ALU.subtract).then_inc(decoded, 1)

            decode(0, 16)
            dve.wait_ge(own_in, 32)
            dve.wait_ge(hist_in, 16)
            dve.wait_ge(crow_in, 16)
            A = own[:, :, 0:H].rearrange("p u q -> p q u")
            acl = crow[:, 0:H].to_broadcast([128, H, U])
            V.tensor_copy(ad[:, :, :], own_ad[:, :, :].rearrange("p u q -> p q u"))
            V.tensor_scalar(su[:, 0, :], ccnt[:, :], 0.5, -BIG, ALU.is_lt, ALU.mult)
            dve.drain()
            V.tensor_tensor(cm[:, :, :], su[:, 0, :].unsqueeze(1).to_broadcast([128, H, U]), acl, ALU.add)
            V.tensor_tensor(wself[:, :, :], A, ad[:, :, :], ALU.add)
            V.tensor_tensor(wcl[:, :, :], ad[:, :, :], acl, ALU.add)
            dve.drain()
            V.tensor_tensor(Mx[:, :, :], cm[:, :, :], A, ALU.max)
            V.scalar_tensor_tensor(corr[:, 0], wself[:, :, :], 0.2, wself[:, :, :], ALU.mult, ALU.max)
            V.scalar_tensor_tensor(corr[:, 1], wcl[:, :, :], 0.2, wcl[:, :, :], ALU.mult, ALU.max)
            dve.drain()
            V.tensor_tensor(am[:, :, :], Mx[:, :, :], ad[:, :, :], ALU.add)
            dve.drain()
            V.scalar_tensor_tensor(mtop[:, 1], am[:, :, :], 0.2, am[:, :, :], ALU.mult, ALU.max)
            dve.drain()
            V.tensor_tensor(wself[:, :, :], corr[:, 0], mtop[:, 1], ALU.subtract)
            V.tensor_tensor(wcl[:, :, :], corr[:, 1], mtop[:, 1], ALU.subtract)
            dve.drain()
            V.tensor_scalar(wcl[:, :, :], wcl[:, :, :], 0.0, None, ALU.min).then_inc(self_arg, 1)
            dve.wait_ge(self_exp, 1)
            V.tensor_tensor(wcl[:, :, :], wcl[:, :, :], ccnt[:, :].unsqueeze(1).to_broadcast([128, H, U]), ALU.mult)
            dve.drain()
            for q in range(H):
                at = slice(H + E * q, H + E * q + E)
                V.tensor_tensor(acc[:, at, :], own[:, :, at].rearrange("p u e -> p e u"),
                                wself[:, q, :].unsqueeze(1).to_broadcast([128, E, U]), ALU.mult)
                V.tensor_tensor(s16[:, E * q:E * q + E, :], crow[:, at].to_broadcast([128, E, U]),
                                wcl[:, q, :].unsqueeze(1).to_broadcast([128, E, U]), ALU.mult)
            V.tensor_tensor(acc[:, 0:H, :], wself[:, :, :], wcl[:, :, :], ALU.add)
            dve.drain()
            V.tensor_tensor(acc[:, H:TW, :], acc[:, H:TW, :], s16[:, :, :], ALU.add).then_inc(g_used, 1)

            def add_sums(k):
                V.tensor_tensor(acc[:, :, :], acc[:, :, :], ps[:, 6 + k, 0:AU].rearrange("p (a u) -> p a u", u=U), ALU.add)
                dve.drain()

            def chunk(i, k):
                decode(1 - k, 16 * i + 16 * (k + 1))
                V.tensor_tensor(other, iota_u[:, :].unsqueeze(1).to_broadcast([128, SC, U]),
                                lg[:, k, :].to_broadcast([128, SC, U]), ALU.not_equal)
                dve.drain()
                V.tensor_scalar(other, other, -BIG, None, ALU.mult)
                dve.drain()
                dve.wait_ge(g_in[k], 256 * i + 256)
                V.tensor_tensor(D0, other.unsqueeze(2).to_broadcast([128, SC, H, U]),
                                gs[:, k, :, 0:H].to_broadcast([128, SC, H, U]), ALU.add)
                dve.drain()
                V.tensor_reduce(cm[:, :, :], D0.rearrange("p s q u -> p q u s"), AX.X, ALU.max)
                V.tensor_tensor(D1, D0, ad[:, :, :].unsqueeze(1).to_broadcast([128, SC, H, U]), ALU.add)
                dve.drain()
                V.tensor_tensor(Mx[:, :, :], Mx[:, :, :], cm[:, :, :], ALU.max)
                V.scalar_tensor_tensor(D0, D1, 0.2, D1, ALU.mult, ALU.max)
                dve.drain()
                V.tensor_tensor(am[:, :, :], Mx[:, :, :], ad[:, :, :], ALU.add)
                dve.drain()
                V.scalar_tensor_tensor(mtop[:, k], am[:, :, :], 0.2, am[:, :, :], ALU.mult, ALU.max)
                dve.drain()
                V.tensor_tensor(carg[:, k], mtop[:, 1 - k], mtop[:, k], ALU.subtract)
                V.tensor_tensor(D1, D0, mtop[:, k].unsqueeze(1).to_broadcast([128, SC, H, U]), ALU.subtract).then_inc(e_arg, 1)
                dve.wait_ge(sum_ps, 2 * i + (k + 1))
                add_sums(1 - k)
                dve.wait_ge(e_exp, 2 * i + (k + 1))
                V.tensor_tensor(acc[:, 0:H, :], acc[:, 0:H, :], corr[:, k], ALU.mult)
                V.tensor_tensor(acc[:, H:TW, :].rearrange("p (q e) u -> p q e u", e=E),
                                acc[:, H:TW, :].rearrange("p (q e) u -> p q e u", e=E),
                                corr[:, k].unsqueeze(2).to_broadcast([128, H, E, U]), ALU.mult)
                for q in range(H):
                    V.tensor_tensor(vr[:, :, HU + q * E * U:HU + (q + 1) * E * U].rearrange("p s (e u) -> p s e u", e=E),
                                    vr[:, :, q * U:q * U + U].unsqueeze(2).to_broadcast([128, SC, E, U]),
                                    gs[:, k, :, H + E * q:H + E * q + E].to_broadcast([128, SC, E, U]), ALU.mult)
                dve.drain()
                V.tensor_tensor(vr[:, 0:SC // 2, :], vr[:, 0:SC // 2, :], vr[:, SC // 2:SC, :], ALU.add).then_inc(num_ready, 1)
                dve.drain()
                V.memset(mark[:, :], 0.0).then_inc(g_used, 1)

            n_chunks2 = dve.value_load(ni[0:1, 1:2], min_val=PAIRS + 1, max_val=NE // (2 * SC) + 1)
            with dve.Fori(0, n_chunks2) as i:
                for k in range(2):
                    chunk(i, k)
            dve.wait_ge(sum_ps, 2 * n_chunks2 + 1)
            add_sums(1)
            F = s16[:, :, :]
            V.tensor_scalar(s4[:, 0], acc[:, 0:H, :], 1e-16, None, ALU.add)
            dve.drain()
            V.reciprocal(s4[:, 1], s4[:, 0])
            dve.drain()
            V.tensor_tensor(F.rearrange("p (q e) u -> p q e u", e=E), acc[:, H:TW, :].rearrange("p (q e) u -> p q e u", e=E),
                            s4[:, 1].unsqueeze(2).to_broadcast([128, H, E, U]), ALU.mult)
            dve.drain()

            def by_feature(r):
                return r[:, :].to_broadcast([128, HE, U])

            def by_node(a):
                return a.unsqueeze(1).to_broadcast([128, HE, U])

            V.tensor_tensor(F, F, by_feature(bgat_row), ALU.add)
            dve.drain()
            V.tensor_reduce(su[:, 0, :], F.rearrange("p f u -> p u f"), AX.X, ALU.add)
            dve.drain()
            V.tensor_scalar(su[:, 0, :], su[:, 0, :], 1.0 / HE, None, ALU.mult)
            dve.drain()
            V.tensor_tensor(F, F, by_node(su[:, 0, :]), ALU.subtract)
            dve.drain()
            V.tensor_tensor(acc[:, 0:HE, :], F, F, ALU.mult)
            dve.drain()
            V.tensor_reduce(su[:, 0, :], acc[:, 0:HE, :].rearrange("p f u -> p u f"), AX.X, ALU.add)
            dve.drain()
            V.tensor_scalar(su[:, 1, :], su[:, 0, :], 1.0 / HE, 1e-5, ALU.mult, ALU.add).then_inc(gv_ready, 1)
            dve.wait_ge(gs_ready, 1)
            V.reciprocal(su[:, 3, :], su[:, 2, :])
            dve.drain()
            V.tensor_tensor(F, F, by_node(su[:, 3, :]), ALU.mult)
            dve.drain()
            V.tensor_tensor(F, F, by_feature(gamma_row), ALU.mult)
            dve.drain()
            V.tensor_tensor(F, F, by_feature(beta_row), ALU.add)
            dve.drain()
            V.tensor_reduce(s4[:, 0], F.rearrange("p (h k) u -> p k u h", h=H), AX.X, ALU.add)
            dve.drain()
            V.tensor_scalar(s4[:, 1], s4[:, 0], 1.0 / H, None, ALU.mult)
            dve.drain()
            V.tensor_reduce(su[:, 0, :], s4[:, 1].rearrange("p e u -> p u e"), AX.X, ALU.max)
            for n in range(1, E):
                for e in range(E):
                    f = (e + n) % E
                    V.tensor_tensor(s4[:, 3 if n == 1 else 4, e, :], s4[:, 1, f, :], s4[:, 1, e, :],
                                    ALU.is_ge if f < e else ALU.is_gt)
                dve.drain()
                if n > 1:
                    V.tensor_tensor(s4[:, 3], s4[:, 3], s4[:, 4], ALU.add)
                    dve.drain()
            V.tensor_tensor(s4[:, 2], s4[:, 1], su[:, 0, :].unsqueeze(1).to_broadcast([128, E, U]), ALU.subtract).then_inc(top_arg, 1)
            dve.wait_ge(top_exp, 1)
            V.scalar_tensor_tensor(s4[:, 4], s4[:, 3], 1.5, s4[:, 2], ALU.is_lt, ALU.mult)
            dve.drain()
            V.tensor_reduce(su[:, 5, :], s4[:, 4].rearrange("p e u -> p u e"), AX.X, ALU.add)
            dve.drain()
            V.reciprocal(su[:, 6, :], su[:, 5, :])
            dve.drain()
            V.tensor_tensor(gown[:, :, :].rearrange("p u e -> p e u"), s4[:, 4],
                            su[:, 6, :].unsqueeze(1).to_broadcast([128, E, U]), ALU.mult).then_inc(gate_ready, 1)
            dve.wait_ge(gate_in, 16)
            dve.wait_ge(b2_added, 1)
            V.tensor_tensor(Oe, Oe, gate[:, :, :].to_broadcast([P, G, E, C]), ALU.mult)
            dve.drain()
            V.tensor_reduce(mix, Oe.rearrange("p g e c -> p g c e"), AX.X, ALU.add)
            dve.drain()
            V.tensor_tensor(h[:, :, :], h[:, :, :], mix, ALU.add)
            dve.drain()
            normed(2)
            V.memset(mark[:, :], 0.0).then_inc(so_ev, 1)
            def low_parts(i):
                dve.wait_ge(sq_hi, 2 * i + 2)
                V.tensor_tensor(lows[:, 0:NW], yT2[:, bass.ds(i * NW, NW)], highs[:, 0:NW].bitcast(F32), ALU.subtract)
                V.tensor_tensor(parts[64:128, 0:NW].rearrange("p (a n) -> p a n", a=2), ps[64:128, 2:4, 0:HALF],
                                parts[64:128, 0:NW].bitcast(F32).rearrange("p (a n) -> p a n", a=2),
                                ALU.subtract).then_inc(sq_ev, 1)

            def attend_sigmoid(i, last):
                if not last:
                    low_parts(i + 1)
                dve.wait_ge(so_ps, i + 1)
                hb = h[:, bass.ds(i * T, T), :]
                V.tensor_tensor(hb, hb, ps[0:P, 0, 0:T * C].rearrange("p (t c) -> p t c", t=T), ALU.add).then_inc(so_ev, 1)

            low_parts(0)
            with dve.Fori(0, B - 1) as i:
                attend_sigmoid(i, False)
            attend_sigmoid(B - 1, True)
            dve.drain()
            normed(3)
            V.scalar_tensor_tensor(sqA, yA, -1.0, yA, ALU.mult, ALU.max)
            dve.drain()
            V.tensor_scalar(sqA, sqA, 1e-8, None, ALU.add).then_inc(la_ready, 1)
            dve.wait_ge(la_ln, 1)
            V.tensor_reduce(st[:, 0, :], sqA, AX.X, ALU.max)
            dve.drain()
            V.tensor_tensor(sqA, sqA, st[:, 0, :].to_broadcast([P, G, C]), ALU.subtract).then_inc(la_sub, 1)
            dve.wait_ge(lo_ln, 1)
            V.tensor_tensor(cenA, cenA, st[:, 0, :].to_broadcast([P, G, C]), ALU.add)
            dve.drain()
            V.tensor_tensor(cenA, cenA, mw_row[:, :].unsqueeze(1).to_broadcast([P, G, C]), ALU.add).then_inc(lo_arg, 1)
            dve.wait_ge(lo_exp, 1)
            V.tensor_tensor(cenA, cenA, sqA, ALU.mult)
            dve.drain()
            V.tensor_tensor(cenA, cenA, lbias_row[:, :].unsqueeze(1).to_broadcast([P, G, C]), ALU.add)
            dve.drain()
            V.tensor_tensor(h[:, :, :], h[:, :, :], cenA, ALU.add).then_inc(h_ready, 1)

        @block.tensor
        def _(pe):
            mm = nc.tensor.matmul

            def turn(out_, in_):
                n = in_.shape[0]
                return mm(out_, in_, ident[0:n, 0:n], start=True, stop=True)

            pe.wait_ge(c_ready, 4)
            pe.wait_ge(x_in, 16 * XT)
            for pr in range(PAIRS):
                for t in range(XT):
                    ins = turn(ps[:, 2 * pr + t // 3, XP * (t % 3):XP * (t % 3) + XP], xt[:, t, 128 * pr:128 * pr + 128])
                ins.then_inc(x_tr, 1)
            pe.wait_ge(w_in, 16 * N_W)
            for pr in range(PAIRS):
                pe.wait_ge(x_ev, 2 * pr + 2)
                def argument(s):
                    n = WIN * pr + s
                    if n >= 2:
                        pe.wait_ge(tanh_done, n - 1)
                    for k in range(2):
                        out = ps[:, 4 + 2 * (n % 2) + k, 0:HALF]
                        o, m = s + HALF * k, WIN // 2 + HALF * k
                        mm(out, wk2[:, :], xT[:, pr, o:o + HALF], start=True, stop=False)
                        ins = mm(out, wq2[:, :], xT[:, pr, m:m + HALF], start=False, stop=True)
                    ins.then_inc(kq_ps, 1)

                argument(0)
                sc = ps[0:P, 2 * pr, 0:2 * T * WIN].rearrange("p (b t s) -> p b t s", b=2, s=WIN)
                for s in range(WIN):
                    n = WIN * pr + s
                    if s + 1 < WIN:
                        argument(s + 1)
                    if n == 0:
                        pe.wait_ge(x_ev, 4)
                        pe.wait_ge(cnt_ready, 1)
                        mm(ps[0:1, 3, 0:128], cnt[:, :], ident[:, :], start=True, stop=True).then_inc(cnt_row, 1)
                    pe.wait_ge(tanh_done, n + 1)
                    for t in range(T):
                        ins = mm(sc[:, :, t, s], tile(ring[:, n % 3, :], t), v2[:, :], start=True, stop=True)
                    ins.then_inc(sc_ps, 1)

            pe.wait_ge(wl_act, 3)
            for k in range(3):
                turn(ps[0:C, 1, C * k:C * k + C], wraw[:, k, :])
            turn(ps[:, 1, 3 * C:3 * C + 128], wl2[:, :])
            turn(ps[0:C, 1, 384:384 + C], wsig[:, :])
            mm(ps[0:P, 1, 320:320 + C], mw[0:C, 0:1].to_broadcast([C, P]), ident[0:C, 0:C],
               start=True, stop=True).then_inc(wT_ps, 1)
            pe.wait_ge(shares_ready, 1)
            mm(ps[0:1, 5, 0:OW], ones[:, 0:1], share[:, :], start=True, stop=True)
            mm(ps[:, 5, 128:128 + OW], before[:, :], share[:, :], start=True, stop=True)
            mm(ps[0:OW, 5, 256:257], share[:, :], ones[:, 0:1], start=True, stop=True).then_inc(tot_ps, 1)
            pe.wait_ge(own_rows, 3)
            mm(ps[:, 6, 0:OW], rows_o[0:OW, 0:1].to_broadcast([OW, 128]), before[0:OW, 0:OW], start=True, stop=True)
            mm(ps[0:OW, 6, 256:257], before[0:OW, 0:OW], rows_o[0:OW, 0:1], start=True, stop=True).then_inc(base_ps, 1)

            def settle(bank, w):
                mm(ps[:, bank, 0:1], w, zcol[:, :], start=True, stop=True)

            def turn_all(n):
                for b in range(B):
                    pe.wait_ge(y_ready[n], b + 1)
                    for t in range(T):
                        out = ps[:, 2 * b + t // 4, P * (t % 4):P * (t % 4) + P]
                        ins = turn(out[0:C], yA[:, T * b + t, :])
                        if n == 2:
                            ins = turn(out[C:2 * C], yA[:, T * b + t, :])
                    ins.then_inc(yT_ps[n], 1)

            def count(c, k):
                pe.wait_ge(oh_ready, c + 1)
                for n in range(HC):
                    ins = mm(ps[0:DA, HB, 0:DB], oha[:, :, n], ohb[k][:, :, n], start=False, stop=False)
                ins.then_inc(oh_free, 1)

            pe.wait_ge(w_prep, 1)
            pe.wait_ge(place_ready, 1)
            turn_all(0)
            for b in range(B):
                pe.wait_ge(yT_ev[0], b + 1)
                for t in range(T):
                    ins = mm(ps[0:P, b, C * t:C * t + C], tile(yTa, T * b + t), wT[:, 2, :], start=True, stop=True)
                ins.then_inc(v_all_ps, 1)
            mm(ps[0:DA, HB, 0:DB], zrow[0:1, 0:DA], zrow[0:1, 0:DB], start=True, stop=False).then_inc(oh_free, 1)
            pe.wait_ge(v_all, B)
            def keys_queries(i):
                settle(2, wq_st[:, :])
                for k in range(2):
                    yk = yTa[:, bass.ds(i * NW + HALF * k, HALF)]
                    mm(ps[:, 2 + k, 0:HALF], wq_st[:, :], yk, start=True, stop=True)
                    ins = mm(ps[:, 4 + k, 0:HALF], wk_st[:, :], yk, start=True, stop=True)
                ins.then_inc(qkv_ps, 1)

            def attend(i, last):
                pe.wait_ge(qkv_ev, i + 1)
                for t in range(T):
                    if t >= 2:
                        pe.wait_ge(s_max, T * i + (t - 1))
                    for k in range(2):
                        out, at = ps[0:P, 2 * (t % 2) + k, 0:EVEN], slice(LAST * k, LAST * k + EVEN)
                        mm(out, tile(parts, t), highs[:, at], start=True, stop=False)
                        ins = mm(out, tile(parts, t), lows[:, at], start=False, stop=True)
                    ins.then_inc(s_ps, 1)
                count(2 * i, 0)
                pe.wait_ge(o_ev, i + 1)
                pe.wait_ge(nm_ready, i + 1)
                for t in range(T):
                    ins = mm(ps[64:97, 6 + t // 4, P * (t % 4):P * (t % 4) + P], nmx[:, t, :], ident[0:P, 0:P],
                             start=True, stop=True)
                ins.then_inc(m_ps, 1)
                pe.wait_ge(m_ev, i + 1)
                for t in range(T):
                    if t >= 3:
                        pe.wait_ge(p_ready, T * i + (t - 2))
                    for k in range(2):
                        out, at = ps[0:P, 2 * (t % 3) + k, 0:EVEN], slice(EVEN * k, EVEN * k + EVEN)
                        mm(out, tile(highs, t), parts[:, at], start=True, stop=False)
                        mm(out, tile(lows, t), parts[:, at], start=False, stop=False)
                        ins = mm(out, ones33[:, :], mrow[:, at], start=False, stop=True)
                    ins.then_inc(st_ps, 1)
                count(2 * i + 1, 1)
                pe.wait_ge(p_ready, T * i + T)
                if not last:
                    keys_queries(i + 1)
                for t in range(T):
                    for u in range(T):
                        ins = mm(ps[0:P, 6, (C + 1) * t:(C + 1) * (t + 1)], tile(PT[:, u, :], t),
                                 va[:, bass.ds(T * i + u, 1), :].rearrange("p g c -> p (g c)"),
                                 start=(u == 0), stop=(u == T - 1))
                ins.then_inc(o_ps, 1)

            keys_queries(0)
            with pe.Fori(0, B - 1) as i:
                attend(i, False)
            attend(B - 1, True)
            pe.wait_ge(o_ev, B + 1)
            mm(ps[0:DA, HB, 0:DB], zrow[0:1, 0:DA], zrow[0:1, 0:DB], start=False, stop=True).then_inc(hist_ps, 1)
            turn_all(1)
            pe.wait_ge(yT_ev[1], B)
            for g in range(G):
                ins = mm(ps[0:P, 0, HE * g:HE * g + HE], tile(yT, g), wgat[:, :], start=True, stop=True)
            ins.then_inc(gat_ps, 1)
            mm(ps[:, 7, 0:AU], zrow[0:1, 0:128], zrow[0:1, 0:AU], start=True, stop=True).then_inc(sum_ps, 1)
            n_chunks2 = pe.value_load(ni[0:1, 1:2], min_val=PAIRS + 1, max_val=NE // (2 * SC) + 1)
            pe.wait_ge(T_ready, 3)

            def sums(i, k):
                pe.wait_ge(num_ready, 2 * i + (k + 1))
                for s in range(SC // 2):
                    ins = mm(ps[:, 6 + k, 0:AU], ident[:, :], vr[:, s, :], start=(s == 0), stop=(s == SC // 2 - 1))
                ins.then_inc(sum_ps, 1)

            with pe.Fori(0, PAIRS) as i:
                for k in range(2):
                    for n in range(2 * E):
                        if n >= 4:
                            pe.wait_ge(hid_ev, 4 * E * i + (2 * E * k + n - 3))
                            settle(n % 4, w1[:, n // 2, :])
                        mm(ps[:, n % 4, 0:HALF], w1[:, n // 2, :], yT[:, bass.ds(2 * NW * i + (NW * k + HALF * (n % 2)), HALF)],
                           start=True, stop=True).then_inc(hid_ps, 1)
                    sums(i, k)
                    pe.wait_ge(hid_ev, 4 * E * i + (2 * E * k + 2 * E))
                    for t in range(T):
                        if t >= 2:
                            pe.wait_ge(ex_ev, 2 * T * i + (T * k + t - 1))
                        for e in range(E):
                            ins = mm(ps[0:P, 4 + t % 2, C * e:C * e + C], tile(HH[:, e, :], t), w2[:, e, :], start=True, stop=True)
                        ins.then_inc(ex_ps, 1)
                    pe.wait_ge(ex_ev, 2 * T * i + (T * k + T))
            with pe.Fori(PAIRS, n_chunks2) as i:
                for k in range(2):
                    sums(i, k)
            turn_all(2)
            pe.wait_ge(yT_ev[2], B)

            def keys(i):
                for k in range(2):
                    ins = mm(ps[:, 2 + k, 0:HALF], wsT2[:, :], yT[:, bass.ds(i * NW + HALF * k, HALF)], start=True, stop=True)
                ins.then_inc(sq_ps, 1)

            def attend_sigmoid(i, last):
                pe.wait_ge(sq_ev, i + 1)
                for t in range(T):
                    if t >= 2:
                        pe.wait_ge(sg_ev, T * i + (t - 1))
                    for k in range(2):
                        out, at = ps[0:P, 4 + 2 * (t % 2) + k, 0:EVEN], slice(EVEN * k, EVEN * k + EVEN)
                        mm(out, tile(parts, t), highs[:, at], start=True, stop=False)
                        ins = mm(out, tile(parts, t), lows[:, at], start=False, stop=True)
                    ins.then_inc(sg_ps, 1)
                if not last:
                    keys(i + 1)
                pe.wait_ge(so_ev, i + 1)
                pe.wait_ge(sg_ev, T * i + T)
                for t in range(T):
                    for u in range(T):
                        ins = mm(ps[0:P, 0, C * t:C * t + C], tile(PT[:, u, :], t),
                                 yA[:, bass.ds(T * i + u, 1), :].rearrange("p g c -> p (g c)"),
                                 start=(u == 0), stop=(u == T - 1))
                ins.then_inc(so_ps, 1)

            keys(0)
            with pe.Fori(0, B - 1) as i:
                attend_sigmoid(i, False)
            attend_sigmoid(B - 1, True)
            pe.wait_ge(la_exp, 1)
            for b in range(B):
                for t in range(T):
                    ins = turn(ps[:, 2 * b + t // 4, P * (t % 4):P * (t % 4) + P], ES[:, T * b + t, :])
                ins.then_inc(lt_ps, 1)
            pe.wait_ge(lt_ev, B)
            for n in range(G // 4):
                for t in range(4):
                    ins = mm(ps[0:P, n, 128 * t:128 * t + 128], tile(esT, 4 * n + t), wlT[:, :], start=True, stop=True)
                ins.then_inc(lo_ps, 1)


_INS = ['x', 'L0_tok_W_qry', 'L0_tok_W_key', 'L0_tok_v', 'L0_tok_b', 'L0_attn_Wq', 'L0_attn_bq', 'L0_attn_Wk',
        'L0_attn_bk', 'L0_attn_Wv', 'L0_attn_bv', 'L0_ffn_W_gat', 'L0_ffn_att_src', 'L0_ffn_att_dst', 'L0_ffn_b_gat',
        'L0_ffn_ln_gamma', 'L0_ffn_ln_beta', 'L0_ffn_W1', 'L0_ffn_b1', 'L0_ffn_W2', 'L0_ffn_b2', 'L0_ffn_edge_index',
        'L1_attn_q_weight', 'L1_ffn_weight', 'L1_ffn_bias']
_OUTS = [((4, 742, 64), 'float32')]


def kernel(**inputs):
    import numpy as _np
    import concourse.bacc as _bacc
    from concourse import mybir as _mybir
    from concourse.bass_utils import run_bass_kernel_spmd as _run

    nc = _bacc.Bacc("TRN2", target_bir_lowering=False, num_devices=1)
    arrays, args = {}, []
    for name in _INS:
        a = _np.ascontiguousarray(inputs[name])
        arrays[f"in_{name}_dram"] = a
        args.append(nc.dram_tensor(f"in_{name}_dram", a.shape, _mybir.dt.from_np(a.dtype), kind="ExternalInput").ap())
    for i, (shape, dtype) in enumerate(_OUTS):
        dt = _mybir.dt.from_np(_np.dtype(dtype))
        args.append(nc.dram_tensor(f"out_{i}_dram", shape, dt, kind="ExternalOutput").ap())
    audio_tower(nc, *args)
    r = _run(nc, [arrays], core_ids=[0])
    return r.results[0]["out_0_dram"]
```
